# Optimizing a Trainium2 kernel written in Bass

```python
import numpy as np
import jax
import jax.numpy as jnp

def _softmax(x, axis=-1):
    return jax.nn.softmax(x, axis=axis)

def _gelu(x):
    return jax.nn.gelu(x, approximate=True)

def _silu(x):
    return jax.nn.silu(x)

def _sigmoid(x):
    return jax.nn.sigmoid(x)

def _layernorm(x, axis=-1, eps=1e-05):
    m = jnp.mean(x, axis=axis, keepdims=True)
    v = jnp.var(x, axis=axis, keepdims=True)
    return (x - m) / jnp.sqrt(v + eps)

def _scatter_add(tgt, idx, src, axis=0):
    return tgt.at[idx].add(src)

def _segment_sum(src, seg, n):
    return jax.ops.segment_sum(src, seg, n)
kernel_name = 'mk_hybrid_d2_jaxref_r8_3f3c28'

def setup_inputs(seed: int=0):
    np.random.seed(seed)
    _w = jnp.asarray

    def _L0_attn_a_setup():
        import jax, jax.numpy as jnp
        import numpy as np
        B_SZ, SEQ, D_IN = (8, 512, 128)
        STATE, HEADS = (128, 16)
        HEAD_DIM = STATE // HEADS
        LN_EPS = 1e-05
        key = jax.random.key(seed)
        ks = jax.random.split(key, 10)
        inp = {'x': jax.random.normal(ks[0], (B_SZ, SEQ, D_IN), dtype=jnp.float32), 'W_in': jax.random.normal(ks[1], (STATE, D_IN), dtype=jnp.float32) * (1.0 / np.sqrt(D_IN)), 'b_in': jnp.zeros((STATE,), dtype=jnp.float32), 'log_A': jax.random.normal(ks[2], (HEADS, HEAD_DIM), dtype=jnp.float32) * 0.1 + 0.1, 'B_p': jax.random.normal(ks[3], (HEADS, HEAD_DIM), dtype=jnp.float32) * 0.1 + 0.1, 'C_p': jax.random.normal(ks[4], (HEADS, HEAD_DIM), dtype=jnp.float32) * 0.1 + 0.1, 'W_out': jax.random.normal(ks[5], (STATE, STATE), dtype=jnp.float32) * (1.0 / np.sqrt(STATE)), 'b_out': jnp.zeros((STATE,), dtype=jnp.float32), 'gamma': jnp.ones((STATE,), dtype=jnp.float32), 'beta': jnp.zeros((STATE,), dtype=jnp.float32)}
        return inp
    _L0_attn_a_in = _L0_attn_a_setup()

    def _L0_attn_b_setup():
        import jax, jax.numpy as jnp
        import numpy as np
        NUM_LANDMARKS = 64
        key = jax.random.key(seed)
        ks = jax.random.split(key, 4)
        B, S, D = (4, 512, 128)
        init = 0.02
        return {'hidden_states': jax.random.normal(ks[0], (B, S, D), dtype=jnp.float32), 'Wq': jax.random.normal(ks[1], (D, D), dtype=jnp.float32) * init, 'bq': jnp.zeros((D,), dtype=jnp.float32), 'Wk': jax.random.normal(ks[2], (D, D), dtype=jnp.float32) * init, 'bk': jnp.zeros((D,), dtype=jnp.float32), 'Wv': jax.random.normal(ks[3], (D, D), dtype=jnp.float32) * init, 'bv': jnp.zeros((D,), dtype=jnp.float32)}
    _L0_attn_b_in = _L0_attn_b_setup()

    def _L0_ffn_setup():
        import jax, jax.numpy as jnp
        import numpy as np
        W_SCALE = 0.02
        TOP_K = 2
        key = jax.random.key(seed)
        ks = jax.random.split(key, 5)
        B, S, H, I, E = (2, 128, 128, 512, 8)
        return {'x': jax.random.normal(ks[0], (B, S, H), dtype=jnp.float32), 'gate': jax.random.normal(ks[1], (H, E), dtype=jnp.float32) * W_SCALE, 'experts_w1': jax.random.normal(ks[2], (E, H, I), dtype=jnp.float32) * W_SCALE, 'experts_w2': jax.random.normal(ks[3], (E, I, H), dtype=jnp.float32) * W_SCALE, 'experts_w3': jax.random.normal(ks[4], (E, H, I), dtype=jnp.float32) * W_SCALE}
    _L0_ffn_in = _L0_ffn_setup()

    def _L1_attn_a_setup():
        import math
        import jax, jax.numpy as jnp
        import numpy as np
        N_HEADS = 16
        NUM_BUCKETS = 32
        MAX_DISTANCE = 128
        ROTARY_BASE = 10000.0

        def rotate_half(x):
            x1, x2 = jnp.split(x, 2, axis=-1)
            return jnp.concatenate((-x2, x1), axis=-1)

        def rotary_freqs(T, dim):
            inv_freq = 1.0 / ROTARY_BASE ** (jnp.arange(0, dim, 2, dtype=jnp.float32) / dim)
            t = jnp.arange(T, dtype=jnp.float32)
            freqs = jnp.einsum('i,j->ij', t, inv_freq)
            return jnp.concatenate((freqs, freqs), axis=-1)

        def rel_pos_bucket_causal(rel_pos, num_buckets=NUM_BUCKETS, max_distance=MAX_DISTANCE):
            n = jnp.maximum(-rel_pos, 0)
            max_exact = num_buckets // 2
            is_small = n < max_exact
            n_safe = jnp.maximum(n, 1).astype(jnp.float32)
            val_if_large = max_exact + (jnp.log(n_safe / max_exact) / math.log(max_distance / max_exact) * (num_buckets - max_exact)).astype(jnp.int32)
            val_if_large = jnp.minimum(val_if_large, num_buckets - 1)
            return jnp.where(is_small, n, val_if_large)
        key = jax.random.key(seed)
        ks = jax.random.split(key, 10)
        B, T, C = (2, 256, 128)
        s = 0.02
        return {'x': jax.random.normal(ks[0], (B, T, C), dtype=jnp.float32), 'Wq': jax.random.normal(ks[1], (C, C), dtype=jnp.float32) * s, 'bq': jnp.zeros((C,), dtype=jnp.float32), 'Wk': jax.random.normal(ks[2], (C, C), dtype=jnp.float32) * s, 'bk': jnp.zeros((C,), dtype=jnp.float32), 'Wv': jax.random.normal(ks[3], (C, C), dtype=jnp.float32) * s, 'bv': jnp.zeros((C,), dtype=jnp.float32), 'Wp': jax.random.normal(ks[4], (C, C), dtype=jnp.float32) * s, 'bp': jnp.zeros((C,), dtype=jnp.float32), 'rel_bias_table': jax.random.normal(ks[5], (NUM_BUCKETS, N_HEADS), dtype=jnp.float32) * s}
    _L1_attn_a_in = _L1_attn_a_setup()

    def _L1_attn_b_setup():
        import jax, jax.numpy as jnp
        import numpy as np
        HEADS = 16
        DIM_HEAD = 64
        SEG = 32
        SCALE = DIM_HEAD ** (-0.5)
        INNER = HEADS * DIM_HEAD

        def elu1(x):
            return jax.nn.elu(x) + 1.0

        def rope(t, pos):
            d = t.shape[-1]
            freqs = 10000.0 ** (-jnp.arange(0, d, 2, dtype=jnp.float32) / d)
            ang = pos[:, None] * freqs
            cos = jnp.repeat(jnp.cos(ang), 2, axis=-1)
            sin = jnp.repeat(jnp.sin(ang), 2, axis=-1)
            t2 = t.reshape(t.shape[:-1] + (d // 2, 2))
            rot = jnp.stack((-t2[..., 1], t2[..., 0]), axis=-1).reshape(t.shape)
            return t * cos + rot * sin

        def _reference_tuple_inner(x, w_qkv, w_out, ln_g, ln_b, mem_beta):
            B, N, D = x.shape
            mu = x.mean(-1, keepdims=True)
            var = x.var(-1, keepdims=True)
            xn = (x - mu) / jnp.sqrt(var + 1e-05) * ln_g + ln_b
            qkv = xn @ w_qkv
            q, k, v = jnp.split(qkv, 3, axis=-1)

            def to_heads(t):
                return t.reshape(B, N, HEADS, DIM_HEAD).transpose(0, 2, 1, 3)
            q, k, v = map(to_heads, (q, k, v))
            next_k, next_v = (k, v)
            pos = jnp.arange(N, dtype=jnp.float32)
            qr, kr = (rope(q, pos), rope(k, pos))
            W = N // SEG

            def to_segs(t):
                return t.reshape(B, HEADS, W, SEG, DIM_HEAD).transpose(2, 0, 1, 3, 4)
            qs, ks, vs, qnope, knope = map(to_segs, (qr, kr, v, q, k))
            mask = jnp.tril(jnp.ones((SEG, SEG), bool))
            beta = jax.nn.sigmoid(mem_beta)
            mem0 = jnp.zeros((B, HEADS, DIM_HEAD, DIM_HEAD), x.dtype)
            z0 = jnp.full((B, HEADS, DIM_HEAD), 1e-06, x.dtype)

            def step(carry, inp):
                mem, z = carry
                q_s, k_s, v_s, qn_s, kn_s = inp
                scores = jnp.einsum('bhnd,bhmd->bhnm', q_s, k_s) * SCALE
                scores = jnp.where(mask, scores, -jnp.inf)
                sdpa = jnp.einsum('bhnm,bhmd->bhnd', jax.nn.softmax(scores, axis=-1), v_s)
                sq = elu1(qn_s)
                num = jnp.einsum('bhnk,bhkv->bhnv', sq, mem)
                den = jnp.einsum('bhnk,bhk->bhn', sq, z)[..., None]
                mem_out = num / (den + 1e-06)
                out = beta * mem_out + (1.0 - beta) * sdpa
                sk = elu1(kn_s)
                prev_v = jnp.einsum('bhnk,bhkv->bhnv', sk, mem) / jnp.einsum('bhnk,bhk->bhn', sk, z)[..., None]
                mem = mem + jnp.einsum('bhnk,bhnv->bhkv', sk, v_s - prev_v)
                z = z + sk.sum(axis=2)
                return ((mem, z), out)
            _, outs = jax.lax.scan(step, (mem0, z0), (qs, ks, vs, qnope, knope))
            o = outs.transpose(1, 0, 3, 2, 4).reshape(B, N, INNER)
            out = o @ w_out
            return (out, next_k, next_v)
        key = jax.random.key(seed)
        k1, k2, k3 = jax.random.split(key, 3)
        B, N, D = (4, 512, 128)
        x = jax.random.normal(k1, (B, N, D), dtype=jnp.float32)
        w_qkv = jax.random.normal(k2, (D, 3 * INNER), dtype=jnp.float32) * 0.02
        w_out = jax.random.normal(k3, (INNER, D), dtype=jnp.float32) * 0.02
        ln_g = jnp.ones((D,), jnp.float32)
        ln_b = jnp.zeros((D,), jnp.float32)
        mem_beta = jnp.zeros((1, HEADS, 1, 1), jnp.float32)
        return {'x': x, 'w_qkv': w_qkv, 'w_out': w_out, 'ln_g': ln_g, 'ln_b': ln_b, 'mem_beta': mem_beta}
    _L1_attn_b_in = _L1_attn_b_setup()

    def _L1_ffn_setup():
        import jax, jax.numpy as jnp
        import numpy as np
        B, S, D = (2, 256, 128)
        E = 4
        H = 4 * D
        key = jax.random.key(seed)
        k_x, k_r, k_wv, k_wp = jax.random.split(key, 4)
        x = jax.random.normal(k_x, (B, S, D), dtype=jnp.float32)
        w_router = jax.random.normal(k_r, (D, E), dtype=jnp.float32) * 0.02
        w_v = jax.random.normal(k_wv, (E, D, 2 * H), dtype=jnp.float32) * 0.02
        w_proj = jax.random.normal(k_wp, (E, H, D), dtype=jnp.float32) * 0.02
        return {'x': x, 'w_router': w_router, 'w_v': w_v, 'w_proj': w_proj}
    _L1_ffn_in = _L1_ffn_setup()
    _d = {'L0_attn_a_x': _L0_attn_a_in['x'], 'L0_attn_a_W_in': _L0_attn_a_in['W_in'], 'L0_attn_a_b_in': _L0_attn_a_in['b_in'], 'L0_attn_a_log_A': _L0_attn_a_in['log_A'], 'L0_attn_a_B_p': _L0_attn_a_in['B_p'], 'L0_attn_a_C_p': _L0_attn_a_in['C_p'], 'L0_attn_a_W_out': _L0_attn_a_in['W_out'], 'L0_attn_a_b_out': _L0_attn_a_in['b_out'], 'L0_attn_a_gamma': _L0_attn_a_in['gamma'], 'L0_attn_a_beta': _L0_attn_a_in['beta'], 'L0_attn_b_Wq': _L0_attn_b_in['Wq'], 'L0_attn_b_bq': _L0_attn_b_in['bq'], 'L0_attn_b_Wk': _L0_attn_b_in['Wk'], 'L0_attn_b_bk': _L0_attn_b_in['bk'], 'L0_attn_b_Wv': _L0_attn_b_in['Wv'], 'L0_attn_b_bv': _L0_attn_b_in['bv'], 'L0_ffn_gate': _L0_ffn_in['gate'], 'L0_ffn_experts_w1': _L0_ffn_in['experts_w1'], 'L0_ffn_experts_w2': _L0_ffn_in['experts_w2'], 'L0_ffn_experts_w3': _L0_ffn_in['experts_w3'], 'L1_attn_a_Wq': _L1_attn_a_in['Wq'], 'L1_attn_a_bq': _L1_attn_a_in['bq'], 'L1_attn_a_Wk': _L1_attn_a_in['Wk'], 'L1_attn_a_bk': _L1_attn_a_in['bk'], 'L1_attn_a_Wv': _L1_attn_a_in['Wv'], 'L1_attn_a_bv': _L1_attn_a_in['bv'], 'L1_attn_a_Wp': _L1_attn_a_in['Wp'], 'L1_attn_a_bp': _L1_attn_a_in['bp'], 'L1_attn_a_rel_bias_table': _L1_attn_a_in['rel_bias_table'], 'L1_attn_b_w_qkv': _L1_attn_b_in['w_qkv'], 'L1_attn_b_w_out': _L1_attn_b_in['w_out'], 'L1_attn_b_ln_g': _L1_attn_b_in['ln_g'], 'L1_attn_b_ln_b': _L1_attn_b_in['ln_b'], 'L1_attn_b_mem_beta': _L1_attn_b_in['mem_beta'], 'L1_ffn_w_router': _L1_ffn_in['w_router'], 'L1_ffn_w_v': _L1_ffn_in['w_v'], 'L1_ffn_w_proj': _L1_ffn_in['w_proj']}
    _x0 = _d['L0_attn_a_x']
    _d['L0_attn_a_x'] = jax.random.normal(jax.random.fold_in(jax.random.key(seed), 1), (4, 1024, 128), dtype=_x0.dtype)
    del _x0
    return _d

def reference(L0_attn_a_x, L0_attn_a_W_in, L0_attn_a_b_in, L0_attn_a_log_A, L0_attn_a_B_p, L0_attn_a_C_p, L0_attn_a_W_out, L0_attn_a_b_out, L0_attn_a_gamma, L0_attn_a_beta, L0_attn_b_Wq, L0_attn_b_bq, L0_attn_b_Wk, L0_attn_b_bk, L0_attn_b_Wv, L0_attn_b_bv, L0_ffn_gate, L0_ffn_experts_w1, L0_ffn_experts_w2, L0_ffn_experts_w3, L1_attn_a_Wq, L1_attn_a_bq, L1_attn_a_Wk, L1_attn_a_bk, L1_attn_a_Wv, L1_attn_a_bv, L1_attn_a_Wp, L1_attn_a_bp, L1_attn_a_rel_bias_table, L1_attn_b_w_qkv, L1_attn_b_w_out, L1_attn_b_ln_g, L1_attn_b_ln_b, L1_attn_b_mem_beta, L1_ffn_w_router, L1_ffn_w_v, L1_ffn_w_proj):

    def _L0_attn_a_ref(x, W_in, b_in, log_A, B_p, C_p, W_out, b_out, gamma, beta):
        import jax, jax.numpy as jnp
        import numpy as np
        B_SZ, SEQ, D_IN = (8, 512, 128)
        STATE, HEADS = (128, 16)
        HEAD_DIM = STATE // HEADS
        LN_EPS = 1e-05
        Bsz, S, _ = x.shape
        H, Dh = log_A.shape
        h = jnp.einsum('bsd,ed->bse', x, W_in) + b_in
        h = h.reshape(Bsz, S, H, Dh)
        decay = jnp.exp(-jax.nn.softplus(log_A))

        def step(s, xt):
            s = s * decay + B_p * xt
            return (s, C_p * s)
        s0 = jnp.zeros((Bsz, H, Dh), dtype=h.dtype)
        _, ys = jax.lax.scan(step, s0, jnp.swapaxes(h, 0, 1))
        y = jnp.swapaxes(ys, 0, 1).reshape(Bsz, S, H * Dh)
        out = jnp.einsum('bse,fe->bsf', y, W_out) + b_out
        mu = out.mean(-1, keepdims=True)
        var = out.var(-1, keepdims=True)
        return (out - mu) * jax.lax.rsqrt(var + LN_EPS) * gamma + beta

    def _L0_attn_b_ref(hidden_states, Wq, bq, Wk, bk, Wv, bv):
        import jax, jax.numpy as jnp
        import numpy as np
        NUM_LANDMARKS = 64
        B, S, D = hidden_states.shape
        L = NUM_LANDMARKS
        q = hidden_states @ Wq + bq
        k = hidden_states @ Wk + bk
        v = hidden_states @ Wv + bv
        q = jax.nn.softmax(q, axis=-1)
        k = jax.nn.softmax(k, axis=-1)
        k_landmarks = k.reshape(B, L, S // L, D).mean(axis=2)
        kernel_1 = jnp.einsum('bqd,bkd->bqk', q, k_landmarks)
        kernel_2 = jnp.einsum('bkd,bld->bkl', k_landmarks, k)
        kernel_3 = k * v
        mid = jnp.einsum('bkl,bld->bkd', kernel_2, kernel_3)
        output = jnp.einsum('bqk,bkd->bqd', kernel_1, mid)
        return output

    def _L0_ffn_ref(x, gate, experts_w1, experts_w2, experts_w3):
        import jax, jax.numpy as jnp
        import numpy as np
        W_SCALE = 0.02
        TOP_K = 2
        E = experts_w1.shape[0]
        router_logits = jnp.einsum('bsh,he->bse', x, gate)
        routing_weights, selected = jax.lax.top_k(router_logits, TOP_K)
        routing_weights = jax.nn.softmax(routing_weights, axis=-1)
        onehot = jax.nn.one_hot(selected, E, dtype=x.dtype)
        tok_w = jnp.einsum('bsk,bske->bse', routing_weights, onehot)
        g = jnp.einsum('bsh,ehi->ebsi', x, experts_w1)
        u = jnp.einsum('bsh,ehi->ebsi', x, experts_w3)
        hid = jax.nn.silu(g) * u
        eo = jnp.einsum('ebsi,eih->ebsh', hid, experts_w2)
        out = jnp.einsum('ebsh,bse->bsh', eo, tok_w)
        return out

    def _L1_attn_a_ref(x, Wq, bq, Wk, bk, Wv, bv, Wp, bp, rel_bias_table):
        import math
        import jax, jax.numpy as jnp
        import numpy as np
        N_HEADS = 16
        NUM_BUCKETS = 32
        MAX_DISTANCE = 128
        ROTARY_BASE = 10000.0

        def rotate_half(x):
            x1, x2 = jnp.split(x, 2, axis=-1)
            return jnp.concatenate((-x2, x1), axis=-1)

        def rotary_freqs(T, dim):
            inv_freq = 1.0 / ROTARY_BASE ** (jnp.arange(0, dim, 2, dtype=jnp.float32) / dim)
            t = jnp.arange(T, dtype=jnp.float32)
            freqs = jnp.einsum('i,j->ij', t, inv_freq)
            return jnp.concatenate((freqs, freqs), axis=-1)

        def rel_pos_bucket_causal(rel_pos, num_buckets=NUM_BUCKETS, max_distance=MAX_DISTANCE):
            n = jnp.maximum(-rel_pos, 0)
            max_exact = num_buckets // 2
            is_small = n < max_exact
            n_safe = jnp.maximum(n, 1).astype(jnp.float32)
            val_if_large = max_exact + (jnp.log(n_safe / max_exact) / math.log(max_distance / max_exact) * (num_buckets - max_exact)).astype(jnp.int32)
            val_if_large = jnp.minimum(val_if_large, num_buckets - 1)
            return jnp.where(is_small, n, val_if_large)
        B, T, C = x.shape
        H = N_HEADS
        D = C // H

        def heads(y):
            return y.reshape(B, T, H, D).transpose(0, 2, 1, 3)
        q = heads(x @ Wq + bq)
        k = heads(x @ Wk + bk)
        v = heads(x @ Wv + bv)
        freqs = rotary_freqs(T, D)
        cos, sin = (jnp.cos(freqs), jnp.sin(freqs))
        q = q * cos + rotate_half(q) * sin
        k = k * cos + rotate_half(k) * sin
        pos = jnp.arange(T)
        rel_pos = pos[None, :] - pos[:, None]
        bucket = rel_pos_bucket_causal(rel_pos)
        bias = rel_bias_table[bucket]
        bias = bias.transpose(2, 0, 1)
        att = jnp.einsum('bhid,bhjd->bhij', q, k) + bias[None]
        att = att * (1.0 / math.sqrt(D))
        causal = pos[None, :] <= pos[:, None]
        att = jnp.where(causal[None, None], att, -jnp.inf)
        att = jax.nn.softmax(att, axis=-1)
        y = jnp.einsum('bhij,bhjd->bhid', att, v)
        y = y.transpose(0, 2, 1, 3).reshape(B, T, C)
        return y @ Wp + bp

    def _L1_attn_b_ref(x, w_qkv, w_out, ln_g, ln_b, mem_beta):
        import jax, jax.numpy as jnp
        import numpy as np
        HEADS = 16
        DIM_HEAD = 64
        SEG = 32
        SCALE = DIM_HEAD ** (-0.5)
        INNER = HEADS * DIM_HEAD

        def elu1(x):
            return jax.nn.elu(x) + 1.0

        def rope(t, pos):
            d = t.shape[-1]
            freqs = 10000.0 ** (-jnp.arange(0, d, 2, dtype=jnp.float32) / d)
            ang = pos[:, None] * freqs
            cos = jnp.repeat(jnp.cos(ang), 2, axis=-1)
            sin = jnp.repeat(jnp.sin(ang), 2, axis=-1)
            t2 = t.reshape(t.shape[:-1] + (d // 2, 2))
            rot = jnp.stack((-t2[..., 1], t2[..., 0]), axis=-1).reshape(t.shape)
            return t * cos + rot * sin

        def _reference_tuple_inner(x, w_qkv, w_out, ln_g, ln_b, mem_beta):
            B, N, D = x.shape
            mu = x.mean(-1, keepdims=True)
            var = x.var(-1, keepdims=True)
            xn = (x - mu) / jnp.sqrt(var + 1e-05) * ln_g + ln_b
            qkv = xn @ w_qkv
            q, k, v = jnp.split(qkv, 3, axis=-1)

            def to_heads(t):
                return t.reshape(B, N, HEADS, DIM_HEAD).transpose(0, 2, 1, 3)
            q, k, v = map(to_heads, (q, k, v))
            next_k, next_v = (k, v)
            pos = jnp.arange(N, dtype=jnp.float32)
            qr, kr = (rope(q, pos), rope(k, pos))
            W = N // SEG

            def to_segs(t):
                return t.reshape(B, HEADS, W, SEG, DIM_HEAD).transpose(2, 0, 1, 3, 4)
            qs, ks, vs, qnope, knope = map(to_segs, (qr, kr, v, q, k))
            mask = jnp.tril(jnp.ones((SEG, SEG), bool))
            beta = jax.nn.sigmoid(mem_beta)
            mem0 = jnp.zeros((B, HEADS, DIM_HEAD, DIM_HEAD), x.dtype)
            z0 = jnp.full((B, HEADS, DIM_HEAD), 1e-06, x.dtype)

            def step(carry, inp):
                mem, z = carry
                q_s, k_s, v_s, qn_s, kn_s = inp
                scores = jnp.einsum('bhnd,bhmd->bhnm', q_s, k_s) * SCALE
                scores = jnp.where(mask, scores, -jnp.inf)
                sdpa = jnp.einsum('bhnm,bhmd->bhnd', jax.nn.softmax(scores, axis=-1), v_s)
                sq = elu1(qn_s)
                num = jnp.einsum('bhnk,bhkv->bhnv', sq, mem)
                den = jnp.einsum('bhnk,bhk->bhn', sq, z)[..., None]
                mem_out = num / (den + 1e-06)
                out = beta * mem_out + (1.0 - beta) * sdpa
                sk = elu1(kn_s)
                prev_v = jnp.einsum('bhnk,bhkv->bhnv', sk, mem) / jnp.einsum('bhnk,bhk->bhn', sk, z)[..., None]
                mem = mem + jnp.einsum('bhnk,bhnv->bhkv', sk, v_s - prev_v)
                z = z + sk.sum(axis=2)
                return ((mem, z), out)
            _, outs = jax.lax.scan(step, (mem0, z0), (qs, ks, vs, qnope, knope))
            o = outs.transpose(1, 0, 3, 2, 4).reshape(B, N, INNER)
            out = o @ w_out
            return (out, next_k, next_v)
        return _reference_tuple_inner(x, w_qkv, w_out, ln_g, ln_b, mem_beta)[0]

    def _L1_ffn_ref(x, w_router, w_v, w_proj):
        import jax, jax.numpy as jnp
        import numpy as np
        B, S, D = (2, 256, 128)
        E = 4
        H = 4 * D
        logits = jnp.einsum('bsd,de->bse', x, w_router)
        probs = jax.nn.softmax(logits, axis=-1)
        expert_idx = jnp.argmax(probs, axis=-1)
        gv = jnp.einsum('bsd,edh->ebsh', x, w_v)
        gate_raw, value = jnp.split(gv, 2, axis=-1)
        h = gate_raw * jax.nn.sigmoid(gate_raw) * value
        y = jnp.einsum('ebsh,ehd->ebsd', h, w_proj)
        onehot = jax.nn.one_hot(expert_idx, w_v.shape[0], dtype=x.dtype)
        return jnp.einsum('bse,ebsd->bsd', onehot, y)
    x = L0_attn_a_x
    x = x + _L0_attn_a_ref(_layernorm(x, axis=-1), L0_attn_a_W_in, L0_attn_a_b_in, L0_attn_a_log_A, L0_attn_a_B_p, L0_attn_a_C_p, L0_attn_a_W_out, L0_attn_a_b_out, L0_attn_a_gamma, L0_attn_a_beta)
    x = x + _L0_ffn_ref(_layernorm(x, axis=-1), L0_ffn_gate, L0_ffn_experts_w1, L0_ffn_experts_w2, L0_ffn_experts_w3)
    x = x + _L0_attn_b_ref(_layernorm(x, axis=-1), L0_attn_b_Wq, L0_attn_b_bq, L0_attn_b_Wk, L0_attn_b_bk, L0_attn_b_Wv, L0_attn_b_bv)
    x = x + _L0_ffn_ref(_layernorm(x, axis=-1), L0_ffn_gate, L0_ffn_experts_w1, L0_ffn_experts_w2, L0_ffn_experts_w3)
    x = x + _L1_attn_a_ref(_layernorm(x, axis=-1), L1_attn_a_Wq, L1_attn_a_bq, L1_attn_a_Wk, L1_attn_a_bk, L1_attn_a_Wv, L1_attn_a_bv, L1_attn_a_Wp, L1_attn_a_bp, L1_attn_a_rel_bias_table)
    x = x + _L1_ffn_ref(_layernorm(x, axis=-1), L1_ffn_w_router, L1_ffn_w_v, L1_ffn_w_proj)
    x = x + _L1_attn_b_ref(_layernorm(x, axis=-1), L1_attn_b_w_qkv, L1_attn_b_w_out, L1_attn_b_ln_g, L1_attn_b_ln_b, L1_attn_b_mem_beta)
    x = x + _L1_ffn_ref(_layernorm(x, axis=-1), L1_ffn_w_router, L1_ffn_w_v, L1_ffn_w_proj)
    return x

_drawn_inputs = setup_inputs


def setup_inputs(seed=0):
    import zlib

    import numpy as np

    out = dict(_drawn_inputs(seed))
    spreads = {'L0_attn_a_b_in': (0.0, 0.295),
     'L0_attn_a_b_out': (0.0, 0.1),
     'L0_attn_a_gamma': (1.0, 0.2),
     'L0_attn_a_beta': (0.0, 0.1),
     'L0_attn_b_bq': (0.0, 0.8),
     'L0_attn_b_bk': (0.0, 0.8),
     'L0_attn_b_bv': (0.0, 0.8),
     'L1_attn_a_bq': (0.0, 2.0),
     'L1_attn_a_bk': (0.0, 2.0),
     'L1_attn_a_bv': (0.0, 0.511),
     'L1_attn_a_bp': (0.0, 0.1),
     'L1_attn_b_ln_g': (1.0, 0.6),
     'L1_attn_b_ln_b': (0.0, 0.8),
     'L1_attn_b_mem_beta': (0.0, 2.0)}
    factors = {'L0_attn_a_log_A': 8.0,
     'L0_attn_b_Wq': 8.0,
     'L0_attn_b_Wk': 8.0,
     'L0_attn_b_Wv': 8.0,
     'L0_ffn_gate': 5.573,
     'L0_ffn_experts_w1': 4.683,
     'L0_ffn_experts_w2': 4.795,
     'L0_ffn_experts_w3': 4.858,
     'L1_attn_a_Wq': 29.098,
     'L1_attn_a_Wk': 22.335,
     'L1_attn_a_rel_bias_table': 64.0,
     'L1_ffn_w_router': 4.096,
     'L1_ffn_w_v': 3.457,
     'L1_ffn_w_proj': 3.58}
    for name, (base, spread) in spreads.items():
        noise = np.random.default_rng([zlib.crc32(name.encode()), seed]).standard_normal(out[name].shape)
        drawn = base * np.exp(spread * noise) if base else spread * noise
        out[name] = jnp.asarray(drawn.astype(out[name].dtype))
    for name, factor in factors.items():
        out[name] = (out[name] * factor).astype(out[name].dtype)
    return out
```

```python
from contextlib import ExitStack

import concourse.bass as bass
from concourse import mybir

F32 = mybir.dt.float32
U32 = mybir.dt.uint32
ALU = mybir.AluOpType
ACT = mybir.ActivationFunctionType
AX_X = mybir.AxisListType.X

P = 128
BATCH, SEQ = 4, 1024
NT = BATCH * SEQ // P
CT = 4
CHUNK = CT * P
NC_ = NT // CT
EPS = 1e-5


class Scope:

    def __init__(self, nc, ctx, prefix):
        self.nc, self.ctx, self.prefix, self.sems = nc, ctx, prefix, []

    def sb(self, name, shape, dt=F32):
        return self.ctx.enter_context(self.nc.sbuf_tensor(f"{self.prefix}_{name}", shape, dt))

    def ps(self, name, shape, dt=F32):
        return self.ctx.enter_context(self.nc.psum_tensor(f"{self.prefix}_{name}", shape, dt))

    def sem(self, name):
        self.sems.append(self.nc.alloc_semaphore(f"{self.prefix}_{name}"))
        return self.sems[-1]

    def clear(self):
        self.nc.clear_and_free_semaphores(self.sems)
        self.nc.all_engine_barrier()


class Chain:

    def __init__(self, eng, sem, base=0):
        self.eng, self.sem, self.base, self.n = eng, sem, base, 0

    def mark(self, ins):
        self.n += 1
        return ins.then_inc(self.sem, 1)

    def wait(self):
        hold(self.eng, self.sem, self.base + self.n)

    def link(self, ins):
        self.mark(ins)
        self.wait()


def hold(eng, sem, value):
    eng.wait_ge(sem, value)
    eng.nop(nofuse=True)


def bc(ap, k):
    return ap.unsqueeze(1).to_broadcast([ap.shape[0], k, ap.shape[1]])


def bl(ap, n):
    return ap.unsqueeze(2).to_broadcast([ap.shape[0], ap.shape[1], n])


def tile_of(t, n):
    return t[:, bass.ds(n, 1), :].rearrange("p a d -> p (a d)")


def load_and_constants(nc, g, x):
    with ExitStack() as ctx:
        s = Scope(nc, ctx, "init")
        raw = s.sb("raw", [P, NT, 6])
        x_loaded, zeroed = s.sem("x_loaded"), s.sem("zeroed")
        stats_done = s.sem("stats_done")
        with nc.Block() as block:
            @block.sync
            def _(sp):
                xs = x.rearrange("b (n p) d -> p (b n) d", p=P)
                for c in range(NC_):
                    sp.dma_start(g.X[:, CT * c:CT * c + CT, :], xs[:, CT * c:CT * c + CT, :]).then_inc(x_loaded, 16)
                g.load_weights(sp)

            @block.gpsimd
            def _(pool):
                nc.gpsimd.memset(g.ident[:], 0.0).then_inc(zeroed, 1)
                nc.gpsimd.memset(g.eps[:], EPS)
                nc.gpsimd.memset(g.ones[:], 1.0)
                nc.gpsimd.iota(g.iota8[:], pattern=[[1, 8]], base=0, channel_multiplier=0,
                               allow_small_or_imprecise_dtypes=True)
                pool.wait_ge(zeroed, 1)
                nc.gpsimd.affine_select(out=g.ident[:], in_=g.ident[:], compare_op=ALU.not_equal, fill=1.0,
                                        base=0, pattern=[[-1, P]], channel_multiplier=1)

            @block.vector
            def _(dve):
                dve.wait_ge(x_loaded, 16 * NC_)
                for n in range(NT):
                    last = nc.vector.bn_stats(raw[:, n, :], g.X[:, n, :])
                last.then_inc(stats_done, 1)
                dve.wait_ge(stats_done, 1)
                for n in range(NT):
                    nc.vector.bn_aggr(g.MV[:, n, :], raw[:, n, :])
        s.clear()


class Norm:

    def __init__(self, nc, g, s, bufs=1):
        self.nc, self.g = nc, g
        self.std = s.sb("std", [P, NT])
        self.RS = s.sb("rstd", [P, NT])
        self.xn = s.sb("xn", [P, CT, P])
        self.std_ready, self.rs_ready = s.sem("std_ready"), s.sem("rs_ready")

    def act_std(self, act):
        self.nc.scalar.activation(self.std[:], self.g.MV[:, :, 1], ACT.Sqrt, bias=self.g.eps[:, 0:1]).then_inc(self.std_ready, 1)

    def dve_rstd(self, dve):
        dve.wait_ge(self.std_ready, 1)
        self.nc.vector.reciprocal(self.RS[:], self.std[:]).then_inc(self.rs_ready, 1)
        dve.wait_ge(self.rs_ready, 1)

    def dve_rows(self, c):
        for k in range(CT):
            n = c * CT + k
            last = self.nc.vector.tensor_scalar(self.xn[:, k, :], tile_of(self.g.X, n),
                                                tile_of(self.g.MV, n)[:, 0:1], self.RS[:, bass.ds(n, 1)],
                                                ALU.subtract, ALU.mult)
        return last


def dve_new_stats(nc, dve, g, raw, c, ch):
    for k in range(CT):
        last = nc.vector.bn_stats(raw[:, k, :], tile_of(g.X, c * CT + k))
    ch.link(last)
    for k in range(CT):
        last = nc.vector.bn_aggr(g.mv4[:, k, :], raw[:, k, :])
    ch.link(last)
    return nc.vector.tensor_copy(g.MV[:, bass.ds(c * CT, CT), :], g.mv4[:])


def ssm_layer(nc, g, w_in_t, b_in, log_a, b_p, c_p, w_out_t, b_out, gamma, beta):
    with ExitStack() as ctx:
        s = Scope(nc, ctx, "ssm")
        norm = Norm(nc, g, s)
        win, wout, woc = s.sb("win", [P, P]), s.sb("wout", [P, P]), s.sb("woc", [P, P])
        cols = s.sb("cols", [P, 8])
        decay = s.sb("decay", [P, CHUNK])
        rows = s.sb("rows", [P, 2, P])
        bo4 = s.sb("bo4", [1, CT, P])
        xt = s.sb("xt", [P, CHUNK])
        bh = s.sb("bh", [P, CHUNK])
        y = s.sb("y", [P, 2, CHUNK])
        t = s.sb("t", [P, CT, P])
        raw, mv = s.sb("raw", [P, CT, 6]), s.sb("mv", [P, CT, 2])
        so, ro = s.sb("so", [P, CT]), s.sb("ro", [P, CT])
        ps_t, ps_h, ps_o = s.ps("ps_t", [P, CHUNK]), s.ps("ps_h", [P, CHUNK]), s.ps("ps_o", [P, CT, P])
        loaded = s.sem("loaded")
        setup, chain, e_ready = s.sem("setup"), s.sem("chain"), s.sem("e_ready")
        consts_ready = s.sem("consts_ready")
        xn_ready, xn_turned, xt_ready = s.sem("xn_ready"), s.sem("xn_turned"), s.sem("xt_ready")
        h_ready, bh_ready, y_ready, o_ready = s.sem("h_ready"), s.sem("bh_ready"), s.sem("y_ready"), s.sem("o_ready")
        mv_ready, so_ready, o_used = s.sem("mv_ready"), s.sem("so_ready"), s.sem("o_used")
        STEPS = 8

        with nc.Block() as block:
            @block.sync
            def _(sp):
                for dst, src in ((win[:], w_in_t), (wout[:], w_out_t),
                                 (cols[:, 0:1], b_in.rearrange("(p a) -> p a", a=1)),
                                 (cols[:, 1:2], log_a.rearrange("h (d a) -> (h d) a", a=1)),
                                 (cols[:, 2:3], b_p.rearrange("h (d a) -> (h d) a", a=1)),
                                 (cols[:, 3:4], c_p.rearrange("h (d a) -> (h d) a", a=1)),
                                 (rows[:, 0, :], gamma.partition_broadcast(P)),
                                 (rows[:, 1, :], beta.partition_broadcast(P))):
                    sp.dma_start(dst, src).then_inc(loaded, 16)
                for k in range(CT):
                    sp.dma_start(bo4[:, k, :], b_out.rearrange("(a n) -> a n", a=1)).then_inc(loaded, 16)

            @block.scalar
            def _(act):
                norm.act_std(act)
                act.wait_ge(loaded, 16 * 12)
                nc.scalar.activation(cols[:, 6:7], cols[:, 1:2], ACT.Exp).then_inc(e_ready, 1)
                act.wait_ge(consts_ready, 1)
                with act.Fori(0, NC_) as c:
                    act.wait_ge(xn_turned, c + 1)
                    nc.scalar.activation(xt[:], ps_t[:], ACT.Copy).then_inc(xt_ready, 1)
                    act.wait_ge(h_ready, c + 1)
                    act.wait_ge(y_ready, c + 1)
                    nc.scalar.activation(bh[:], ps_h[:], ACT.Identity, bias=cols[:, 5:6], scale=cols[:, 2:3]).then_inc(bh_ready, 1)
                    act.wait_ge(mv_ready, c + 1)
                    nc.scalar.activation(so[:], mv[:, :, 1], ACT.Sqrt, bias=g.eps[:, 0:1]).then_inc(so_ready, 1)

            @block.tensor
            def _(pe):
                pe.wait_ge(consts_ready, 1)
                with pe.Fori(0, NC_ // 2) as i:
                    for u in range(2):
                        c = i * 2 + u
                        pe.wait_ge(xn_ready, c + 1)
                        for k in range(CT):
                            last = nc.tensor.transpose(ps_t[:, k * P:k * P + P], norm.xn[:, k, :], g.ident[:])
                        last.then_inc(xn_turned, 1)
                        pe.wait_ge(xt_ready, c + 1)
                        pe.wait_ge(y_ready, c + 1)
                        nc.tensor.matmul(ps_h[:], win[:], xt[:], start=True, stop=True).then_inc(h_ready, 1)
                        pe.wait_ge(y_ready, c + 2)
                        pe.wait_ge(o_used, c + 1)
                        nc.tensor.matmul(ps_o[:].rearrange("p a b -> p (a b)"), g.ones[0:1, :], bo4[:].rearrange("p a b -> p (a b)"), start=True, stop=False, skip_group_check=True)
                        for k in range(CT):
                            last = nc.tensor.matmul(ps_o[:, k, :], y[:, u, k * P:k * P + P], woc[:], start=False, stop=True, skip_group_check=True)
                        last.then_inc(o_ready, 1)

            @block.vector
            def _(dve):
                norm.dve_rstd(dve)
                st = Chain(dve, setup)
                dve.wait_ge(e_ready, 1)
                st.link(nc.vector.tensor_scalar_add(cols[:, 6:7], cols[:, 6:7], 1.0))
                st.link(nc.vector.reciprocal(cols[:, 4:5], cols[:, 6:7]))
                nc.vector.tensor_copy(decay[:], cols[:, 4:5].to_broadcast([P, CHUNK]))
                nc.vector.tensor_tensor(cols[:, 5:6], cols[:, 2:3], cols[:, 0:1], ALU.mult)
                st.link(nc.vector.tensor_scalar(woc[:], wout[:], cols[:, 3:4], None, ALU.mult))
                dve.sem_inc(y_ready, 1)
                dve.sem_inc(o_used, 1)
                dve.sem_inc(consts_ready, 1)
                with dve.Fori(0, NC_ // 2) as i:
                    for u in range(2):
                        c = i * 2 + u
                        ch = Chain(dve, chain, c * STEPS)
                        norm.dve_rows(c).then_inc(xn_ready, 1)
                        dve.wait_ge(bh_ready, c + 1)
                        first = 0.0 if u == 0 else y[:, 0, CHUNK - 1:CHUNK]
                        nc.vector.tensor_tensor_scan(y[:, u, :], decay[:], bh[:], first, ALU.mult, ALU.add).then_inc(y_ready, 1)
                        hold(dve, o_ready, c + 1)
                        for k in range(CT):
                            last = nc.vector.bn_stats(raw[:, k, :], ps_o[:, k, :])
                        ch.link(last)
                        for k in range(CT):
                            last = nc.vector.bn_aggr(mv[:, k, :], raw[:, k, :])
                        last.then_inc(mv_ready, 1)
                        dve.wait_ge(so_ready, c + 1)
                        ch.link(nc.vector.reciprocal(ro[:], so[:]))
                        for k in range(CT):
                            last = nc.vector.tensor_scalar(t[:, k, :], ps_o[:, k, :], mv[:, k, 0:1], ro[:, k:k + 1], ALU.subtract, ALU.mult)
                        last.then_inc(o_used, 1)
                        dve.wait_ge(o_used, c + 2)
                        ch.link(nc.vector.tensor_tensor(t[:], t[:], bc(rows[:, 0, :], CT), ALU.mult))
                        ch.link(nc.vector.tensor_tensor(t[:], t[:], bc(rows[:, 1, :], CT), ALU.add))
                        xc = g.X[:, bass.ds(c * CT, CT), :]
                        ch.link(nc.vector.tensor_tensor(xc, xc, t[:], ALU.add))
                        ch.link(dve_new_stats(nc, dve, g, raw, c, ch))
                        assert ch.n == STEPS, ch.n
        s.clear()


def expert_layer(nc, g, name, experts, top, gate_w, up_g, up_u, down):
    IB = 4
    STEPS = 12 if top == 2 else 8
    with ExitStack() as ctx:
        s = Scope(nc, ctx, name)
        norm = Norm(nc, g, s)
        xt = s.sb("xt", [P, CHUNK])
        sg = s.sb("sg", [P, 2, CHUNK])
        hid = s.sb("hid", [P, 2 * IB, CHUNK])
        lg = s.sb("logits", [P, CT, 8])
        ex, wgap = s.sb("ex", [P, CT]), s.sb("wgap", [P, CT])
        top8, idx = s.sb("top8", [P, CT, 8]), s.sb("idx", [P, CT, 8], U32)
        idf = s.sb("idf", [P, CT, 8])
        hot = s.sb("hot", [P, 2, CT, 8])
        wsum, w2 = s.sb("wsum", [P, CT]), s.sb("w2", [P, 2, CT])
        tokw = s.sb("tokw", [P, CT, 8])
        raw = s.sb("raw", [P, CT, 6])
        ps_t, ps_l = s.ps("ps_t", [P, CHUNK]), s.ps("ps_l", [P, CT, 8])
        ps_g, ps_u = s.ps("ps_g", [P, 2, CHUNK]), s.ps("ps_u", [P, 2, CHUNK])
        ps_y = s.ps("ps_y", [P, 2, CT, P])
        chain = s.sem("chain")
        xn_ready, xn_turned, xt_ready = s.sem("xn_ready"), s.sem("xn_turned"), s.sem("xt_ready")
        lg_cleared, lg_ready, lg_copied = s.sem("lg_cleared"), s.sem("lg_ready"), s.sem("lg_copied")
        gap_ready, ex_ready = s.sem("gap_ready"), s.sem("ex_ready")
        gu_ready, silu_ready, hid_ready = s.sem("gu_ready"), s.sem("silu_ready"), s.sem("hid_ready")
        y_ready, y_used = s.sem("y_ready"), s.sem("y_used")
        NB = experts * IB

        with nc.Block() as block:
            @block.scalar
            def _(act):
                norm.act_std(act)
                with act.Fori(0, NC_) as c:
                    act.wait_ge(xn_turned, c + 1)
                    nc.scalar.activation(xt[:], ps_t[:], ACT.Copy).then_inc(xt_ready, 1)
                    if top == 2:
                        act.wait_ge(gap_ready, c + 1)
                        nc.scalar.activation(ex[:], wgap[:], ACT.Exp).then_inc(ex_ready, 1)
                    for b in range(NB):
                        act.wait_ge(gu_ready, c * NB + b + 1)
                        act.wait_ge(hid_ready, c * NB + b + 1)
                        nc.scalar.activation(sg[:, b % 2, :], ps_g[:, b % 2, :], ACT.Silu).then_inc(silu_ready, 1)

            @block.tensor
            def _(pe):
                def up(c, e):
                    for j in range(IB):
                        b = e * IB + j
                        pe.wait_ge(hid_ready, c * NB + b + 1)
                        nc.tensor.matmul(ps_g[:, b % 2, :], up_g(e, j), xt[:], start=True, stop=True)
                        nc.tensor.matmul(ps_u[:, b % 2, :], up_u(e, j), xt[:], start=True, stop=True).then_inc(gu_ready, 1)

                def rows(c, e):
                    pe.wait_ge(hid_ready, c * NB + e * IB + IB + 2)
                    pe.wait_ge(y_used, c * experts + e + 1)
                    for k in range(CT):
                        for j in range(IB):
                            b = e * IB + j
                            last = nc.tensor.matmul(ps_y[:, e % 2, k, :], hid[:, b % (2 * IB), k * P:k * P + P], down(e, j),
                                                    start=(j == 0), stop=(j == IB - 1))
                    last.then_inc(y_ready, 1)

                pe.sem_inc(y_ready, 2)
                with pe.Fori(0, NC_) as c:
                    pe.wait_ge(xn_ready, c + 1)
                    for k in range(CT):
                        last = nc.tensor.transpose(ps_t[:, k * P:k * P + P], norm.xn[:, k, :], g.ident[:])
                    last.then_inc(xn_turned, 1)
                    pe.wait_ge(xt_ready, c + 1)
                    for k in range(CT):
                        last = nc.tensor.matmul(ps_l[:, k, 0:experts], xt[:, k * P:k * P + P], gate_w[:], start=True, stop=True)
                    last.then_inc(lg_ready, 1)
                    for e in range(experts):
                        up(c, e)
                        if e:
                            rows(c, e - 1)
                    rows(c, experts - 1)

            @block.vector
            def _(dve):
                def weights(c, ch):
                    dve.wait_ge(lg_ready, c + 1)
                    nc.vector.tensor_copy(lg[:, :, 0:experts], ps_l[:, :, 0:experts]).then_inc(lg_copied, 1)
                    hold(dve, lg_copied, c + 1)
                    for k in range(CT):
                        last = nc.vector.max(top8[:, k, :], lg[:, k, :])
                    ch.link(last)
                    for k in range(CT):
                        last = nc.vector.max_index(idx[:, k, :], top8[:, k, :], lg[:, k, :])
                    ch.link(last)
                    ch.link(nc.vector.tensor_copy(idf[:, :, 0:2], idx[:, :, 0:2]))
                    for r in range(top):
                        last = nc.vector.tensor_tensor(hot[:, r], bc(g.iota8[:], CT), bl(idf[:, :, r], 8), ALU.is_equal)
                    ch.link(last)
                    if top == 1:
                        ch.link(nc.vector.tensor_copy(tokw[:], hot[:, 0]))
                        return
                    nc.vector.tensor_tensor(wgap[:], top8[:, :, 1], top8[:, :, 0], ALU.subtract).then_inc(gap_ready, 1)
                    dve.wait_ge(ex_ready, c + 1)
                    ch.link(nc.vector.tensor_scalar_add(wsum[:], ex[:], 1.0))
                    ch.link(nc.vector.reciprocal(w2[:, 0, :], wsum[:]))
                    ch.link(nc.vector.tensor_tensor(w2[:, 1, :], w2[:, 0, :], ex[:], ALU.mult))
                    for r in range(2):
                        last = nc.vector.tensor_tensor(hot[:, r], hot[:, r], bl(w2[:, r, :], 8), ALU.mult)
                    ch.link(last)
                    ch.link(nc.vector.tensor_tensor(tokw[:], hot[:, 0], hot[:, 1], ALU.add))

                def add_rows(c, e, ch):
                    dve.wait_ge(y_ready, c * experts + e + 3)
                    dve.wait_ge(y_used, c * experts + e + 2)
                    for k in range(CT):
                        xk = tile_of(g.X, c * CT + k)
                        last = nc.vector.scalar_tensor_tensor(xk, ps_y[:, e % 2, k, :], tokw[:, k, e:e + 1], xk, ALU.mult, ALU.add)
                    last.then_inc(y_used, 1)

                norm.dve_rstd(dve)
                nc.vector.memset(lg[:], -3.0e38).then_inc(lg_cleared, 1)
                dve.wait_ge(lg_cleared, 1)
                dve.sem_inc(hid_ready, 2)
                dve.sem_inc(y_used, 2)
                with dve.Fori(0, NC_) as c:
                    ch = Chain(dve, chain, c * STEPS)
                    norm.dve_rows(c).then_inc(xn_ready, 1)
                    weights(c, ch)
                    for e in range(experts):
                        for j in range(IB):
                            b = e * IB + j
                            dve.wait_ge(silu_ready, c * NB + b + 1)
                            if j == 0:
                                dve.wait_ge(y_ready, c * experts + e + 1)
                            nc.vector.tensor_tensor(hid[:, b % (2 * IB), :], sg[:, b % 2, :], ps_u[:, b % 2, :], ALU.mult).then_inc(hid_ready, 1)
                        if e:
                            add_rows(c, e - 1, ch)
                    add_rows(c, experts - 1, ch)
                    hold(dve, y_used, (c + 1) * experts + 2)
                    ch.link(dve_new_stats(nc, dve, g, raw, c, ch))
                    assert ch.n == STEPS, ch.n
        s.clear()


def landmark_layer(nc, g, wq, bq, wk, bk, wv, bv):
    TB = SEQ // P
    LM = 64
    RUN = SEQ // LM
    PER = P // RUN
    WIN = LM - PER
    with ExitStack() as ctx:
        s = Scope(nc, ctx, "lm")
        norm = Norm(nc, g, s)
        w = s.sb("w", [P, 3, P])
        brow = s.sb("brow", [1, 3, P])
        avg = s.sb("avg", [P, WIN + LM])
        xt = s.sb("xt", [P, 2, CHUNK])
        nmx, sums, rs = s.sb("nmx", [P, TB, 2]), s.sb("sums", [P, TB, 2]), s.sb("rs", [P, TB, 2])
        eq, ek = s.sb("eq", [P, 2, P]), s.sb("ek", [P, 2, P])
        kk, k3 = s.sb("kk", [P, 2, P]), s.sb("k3", [P, 2, P])
        eqt = s.sb("eqt", [P, TB, P])
        lm, mm, aa, nn = s.sb("lm", [LM, P]), s.sb("mm", [P, P]), s.sb("aa", [P, P]), s.sb("nn", [P, P])
        raw = s.sb("raw", [P, CT, 6])
        ps_t, ps_qkv, ps_o = s.ps("ps_t", [P, CT, P]), s.ps("ps_qkv", [P, 4, 512]), s.ps("ps_o", [P, CT, P])
        ps_m, ps_lm = s.ps("ps_m", [P, 512]), s.ps("ps_lm", [P, 512])
        loaded, made, chain = s.sem("loaded"), s.sem("made"), s.sem("chain")
        xn_ready, turned, copied = s.sem("xn_ready"), s.sem("turned"), s.sem("copied")
        qkv_ready, mx_ready, exp_ready = s.sem("qkv_ready"), s.sem("mx_ready"), s.sem("exp_ready")
        k3_ready, acc_done = s.sem("k3_ready"), s.sem("acc_done")
        mm_ready, a_done, a_ready, n_done, n_ready = (s.sem(n) for n in ("mm_ready", "a_done", "a_ready", "n_done", "n_ready"))
        o_ready, o_used = s.sem("o_ready"), s.sem("o_used")
        STEPS = TB + 6

        with nc.Block() as block:
            @block.sync
            def _(sp):
                for i, (m, b) in enumerate(((wq, bq), (wk, bk), (wv, bv))):
                    sp.dma_start(w[:, i, :], m).then_inc(loaded, 16)
                    sp.dma_start(brow[:, i, :], b.rearrange("(a n) -> a n", a=1)).then_inc(loaded, 16)

            @block.gpsimd
            def _(pool):
                nc.gpsimd.memset(avg[:], 1.0 / RUN).then_inc(made, 1)
                pool.wait_ge(made, 1)
                nc.gpsimd.affine_select(out=avg[:], in_=avg[:], compare_op=ALU.is_ge, fill=0.0, base=RUN * WIN,
                                        pattern=[[-RUN, WIN + LM]], channel_multiplier=1).then_inc(made, 1)
                pool.wait_ge(made, 2)
                nc.gpsimd.affine_select(out=avg[:], in_=avg[:], compare_op=ALU.is_ge, fill=0.0, base=RUN - 1 - RUN * WIN,
                                        pattern=[[RUN, WIN + LM]], channel_multiplier=-1).then_inc(made, 1)

            @block.scalar
            def _(act):
                norm.act_std(act)
                with act.Fori(0, BATCH) as b:
                    for h in range(2):
                        act.wait_ge(turned, b * 2 + h + 1)
                        nc.scalar.activation(xt[:, h, :], ps_t[:].rearrange("p a b -> p (a b)"), ACT.Copy).then_inc(copied, 1)
                    for t in range(TB + 1):
                        n = b * TB + t
                        if t < TB:
                            act.wait_ge(mx_ready, n + 1)
                            act.wait_ge(k3_ready, n + 3)
                            act.wait_ge(acc_done, n + 1)
                            nc.scalar.activation(ek[:, t % 2, :], ps_qkv[:, t % 4, P:2 * P], ACT.Exp, bias=nmx[:, t, 1:2], accum_out=sums[:, t, 1:2])
                            nc.scalar.activation(eq[:, t % 2, :], ps_qkv[:, t % 4, 0:P], ACT.Exp, bias=nmx[:, t, 0:1], accum_out=sums[:, t, 0:1]).then_inc(exp_ready, 1)
                        if t in (4, 8):
                            act.wait_ge(acc_done, n + 2)
                            nc.scalar.activation(eqt[:, t - 4:t, :], ps_t[:], ACT.Copy).then_inc(copied, 1)

            @block.tensor
            def _(pe):
                pe.wait_ge(loaded, 16 * 6)
                pe.wait_ge(made, 3)
                pe.sem_inc(acc_done, 2)
                with pe.Fori(0, BATCH) as b:
                    for h in range(2):
                        pe.wait_ge(xn_ready, b * 2 + h + 1)
                        pe.wait_ge(copied, b * 4 + h + 1)
                        for k in range(CT):
                            last = nc.tensor.transpose(ps_t[:, k, :], norm.xn[:, k, :], g.ident[:])
                        last.then_inc(turned, 1)
                    for t in range(TB + 1):
                        n = b * TB + t
                        if t < TB:
                            if t % CT == 0:
                                pe.wait_ge(copied, b * 4 + 2 + t // CT)
                            pe.wait_ge(k3_ready, n + 1)
                            if t >= 4:
                                pe.wait_ge(exp_ready, n - 3)
                            out = ps_qkv[:, t % 4, 0:3 * P]
                            nc.tensor.matmul(out, g.ones[0:1, :], brow[:].rearrange("p a b -> p (a b)"), start=True, stop=False)
                            nc.tensor.matmul(out, xt[:, t // CT, t % CT * P:t % CT * P + P], w[:].rearrange("p a b -> p (a b)"),
                                             start=False, stop=True).then_inc(qkv_ready, 1)
                        if t >= 1:
                            r = t - 1
                            pe.wait_ge(k3_ready, n + 4)
                            nc.tensor.matmul(ps_m[:, 0:P], kk[:, r % 2, :], k3[:, r % 2, :], start=(r == 0), stop=(r == TB - 1))
                            nc.tensor.matmul(ps_lm[0:LM, 0:P], avg[:, WIN - PER * r:WIN - PER * r + LM], kk[:, r % 2, :],
                                             start=(r == 0), stop=(r == TB - 1))
                            pe.wait_ge(exp_ready, n)
                            if r % 4 == 0:
                                pe.wait_ge(copied, b * 4 + 3 + r // 4)
                            nc.tensor.transpose(ps_t[:, r % 4, :], eq[:, r % 2, :], g.ident[:]).then_inc(acc_done, 1)
                    pe.wait_ge(mm_ready, b + 1)
                    nc.tensor.matmul(ps_o[:, 0, :], lm[:], lm[:], start=True, stop=True).then_inc(a_done, 1)
                    pe.wait_ge(a_ready, b + 1)
                    nc.tensor.matmul(ps_o[:, 1, :], aa[:], mm[:], start=True, stop=True).then_inc(n_done, 1)
                    pe.wait_ge(n_ready, b + 1)
                    pe.wait_ge(copied, b * 4 + 5)
                    for h in range(2):
                        if h:
                            pe.wait_ge(o_used, b * 2 + 1)
                        for k in range(CT):
                            last = nc.tensor.matmul(ps_o[:, k, :], eqt[:, h * CT + k, :], nn[:], start=True, stop=True)
                        last.then_inc(o_ready, 1)

            @block.vector
            def _(dve):
                norm.dve_rstd(dve)
                dve.sem_inc(k3_ready, 4)
                dve.sem_inc(copied, 1)
                with dve.Fori(0, BATCH) as b:
                    ch = Chain(dve, chain, b * STEPS)
                    for h in range(2):
                        if h:
                            dve.wait_ge(turned, b * 2 + 1)
                        norm.dve_rows(b * 2 + h).then_inc(xn_ready, 1)
                    for t in range(TB + 1):
                        n = b * TB + t
                        if t < TB:
                            dve.wait_ge(qkv_ready, n + 1)
                            nc.vector.tensor_reduce(nmx[:, t, :], ps_qkv[:, t % 4, 0:2 * P].rearrange("p (a b) -> p a b", a=2),
                                                    AX_X, ALU.max, negate=True).then_inc(mx_ready, 1)
                        if t >= 1:
                            r = t - 1
                            dve.wait_ge(exp_ready, n)
                            ch.link(nc.vector.reciprocal(rs[:, r, :], sums[:, r, :]))
                            dve.wait_ge(acc_done, n)
                            nc.vector.tensor_scalar(kk[:, r % 2, :], ek[:, r % 2, :], rs[:, r, 1:2], None, ALU.mult)
                            nc.vector.scalar_tensor_tensor(k3[:, r % 2, :], ek[:, r % 2, :], rs[:, r, 1:2], ps_qkv[:, r % 4, 2 * P:3 * P],
                                                           ALU.mult, ALU.mult).then_inc(k3_ready, 1)
                    dve.wait_ge(acc_done, b * TB + TB + 2)
                    nc.vector.tensor_copy(lm[:], ps_lm[0:LM, 0:P])
                    nc.vector.tensor_copy(mm[:], ps_m[:, 0:P]).then_inc(mm_ready, 1)
                    dve.wait_ge(a_done, b + 1)
                    nc.vector.tensor_copy(aa[:], ps_o[:, 0, :]).then_inc(a_ready, 1)
                    dve.wait_ge(n_done, b + 1)
                    nc.vector.tensor_copy(nn[:], ps_o[:, 1, :]).then_inc(n_ready, 1)
                    for h in range(2):
                        c = b * 2 + h
                        dve.wait_ge(o_ready, c + 1)
                        for k in range(CT):
                            t = h * CT + k
                            xk = tile_of(g.X, b * TB + t)
                            last = nc.vector.scalar_tensor_tensor(xk, ps_o[:, k, :], rs[:, t, 0:1], xk, ALU.mult, ALU.add)
                        last.then_inc(o_used, 1)
                        hold(dve, o_used, c + 1)
                        ch.link(dve_new_stats(nc, dve, g, raw, c, ch))
                    assert ch.n == STEPS, ch.n
        s.clear()


def causal_layer(nc, g, wq, bq, wk, bk, wv, bv, wp, bp, table, wq_sw, bq_sw, wk_sw, bk_sw, rope, onehot):
    H, D = 16, 8
    TB = SEQ // P
    NP = 3
    KD = NP * NP * D
    KM = KD + NP
    G4 = 4
    NG = H // G4
    SCALE = 1.0 / D ** 0.5
    NEG = -1.0e30
    W2 = 2 * P
    blocks = [(q4, kt) for q4 in range(2) for kt in range(4 * q4 + 4)]
    NS = NG * len(blocks) * G4
    BF = mybir.dt.bfloat16

    def span(q4, kt):
        lo, hi = max(kt * P, q4 * CHUNK), q4 * CHUNK + CHUNK
        return lo, min(max(kt * P + W2, lo), hi), hi

    near_of, last_of = {}, []
    i = 0
    for _ in range(NG):
        for q4, kt in blocks:
            for _ in range(G4):
                if span(q4, kt)[0] < span(q4, kt)[1]:
                    near_of[i] = len(near_of)
                i += 1
            if kt == 4 * q4 + 3:
                last_of.append(i - 1)
    NN = len(near_of)
    STEPS = 3 + 2 * NG + 2 * 4

    with ExitStack() as ctx:
        s = Scope(nc, ctx, "ca")
        norm = Norm(nc, g, s)
        w = s.sb("w", [P, 6, P])
        bcol = s.sb("bcol", [P, 4])
        brow = s.sb("brow", [1, 2, CT, P])
        cs = s.sb("cs", [P, 2, SEQ])
        bias_q = s.sb("bias_q", [P, H, W2])
        bias_k = s.sb("bias_k", [P, H, W2])
        xt = s.sb("xt", [P, 2, CHUNK])
        t1, t2 = s.sb("t1", [P, 2, CHUNK]), s.sb("t2", [P, 2, CHUNK])
        full = s.sb("full", [P, 2, SEQ])
        piece = s.sb("piece", [P, NP, SEQ], BF)
        qst, kst = s.sb("qst", [KM, H, SEQ], BF), s.sb("kst", [KM, H, SEQ], BF)
        vp = s.sb("vp", [P, TB, H, D + 1])
        m_near, m_far, m_all = s.sb("m_near", [P, H * TB]), s.sb("m_far", [P, H * TB]), s.sb("m_all", [P, H * TB])
        m_rest, m_piece = s.sb("m_rest", [P, P]), s.sb("m_piece", [P, NP, P], BF)
        near = s.sb("near", [P, 4, W2])
        pt = s.sb("pt", [P, 8, CHUNK])
        ysb, yrs = s.sb("ysb", [P, CHUNK]), s.sb("yrs", [P, CT, G4])
        yy = s.sb("yy", [P, TB, P])
        zero_row = s.sb("zero_row", [1, CHUNK])
        raw = s.sb("raw", [P, CT, 6])
        ps = s.ps("ps", [P, 8, 512])
        dram_bias = nc.dram_tensor("scratch_bias", (2, H, 384), F32).ap()
        dram_toeplitz = nc.dram_tensor("scratch_toeplitz", (2, H, P, W2), F32).ap()
        dram_piece = nc.dram_tensor("scratch_piece", (2, NP, P, SEQ), BF).ap()
        dram_max = nc.dram_tensor("scratch_max", (NP, H * TB, P), BF).ap()

        loaded, bias_made, bias_stored, bias_loaded = (s.sem(n) for n in ("loaded", "bias_made", "bias_stored", "bias_loaded"))
        filled, buckets_ready, bias_ready = s.sem("filled"), s.sem("buckets_ready"), s.sem("bias_ready")
        chain = s.sem("chain")
        xn_ready, turned, xt_ready = s.sem("xn_ready"), s.sem("turned"), s.sem("xt_ready")
        proj_ready, proj_used, v_ready, v_used = (s.sem(n) for n in ("proj_ready", "proj_used", "v_ready", "v_used"))
        full_ready, piece1, rest1, piece2, piece3 = (s.sem(n) for n in ("full_ready", "piece1", "rest1", "piece2", "piece3"))
        pieces_stored, stacks_loaded = s.sem("pieces_stored"), s.sem("stacks_loaded")
        sq_ready, sq_used = s.sem("sq_ready"), s.sem("sq_used")
        m_ready, mt_ready, mp_ready, mp_stored, mp_loaded = (s.sem(n) for n in ("m_ready", "mt_ready", "mp_ready", "mp_stored", "mp_loaded"))
        st_ready, near_ready, p_ready, pv_done = (s.sem(n) for n in ("st_ready", "near_ready", "p_ready", "pv_done"))
        y_copied, yt_ready, yy_ready = (s.sem(n) for n in ("y_copied", "yt_ready", "yy_ready"))
        t_ready, t_copied, o_ready = (s.sem(n) for n in ("t_ready", "t_copied", "o_ready"))
        YB = NG * 2

        with nc.Block() as block:
            @block.sync
            def _(sp):
                for i, m in enumerate((wq, wq_sw, wk, wk_sw, wv, wp)):
                    sp.dma_start(w[:, i, :], m).then_inc(loaded, 16)
                for i, m in enumerate((bq, bq_sw, bk, bk_sw)):
                    sp.dma_start(bcol[:, i:i + 1], m.rearrange("(p a) -> p a", a=1)).then_inc(loaded, 16)
                for i, m in enumerate((bv, bp)):
                    for k in range(CT):
                        sp.dma_start(brow[:, i, k, :], m.rearrange("(a n) -> a n", a=1)).then_inc(loaded, 16)
                sp.dma_start(cs[:], rope).then_inc(loaded, 16)
                sp.dma_start(m_near[0:32, 0:H], table).then_inc(loaded, 16)
                sp.dma_start(near[0:33, 0:3, :].rearrange("p a b -> p (a b)"), onehot).then_inc(loaded, 16)
                sp.wait_ge(bias_made, 2)
                sp.dma_start(dram_bias.rearrange("a h n -> h a n"), full[0:H, :, 0:384]).then_inc(bias_stored, 16)
                sp.wait_ge(bias_stored, 16)
                for side, offset in ((1, P - 1), (0, P)):
                    sp.dma_start(dram_toeplitz[side], bass.AP(dram_bias.tensor, side * H * 384 + offset, [[384, H], [-1, P], [1, W2]])).then_inc(bias_stored, 16)
                sp.wait_ge(bias_stored, 48)
                for bias, side in ((bias_q, 1), (bias_k, 0)):
                    sp.dma_start(bias[:], dram_toeplitz[side].rearrange("h p w -> p h w")).then_inc(bias_loaded, 16)
                with sp.Fori(0, BATCH) as b:
                    for side in range(2):
                        hold(sp, piece3, b * 2 + side + 1)
                        sp.dma_start(dram_piece[side].rearrange("n p t -> p n t"), piece[:]).then_inc(pieces_stored, 16)
                        hold(sp, pieces_stored, b * 32 + side * 16 + 16)
                        for a in range(NP):
                            for c in range(NP):
                                r = (a * NP + c) * D
                                dst = (qst, kst)[side]
                                src = dram_piece[side, (a, c)[side]].rearrange("(h d) t -> d h t", d=D)
                                sp.dma_start(dst[r:r + D], src).then_inc(stacks_loaded, 16)
                    hold(sp, stacks_loaded, b * 288 + 288)
                    hold(sp, mp_ready, b + 1)
                    sp.dma_start(dram_max.rearrange("n p t -> p n t"), m_piece[:]).then_inc(mp_stored, 16)
                    hold(sp, mp_stored, b * 16 + 16)
                    sp.dma_start(qst[KD:KM].rearrange("p h t -> p (h t)"), dram_max.rearrange("n p t -> n (p t)")).then_inc(mp_loaded, 16)
                    hold(sp, mp_loaded, b * 16 + 16)
                    hold(sp, o_ready, b * 2 + 2)

            @block.gpsimd
            def _(pool):
                nc.gpsimd.memset(vp[:, :, :, D:D + 1], 1.0).then_inc(filled, 1)
                pool.wait_ge(filled, 1)
                nc.gpsimd.memset(zero_row[:], 0.0).then_inc(filled, 1)
                pool.wait_ge(filled, 2)
                nc.gpsimd.memset(m_near[32:33, 0:H], 1.0).then_inc(filled, 1)
                pool.wait_ge(filled, 3)
                nc.gpsimd.memset(m_far[:], NEG).then_inc(filled, 1)
                pool.wait_ge(filled, 4)
                nc.gpsimd.memset(kst[64:KM], 1.0).then_inc(filled, 1)
                with pool.Fori(0, BATCH) as b:
                    for side in range(2):
                        pool.wait_ge(piece1, b * 2 + side + 1)
                        nc.gpsimd.tensor_tensor(full[:, side], full[:, side], piece[:, 0, :], ALU.subtract).then_inc(rest1, 1)
                        pool.wait_ge(piece2, b * 2 + side + 1)
                        nc.gpsimd.tensor_tensor(piece[:, 2, :], full[:, side], piece[:, 1, :], ALU.subtract).then_inc(piece3, 1)

            @block.scalar
            def _(act):
                norm.act_std(act)
                act.sem_inc(p_ready, 4)
                act.wait_ge(bias_ready, 1)
                with act.Fori(0, BATCH) as b:
                    for h in range(2):
                        act.wait_ge(turned, b * 2 + h + 1)
                        nc.scalar.activation(xt[:, h, :], ps[:, 4, :], ACT.Copy).then_inc(xt_ready, 1)
                    for side in range(2):
                        n = b * 2 + side
                        act.wait_ge(full_ready, b * 2 + 2)
                        if side:
                            act.wait_ge(pieces_stored, b * 32 + 16)
                        nc.scalar.activation(piece[:, 0, :], full[:, side], ACT.Copy).then_inc(piece1, 1)
                        act.wait_ge(rest1, n + 1)
                        nc.scalar.activation(piece[:, 1, :], full[:, side], ACT.Copy).then_inc(piece2, 1)

                    def copy_y(n):
                        act.wait_ge(pv_done, b * NS + last_of[n] + 9)
                        nc.scalar.activation(ysb[:], ps[:, 6, :], ACT.Copy).then_inc(y_copied, 1)

                    i = 0
                    for gr in range(NG):
                        for q4, kt in blocks:
                            lo, mid, hi = span(q4, kt)
                            c0 = q4 * CHUNK
                            for j in range(G4):
                                act.wait_ge(st_ready, b * NS + i + 1)
                                act.wait_ge(pv_done, b * NS + i + 1)
                                out, src = pt[:, i % 8, :], ps[:, i % 6, :]
                                if lo < mid:
                                    act.wait_ge(near_ready, b * NN + near_of[i] + 1)
                                if mid < hi:
                                    ins = nc.scalar.activation(out[:, mid - c0:hi - c0], src[:, mid - c0:hi - c0], ACT.Exp, scale=SCALE)
                                if lo < mid:
                                    ins = nc.scalar.activation(out[:, lo - c0:mid - c0], near[:, i % 4, 0:mid - lo], ACT.Exp, scale=SCALE)
                                ins.then_inc(p_ready, 1)
                                i += 1
                            if kt == 0 and (gr, q4) != (0, 0):
                                copy_y(gr * 2 + q4 - 1)
                    copy_y(YB - 1)
                    for h in range(2):
                        act.wait_ge(t_ready, b * 2 + h + 1)
                        nc.scalar.activation(pt[:, h, :], ps[:, h, :], ACT.Copy).then_inc(t_copied, 1)

            @block.tensor
            def _(pe):
                pe.wait_ge(loaded, 16 * 21)
                pe.wait_ge(filled, 5)
                for a in range(2):
                    nc.tensor.matmul(ps[0:H, a, 0:384], m_near[0:33, 0:H],
                                     near[0:33, 0:3, :].rearrange("p a b -> p (a b)")[:, a * 384:a * 384 + 384],
                                     start=True, stop=True).then_inc(buckets_ready, 1)
                nc.tensor.matmul(ps[:, 6, :], g.ones[0:1, :], zero_row[:], start=True, stop=True)
                pe.sem_inc(pv_done, 8)
                pe.wait_ge(bias_ready, 1)
                with pe.Fori(0, BATCH) as b:
                    for h in range(2):
                        pe.wait_ge(xn_ready, b * 2 + h + 1)
                        if h:
                            pe.wait_ge(xt_ready, b * 2 + 1)
                        for k in range(CT):
                            last = nc.tensor.transpose(ps[:, 4, k * P:k * P + P], norm.xn[:, k, :], g.ident[:])
                        last.then_inc(turned, 1)
                    for h in range(2):
                        n = b * 2 + h
                        pe.wait_ge(xt_ready, n + 1)
                        pe.wait_ge(proj_used, n + 1)
                        for i in range(4):
                            last = nc.tensor.matmul(ps[:, i, :], w[:, i, :], xt[:, h, :], start=True, stop=True)
                        last.then_inc(proj_ready, 1)
                        pe.wait_ge(v_used, n + 1)
                        nc.tensor.matmul(ps[:, 5, :], g.ones[0:1, :], brow[:, 0].rearrange("p a b -> p (a b)"), start=True, stop=False, skip_group_check=True)
                        for k in range(CT):
                            last = nc.tensor.matmul(ps[:, 5, k * P:k * P + P], xt[:, h, k * P:k * P + P], w[:, 4, :], start=False, stop=True, skip_group_check=True)
                        last.then_inc(v_ready, 1)

                    pe.wait_ge(proj_used, b * 2 + 3)
                    pe.wait_ge(v_used, b * 2 + 3)
                    pe.wait_ge(stacks_loaded, b * 288 + 288)
                    for h in range(H):
                        for qt in range(TB):
                            i = h * TB + qt
                            pe.wait_ge(sq_used, b * H * TB + i + 1)
                            r = 2 * (i % 3)
                            end = (qt + 1) * P
                            for c in range(0, end, 512):
                                e = min(c + 512, end)
                                last = nc.tensor.matmul(ps[:, r + c // 512, 0:e - c], qst[0:KD, h, qt * P:qt * P + P], kst[0:KD, h, c:e], start=True, stop=True)
                            last.then_inc(sq_ready, 1)
                    pe.wait_ge(m_ready, b + 1)
                    nc.tensor.transpose(ps[:, 7, 0:P], m_all[:], g.ident[:]).then_inc(mt_ready, 1)
                    pe.wait_ge(mp_loaded, b * 16 + 16)

                    def products(gr, q4, kt, i):
                        lo, _, hi = span(q4, kt)
                        c0 = q4 * CHUNK
                        if kt == 0:
                            pe.wait_ge(y_copied, b * YB + gr * 2 + q4 + 1)
                        for j in range(G4):
                            pe.wait_ge(p_ready, b * NS + i + j + 5)
                            nc.tensor.matmul(ps[32 * j:32 * j + D + 1, 6, lo - c0:hi - c0], vp[:, kt, gr * G4 + j, :], pt[:, (i + j) % 8, lo - c0:hi - c0],
                                             start=(kt == 0), stop=(kt == 4 * q4 + 3), skip_group_check=True).then_inc(pv_done, 1)

                    def turn_y(n):
                        pe.wait_ge(y_copied, b * YB + n + 2)
                        pe.wait_ge(yy_ready, b * YB + n + 1)
                        for k in range(CT):
                            last = nc.tensor.transpose(ps[:, 7, k * P:k * P + P], ysb[:, k * P:k * P + P], g.ident[:])
                        last.then_inc(yt_ready, 1)

                    i = 0
                    before = None
                    for gr in range(NG):
                        for q4, kt in blocks:
                            lo, _, hi = span(q4, kt)
                            c0 = q4 * CHUNK
                            for j in range(G4):
                                if i + j >= 6:
                                    pe.wait_ge(p_ready, b * NS + i + j - 1)
                                nc.tensor.matmul(ps[:, (i + j) % 6, lo - c0:hi - c0], kst[:, gr * G4 + j, kt * P:kt * P + P], qst[:, gr * G4 + j, lo:hi],
                                                 start=True, stop=True).then_inc(st_ready, 1)
                            if before:
                                products(*before)
                            if kt == 3 and (gr, q4) != (0, 0):
                                turn_y(gr * 2 + q4 - 1)
                            before = (gr, q4, kt, i)
                            i += G4
                    products(*before)
                    turn_y(YB - 1)
                    for h in range(2):
                        pe.wait_ge(yy_ready, b * YB + YB + 1)
                        pe.wait_ge(p_ready, b * NS + NS + 4)
                        for k in range(CT):
                            last = nc.tensor.transpose(ps[:, h, k * P:k * P + P], yy[:, h * CT + k, :], g.ident[:])
                        last.then_inc(t_ready, 1)
                    for h in range(2):
                        pe.wait_ge(t_copied, b * 2 + h + 1)
                        nc.tensor.matmul(ps[:, 2 + h, :], g.ones[0:1, :], brow[:, 1].rearrange("p a b -> p (a b)"), start=True, stop=False, skip_group_check=True)
                        for k in range(CT):
                            last = nc.tensor.matmul(ps[:, 2 + h, k * P:k * P + P], pt[:, h, k * P:k * P + P], w[:, 5, :], start=False, stop=True, skip_group_check=True)
                        last.then_inc(o_ready, 1)

            @block.vector
            def _(dve):
                norm.dve_rstd(dve)
                dve.wait_ge(buckets_ready, 2)
                dve.wait_ge(filled, 4)
                nc.vector.tensor_copy(full[0:H, 0, 0:384], ps[0:H, 0, 0:384]).then_inc(bias_made, 1)
                nc.vector.tensor_copy(full[0:H, 1, 0:384], ps[0:H, 1, 0:384]).then_inc(bias_made, 1)
                dve.sem_inc(proj_used, 1)
                dve.sem_inc(v_used, 1)
                dve.sem_inc(sq_used, 3)
                dve.sem_inc(y_copied, 1)
                dve.sem_inc(yy_ready, 1)
                dve.wait_ge(bias_loaded, 32)
                dve.sem_inc(bias_ready, 2)
                with dve.Fori(0, BATCH) as b:
                    ch = Chain(dve, chain, b * STEPS)
                    for h in range(2):
                        if h:
                            dve.wait_ge(turned, b * 2 + 1)
                        norm.dve_rows(b * 2 + h).then_inc(xn_ready, 1)
                    for h in range(2):
                        n = b * 2 + h
                        tt = slice(h * CHUNK, h * CHUNK + CHUNK)
                        dve.wait_ge(proj_ready, n + 1)
                        for side in range(2):
                            i = 2 * side
                            nc.vector.scalar_tensor_tensor(t1[:, side], ps[:, i, :], bcol[:, i:i + 1], cs[:, 0, tt], ALU.add, ALU.mult)
                            last = nc.vector.scalar_tensor_tensor(t2[:, side], ps[:, i + 1, :], bcol[:, i + 1:i + 2], cs[:, 1, tt], ALU.add, ALU.mult)
                        last.then_inc(proj_used, 1)
                        dve.wait_ge(proj_used, n + 2)
                        nc.vector.tensor_tensor(full[:, :, tt], t1[:], t2[:], ALU.add).then_inc(full_ready, 1)
                        dve.wait_ge(full_ready, n + 1)
                        dve.wait_ge(v_ready, n + 1)
                        nc.vector.tensor_copy(vp[:, h * CT:h * CT + CT, :, 0:D], ps[:, 5, :].rearrange("p (t h d) -> p t h d", t=CT, d=D)).then_inc(v_used, 1)

                    for h in range(H):
                        for qt in range(TB):
                            i = h * TB + qt
                            hold(dve, sq_ready, b * H * TB + i + 1)
                            r = 2 * (i % 3)
                            rows = ps[:, r:r + 2, :].rearrange("p a b -> p (a b)")
                            lo = max(qt - 1, 0) * P
                            hi = qt * P + P
                            if lo:
                                nc.vector.tensor_reduce(m_far[:, i:i + 1], rows[:, 0:lo], AX_X, ALU.max)
                            nc.vector.tensor_tensor_reduce(near[:, i % 4, 0:hi - lo], rows[:, lo:hi], bias_q[:, h, W2 - (hi - lo):W2], 1.0, NEG,
                                                           ALU.add, ALU.max, m_near[:, i:i + 1]).then_inc(sq_used, 1)
                    dve.wait_ge(sq_used, b * H * TB + H * TB + 3)
                    nc.vector.tensor_tensor(m_all[:], m_near[:], m_far[:], ALU.max).then_inc(m_ready, 1)
                    dve.wait_ge(mt_ready, b + 1)
                    ch.link(nc.vector.tensor_scalar(m_piece[:, 0, :], ps[:, 7, 0:P], -1.0, None, ALU.mult))
                    ch.link(nc.vector.scalar_tensor_tensor(m_rest[:], ps[:, 7, 0:P], -1.0, m_piece[:, 0, :], ALU.mult, ALU.subtract))
                    ch.link(nc.vector.tensor_copy(m_piece[:, 1, :], m_rest[:]))
                    nc.vector.tensor_tensor(m_piece[:, 2, :], m_rest[:], m_piece[:, 1, :], ALU.subtract).then_inc(mp_ready, 1)

                    def norm_y(n):
                        gr, q4 = n // 2, n % 2
                        dve.wait_ge(yt_ready, b * YB + n + 1)
                        turned_y = ps[:, 7, :].rearrange("p (t j d) -> p t j d", t=CT, j=G4)
                        ch.link(nc.vector.reciprocal(yrs[:], turned_y[:, :, :, D]))
                        nc.vector.tensor_tensor(yy[:, q4 * CT:q4 * CT + CT, gr * G4 * D:gr * G4 * D + G4 * D].rearrange("p t (j d) -> p t j d", d=D),
                                                turned_y[:, :, :, 0:D], yrs[:].unsqueeze(3).to_broadcast([P, CT, G4, D]), ALU.mult).then_inc(yy_ready, 1)

                    i = 0
                    for gr in range(NG):
                        for q4, kt in blocks:
                            lo, mid, hi = span(q4, kt)
                            c0 = q4 * CHUNK
                            for j in range(G4):
                                if lo < mid:
                                    dve.wait_ge(st_ready, b * NS + i + 1)
                                    dve.wait_ge(p_ready, b * NS + i + 1)
                                    nc.vector.tensor_tensor(near[:, i % 4, 0:mid - lo], ps[:, i % 6, lo - c0:mid - c0],
                                                            bias_k[:, gr * G4 + j, lo - kt * P:mid - kt * P], ALU.add).then_inc(near_ready, 1)
                                i += 1
                            if kt == 3 and (gr, q4) != (0, 0):
                                norm_y(gr * 2 + q4 - 1)
                    norm_y(YB - 1)
                    for h in range(2):
                        c = b * 2 + h
                        dve.wait_ge(o_ready, c + 1)
                        xc = g.X[:, bass.ds(c * CT, CT), :]
                        ch.link(nc.vector.tensor_tensor(xc, ps[:, 2 + h, :].rearrange("p (t d) -> p t d", t=CT), xc, ALU.add))
                        ch.link(dve_new_stats(nc, dve, g, raw, c, ch))
                    assert ch.n == STEPS, ch.n
        s.clear()


def memory_layer(nc, g, wq, wq_sw, wk, wk_sw, wv, w_out, ln_g, ln_b, mem_beta, rope):
    H, D, SEG = 16, 64, 32
    W = SEQ // SEG
    QH = 4
    NQ = H // QH
    PB = QH // 2
    SCALE = D ** -0.5
    E1 = D + 1
    STEPS = NQ * 8
    with ExitStack() as ctx:
        s = Scope(nc, ctx, "im")
        norm = Norm(nc, g, s)
        w4 = s.sb("w4", [P, 4, H // 2, P])
        wv_s = s.sb("wv", [P, H * D])
        wo = s.sb("wo", [P, H // 2, P])
        lncol = s.sb("lncol", [P, 2])
        cs = s.sb("cs", [P, 2, SEG])
        mask = s.sb("mask", [P, SEG])
        gate = s.sb("gate", [P, 3, H])
        XT = s.sb("xt_all", [P, W, BATCH * SEG])
        xw = s.sb("xw", [P, P])
        ee, rr = s.sb("ee", [P, 4 * P]), s.sb("rr", [P, 4 * P])
        t1, t2 = s.sb("t1", [P, 4 * P]), s.sb("t2", [P, 4 * P])
        rope_qk = s.sb("rope_qk", [P, 2, 2 * PB, P])
        el = s.sb("el", [P, 2, 2 * PB, P])
        mem = s.sb("mem", [P, NQ, PB, BATCH, E1])
        zinc = s.sb("zinc", [P, NQ, PB, BATCH])
        vt = s.sb("vt", [P, NQ, QH, D])
        skt = s.sb("skt", [P, NQ, PB, P])
        u1, uu = s.sb("u1", [P, QH, D]), s.sb("uu", [P, 2, QH, D])
        rd = s.sb("rd", [P, QH])
        s1, s2 = s.sb("s1", [P, QH, SEG]), s.sb("s2", [P, QH, SEG])
        pe_, pt = s.sb("pe_", [P, QH, SEG]), s.sb("pt", [P, 2, QH, SEG])
        mx, sm, rs = s.sb("mx", [P, QH]), s.sb("sm", [P, 2, QH]), s.sb("rs", [P, QH])
        dn = s.sb("dn", [P, QH])
        m1, m2 = s.sb("m1", [P, 2, QH, D]), s.sb("m2", [P, QH, D])
        oo = s.sb("oo", [P, H * D])
        ot = s.sb("ot", [P, H // 2, P])
        raw = s.sb("raw", [P, CT, 6])
        b_a, b_s, b_v, b_sc, b_pv, b_pr, b_nu, b_up = (s.ps(n, [P, 512]) for n in ("b_a", "b_s", "b_v", "b_sc", "b_pv", "b_pr", "b_nu", "b_up"))

        names = ("loaded", "made", "g_ready", "setup", "chain", "xn_ready", "turned", "xt_ready", "xw_ready", "proj_ready", "v_ready",
                 "er_ready", "v_copied", "ab_used", "el_ready", "rope_ready", "sk_turned", "sk_copied", "prev_ready", "num_ready", "s_ready",
                 "s1_ready", "s2_ready", "p_ready", "pt_ready", "u_ready", "m1_ready", "pv_ready", "upd_ready", "m2_ready",
                 "mem_ready", "prev_even", "s_even", "num_even", "upd_turns", "pv_turns", "o_ready", "ot_ready", "ot_copied", "out_ready", "x_ready", "stats")
        S = {n: s.sem(n) for n in names}

        def score_view(ap):
            return ap[:, 0:QH * SEG].rearrange("p (h k) -> p h k", h=QH)

        def head_view(ap, width):
            return ap[:, 0:QH * width].rearrange("p (h d) -> p h d", h=QH)

        with nc.Block() as block:
            @block.sync
            def _(sp):
                for i, m in enumerate((wq, wq_sw, wk, wk_sw)):
                    sp.dma_start(w4[:, i], m.rearrange("d (n f) -> d n f", f=P)).then_inc(S["loaded"], 16)
                sp.dma_start(wv_s[:], wv).then_inc(S["loaded"], 16)
                sp.dma_start(wo[:], w_out.rearrange("(n f) d -> f n d", f=P)).then_inc(S["loaded"], 16)
                sp.dma_start(lncol[:, 0:1], ln_g.rearrange("(p a) -> p a", a=1)).then_inc(S["loaded"], 16)
                sp.dma_start(lncol[:, 1:2], ln_b.rearrange("(p a) -> p a", a=1)).then_inc(S["loaded"], 16)
                sp.dma_start(cs[:], rope).then_inc(S["loaded"], 16)
                sp.dma_start(gate[:, 0, :], mem_beta.rearrange("a h b c -> (a h b c)").partition_broadcast(P)).then_inc(S["loaded"], 16)

            @block.gpsimd
            def _(pool):
                nc.gpsimd.memset(mask[:], 0.0).then_inc(S["made"], 1)
                for b in range(BATCH):
                    pool.wait_ge(S["made"], b + 1)
                    nc.gpsimd.affine_select(out=mask[32 * b:32 * b + 32, :], in_=mask[32 * b:32 * b + 32, :], compare_op=ALU.is_ge, fill=-1.0e30,
                                            base=0, pattern=[[-1, SEG]], channel_multiplier=1).then_inc(S["made"], 1)
                pool.wait_ge(S["made"], 5)
                nc.gpsimd.memset(mem[:], 0.0).then_inc(S["made"], 1)
                pool.wait_ge(S["made"], 6)
                nc.gpsimd.memset(mem[:, :, :, :, D], 1.0e-6).then_inc(S["made"], 1)
                with pool.Fori(0, W) as w:
                    for slot in range(NQ + 2):
                        if slot < NQ:
                            k = w * NQ + slot
                            pool.wait_ge(S["ab_used"], k + 2)
                            pool.wait_ge(S["s_ready"], k)  if slot >= 2 else None
                            nc.gpsimd.tensor_tensor(rope_qk[:, slot % 2].rearrange("p a b -> p (a b)"), t1[:], t2[:], ALU.add).then_inc(S["rope_ready"], 1)
                        if slot >= 2:
                            q = slot - 2
                            pool.wait_ge(S["m2_ready"], w * NQ + q + 1)
                            nc.gpsimd.tensor_tensor(oo[:, q * QH * D:(q + 1) * QH * D].rearrange("p (h d) -> p h d", h=QH), m1[:, q % 2], m2[:], ALU.add).then_inc(S["o_ready"], 1)

            @block.scalar
            def _(act):
                norm.act_std(act)
                act.wait_ge(S["loaded"], 160)
                nc.scalar.activation(gate[:, 1, :], gate[:, 0, :], ACT.Exp, scale=-1.0).then_inc(S["g_ready"], 1)
                with act.Fori(0, BATCH) as b:
                    for h in range(2):
                        act.wait_ge(S["turned"], b * 2 + h + 1)
                        out = XT[:, h * 16:h * 16 + 16, bass.ds(b * SEG, SEG)]
                        nc.scalar.activation(out, b_a[:].rearrange("p (w t) -> p w t", t=SEG), ACT.Identity, scale=lncol[:, 0:1], bias=lncol[:, 1:2]).then_inc(S["xt_ready"], 1)
                act.wait_ge(S["xt_ready"], 8)
                with act.Fori(0, W) as w:
                    act.wait_ge(S["x_ready"], w + 1)
                    nc.scalar.activation(xw[:], XT[:, bass.ds(w, 1), :].rearrange("p a b -> p (a b)"), ACT.Copy).then_inc(S["xw_ready"], 1)
                    for slot in range(NQ + 1):
                        if slot < NQ:
                            k = w * NQ + slot
                            act.wait_ge(S["proj_ready"], k + 1)
                            act.wait_ge(S["el_ready"], k + 1)
                            nc.scalar.activation(ee[:], b_a[:], ACT.Exp)
                            nc.scalar.activation(rr[:], b_a[:], ACT.Relu).then_inc(S["er_ready"], 1)
                            act.wait_ge(S["v_ready"], k + 1)
                            nc.scalar.activation(vt[:, slot].rearrange("p a b -> p (a b)"), b_v[:, 0:QH * D], ACT.Copy).then_inc(S["v_copied"], 1)
                        if slot >= 1:
                            k, q = w * NQ + slot - 1, slot - 1
                            act.wait_ge(S["sk_turned"], k + 1)
                            nc.scalar.activation(skt[:, q].rearrange("p a b -> p (a b)"), b_up[:, 0:PB * P], ACT.Copy).then_inc(S["sk_copied"], 1)
                            act.wait_ge(S["s2_ready"], k + 1)
                            nc.scalar.activation(pe_[:], s2[:], ACT.Exp, scale=SCALE).then_inc(S["p_ready"], 1)
                    act.wait_ge(S["ot_ready"], w + 1)
                    nc.scalar.activation(ot[:, 0:4].rearrange("p a b -> p (a b)"), b_a[:], ACT.Copy)
                    nc.scalar.activation(ot[:, 4:8].rearrange("p a b -> p (a b)"), b_s[:], ACT.Copy).then_inc(S["ot_copied"], 1)

            @block.tensor
            def _(pe):
                def project(w, q):
                    k = w * NQ + q
                    pe.wait_ge(S["ab_used"], k + 1)
                    x = XT[:, bass.ds(w, 1), :].rearrange("p a b -> p (a b)")
                    for i in range(2):
                        for n in range(PB):
                            c = (i * PB + n) * P
                            nc.tensor.matmul(b_a[:, c:c + P], w4[:, 2 * i, q * PB + n, :], x, start=True, stop=True)
                            last = nc.tensor.matmul(b_s[:, c:c + P], w4[:, 2 * i + 1, q * PB + n, :], x, start=True, stop=True)
                    last.then_inc(S["proj_ready"], 1)
                    pe.wait_ge(S["v_copied"], k + 1)
                    nc.tensor.matmul(b_v[:, 0:QH * D], xw[:], wv_s[:, q * QH * D:(q + 1) * QH * D], start=True, stop=True).then_inc(S["v_ready"], 1)

                def for_heads(parity, fn):
                    half = slice(D * parity, D * parity + D)
                    for blk in range(PB):
                        for b in range(BATCH):
                            last = fn(2 * blk + parity, half, blk, b, slice(SEG * b, SEG * b + SEG))
                    return last

                def read(w, q):
                    k = w * NQ + q
                    r = q % 2
                    pe.wait_ge(S["el_ready"], k + 2)
                    pe.wait_ge(S["mem_ready"], k + 1 if q == 0 else k)
                    if q == 1:
                        pe.wait_ge(S["sk_copied"], k)
                    for n in range(PB):
                        last = nc.tensor.transpose(b_up[:, n * P:n * P + P], el[:, r, PB + n, :], g.ident[:])
                    last.then_inc(S["sk_turned"], 1)
                    prev = lambda h, half, blk, b, tok: nc.tensor.matmul(b_pr[tok, h * E1:h * E1 + E1], el[half, r, PB + blk, tok], mem[half, q, blk, b, :], start=True, stop=True, skip_group_check=True)
                    score = lambda h, half, blk, b, tok: nc.tensor.matmul(b_sc[tok, h * SEG:h * SEG + SEG], rope_qk[half, r, blk, tok], rope_qk[half, r, PB + blk, tok], start=True, stop=True, skip_group_check=True)
                    num = lambda h, half, blk, b, tok: nc.tensor.matmul(b_nu[tok, h * E1:h * E1 + E1], el[half, r, blk, tok], mem[half, q, blk, b, :], start=True, stop=True, skip_group_check=True)
                    hold(pe, S["u_ready"], k + 1)
                    for_heads(0, prev).then_inc(S["prev_even"], 1)
                    hold(pe, S["rope_ready"], k + 1)
                    hold(pe, S["s1_ready"], k + 1)
                    for_heads(0, score).then_inc(S["s_even"], 1)
                    hold(pe, S["prev_even"], k + 1)
                    for_heads(1, prev).then_inc(S["prev_ready"], 1)
                    hold(pe, S["m1_ready"], k + 1)
                    for_heads(0, num).then_inc(S["num_even"], 1)
                    hold(pe, S["s_even"], k + 1)
                    for_heads(1, score).then_inc(S["s_ready"], 1)
                    hold(pe, S["num_even"], k + 1)
                    for_heads(1, num).then_inc(S["num_ready"], 1)

                def write(w, q):
                    k = w * NQ + q
                    r = q % 2
                    pe.wait_ge(S["sk_copied"], w * NQ + min(q + 1, NQ - 1) + 1)
                    if q == NQ - 1:
                        hold(pe, S["mem_ready"], k + 1)
                    hold(pe, S["u_ready"], k + 2)
                    hold(pe, S["pt_ready"], k + 1)
                    hold(pe, S["m2_ready"], k) if q else None
                    for b in range(BATCH):
                        tok = slice(SEG * b, SEG * b + SEG)
                        if b:
                            hold(pe, S["upd_turns"], (BATCH - 1) * k + b)
                        for h in range(QH):
                            half, c = slice(D * (h % 2), D * (h % 2) + D), (h // 2 * BATCH + b) * D
                            last = nc.tensor.matmul(b_up[half, c:c + D], skt[tok, q, h // 2, half], uu[tok, r, h, :], start=True, stop=True, skip_group_check=True)
                        last.then_inc(S["upd_turns" if b < BATCH - 1 else "upd_ready"], 1)
                        if b:
                            hold(pe, S["pv_turns"], (BATCH - 1) * k + b)
                        for h in range(QH):
                            last = nc.tensor.matmul(b_pv[tok, h * D:h * D + D], pt[tok, r, h, :], vt[tok, q, h, :], start=True, stop=True, skip_group_check=True)
                        last.then_inc(S["pv_turns" if b < BATCH - 1 else "pv_ready"], 1)

                pe.wait_ge(S["loaded"], 160)
                pe.wait_ge(S["made"], 7)
                with pe.Fori(0, 2 * BATCH) as c:
                    pe.wait_ge(S["xn_ready"], c + 1)
                    for n in range(CT):
                        last = nc.tensor.transpose(b_a[:, n * P:n * P + P], norm.xn[:, n, :], g.ident[:])
                    last.then_inc(S["turned"], 1)
                with pe.Fori(0, W) as w:
                    pe.wait_ge(S["xw_ready"], w + 1)
                    for slot in range(NQ + 2):
                        if slot < NQ:
                            project(w, slot)
                        if 1 <= slot <= NQ:
                            read(w, slot - 1)
                        if slot >= 2:
                            write(w, slot - 2)
                    pe.wait_ge(S["o_ready"], w * NQ + NQ)
                    pe.wait_ge(S["ab_used"], w * NQ + NQ + 1)
                    for n in range(H // 2):
                        last = nc.tensor.transpose((b_a, b_s)[n // 4][:, n % 4 * P:n % 4 * P + P], oo[:, n * P:n * P + P], g.ident[:])
                    last.then_inc(S["ot_ready"], 1)
                    pe.wait_ge(S["ot_copied"], w + 1)
                    pe.wait_ge(S["v_copied"], w * NQ + NQ + 1)
                    for n in range(H // 2):
                        last = nc.tensor.matmul(b_v[:, 0:P], ot[:, n, :], wo[:, n, :], start=(n == 0), stop=(n == H // 2 - 1))
                    last.then_inc(S["out_ready"], 1)

            @block.vector
            def _(dve):
                norm.dve_rstd(dve)
                st = Chain(dve, S["setup"])
                dve.wait_ge(S["g_ready"], 1)
                dve.wait_ge(S["made"], 7)
                st.link(nc.vector.tensor_scalar_add(gate[:, 2, :], gate[:, 1, :], 1.0))
                st.link(nc.vector.reciprocal(gate[:, 1, :], gate[:, 2, :]))
                st.link(nc.vector.tensor_scalar(gate[:, 2, :], gate[:, 1, :], -1.0, 1.0, ALU.mult, ALU.add))
                for n, credit in (("ab_used", 1), ("v_copied", 1), ("el_ready", 1), ("mem_ready", 1), ("u_ready", 1), ("s1_ready", 1), ("m1_ready", 1), ("x_ready", 1)):
                    dve.sem_inc(S[n], credit)
                with dve.Fori(0, 2 * BATCH) as c:
                    norm.dve_rows(c).then_inc(S["xn_ready"], 1)
                    dve.wait_ge(S["xt_ready"], c + 1)

                def inputs(w, q, ch):
                    k = w * NQ + q
                    dve.wait_ge(S["proj_ready"], k + 1)
                    dve.wait_ge(S["rope_ready"], k) if q else None
                    seg = lambda ap: ap.rearrange("p (n t) -> p n t", t=SEG)
                    tab = lambda i: bc(cs[:, i, :], 4 * P // SEG)
                    nc.vector.tensor_tensor(seg(t2[:]), seg(b_s[:]), tab(1), ALU.mult)
                    dve.wait_ge(S["er_ready"], k + 1)
                    nc.vector.tensor_tensor(seg(t1[:]), seg(b_a[:]), tab(0), ALU.mult).then_inc(S["ab_used"], 1)
                    e2 = el[:, q % 2].rearrange("p a b -> p (a b)")
                    nc.vector.scalar_tensor_tensor(e2, ee[:], 1.0, rr[:], ALU.min, ALU.add).then_inc(S["el_ready"], 1)
                    dve.wait_ge(S["el_ready"], k + 2)
                    nc.vector.tensor_reduce(zinc[:, q].rearrange("p a b -> p (a b)"), el[:, q % 2, PB:2 * PB].rearrange("p a (b t) -> p (a b) t", t=SEG), AX_X, ALU.add)

                def middle(w, q, ch):
                    k = w * NQ + q
                    r = q % 2
                    pr, nu = head_view(b_pr, E1), head_view(b_nu, E1)
                    dve.wait_ge(S["prev_ready"], k + 1)
                    ch.link(nc.vector.reciprocal(rd[:], pr[:, :, D]))
                    ch.link(nc.vector.tensor_tensor(u1[:], pr[:, :, 0:D], bl(rd[:], D), ALU.mult))
                    dve.wait_ge(S["v_copied"], k + 2)
                    nc.vector.tensor_tensor(uu[:, r], vt[:, q], u1[:], ALU.subtract).then_inc(S["u_ready"], 1)
                    dve.wait_ge(S["s_ready"], k + 1)
                    nc.vector.tensor_tensor(s1[:], score_view(b_sc), bc(mask[:], QH), ALU.add).then_inc(S["s1_ready"], 1)
                    dve.wait_ge(S["s1_ready"], k + 2)
                    ch.link(nc.vector.tensor_reduce(mx[:], s1[:], AX_X, ALU.max))
                    nc.vector.tensor_tensor(s2[:], s1[:], bl(mx[:], SEG), ALU.subtract).then_inc(S["s2_ready"], 1)
                    dve.wait_ge(S["num_ready"], k + 1)
                    ch.link(nc.vector.tensor_scalar_add(dn[:], nu[:, :, D], 1.0e-6))
                    ch.link(nc.vector.reciprocal(dn[:], dn[:]))
                    ch.link(nc.vector.tensor_tensor(dn[:], dn[:], gate[:, 1, q * QH:q * QH + QH], ALU.mult))
                    if q >= 2:
                        hold(dve, S["o_ready"], k - 1)
                    nc.vector.tensor_tensor(m1[:, r], nu[:, :, 0:D], bl(dn[:], D), ALU.mult).then_inc(S["m1_ready"], 1)
                    dve.wait_ge(S["p_ready"], k + 1)
                    nc.vector.tensor_reduce(sm[:, r], pe_[:], AX_X, ALU.add)
                    nc.vector.transpose(pt[:, r].rearrange("p a b -> p (a b)"), pe_[:].rearrange("p a b -> p (a b)")).then_inc(S["pt_ready"], 1)

                def outputs(w, q, ch):
                    k = w * NQ + q
                    r = q % 2
                    dve.wait_ge(S["upd_ready"], k + 1)
                    m = mem[:, q].rearrange("p a b e -> p (a b) e")
                    nc.vector.tensor_tensor(m[:, :, 0:D], m[:, :, 0:D], b_up[:].rearrange("p (n d) -> p n d", d=D), ALU.add)
                    dve.wait_ge(S["num_ready"], k + 1)
                    nc.vector.tensor_tensor(m[:, :, D], m[:, :, D], zinc[:, q].rearrange("p a b -> p (a b)"), ALU.add).then_inc(S["mem_ready"], 1)
                    dve.wait_ge(S["pt_ready"], k + 1)
                    ch.link(nc.vector.reciprocal(rs[:], sm[:, r]))
                    ch.link(nc.vector.tensor_tensor(rs[:], rs[:], gate[:, 2, q * QH:q * QH + QH], ALU.mult))
                    dve.wait_ge(S["pv_ready"], k + 1)
                    dve.wait_ge(S["o_ready"], k) if q else None
                    nc.vector.tensor_tensor(m2[:], head_view(b_pv, D), bl(rs[:], D), ALU.mult).then_inc(S["m2_ready"], 1)

                with dve.Fori(0, W // 4) as w4i:
                    for j in range(4):
                        w = w4i * 4 + j
                        ch = Chain(dve, S["chain"], w * STEPS)
                        for slot in range(NQ + 2):
                            if slot < NQ:
                                inputs(w, slot, ch)
                            if 1 <= slot <= NQ:
                                middle(w, slot - 1, ch)
                            if slot >= 2:
                                outputs(w, slot - 2, ch)
                        dve.wait_ge(S["out_ready"], w + 1)
                        for b in range(BATCH):
                            rows = g.X[32 * j:32 * j + 32, bass.ds(w4i + b * (SEQ // P), 1), :].rearrange("p a d -> p (a d)")
                            last = nc.vector.tensor_tensor(rows, b_v[32 * b:32 * b + 32, 0:P], rows, ALU.add)
                        last.then_inc(S["x_ready"], 1)
                        assert ch.n == STEPS, ch.n
                dve.wait_ge(S["x_ready"], W + 1)
                with dve.Fori(0, NC_) as c:
                    ch = Chain(dve, S["stats"], c * 3)
                    ch.link(dve_new_stats(nc, dve, g, raw, c, ch))
        s.clear()


class Globals:
    pass


STAGES = list(range(8))


def build(nc, a, out):
    with ExitStack() as ctx:
        s = Scope(nc, ctx, "g")
        g = Globals()
        g.X = s.sb("x", [P, NT, P])
        g.MV, g.mv4 = s.sb("mv", [P, NT, 2]), s.sb("mv4", [P, CT, 2])
        g.ident, g.ones = s.sb("ident", [P, P]), s.sb("ones", [P, P])
        g.eps, g.iota8 = s.sb("eps", [P, 1]), s.sb("iota8", [P, 8])
        g.stored = s.sem("stored")
        E0, E1 = a["L0_ffn_gate"].shape[1], a["L1_ffn_w_router"].shape[1]
        first_weights, later_weights = ctx.enter_context(ExitStack()), ctx.enter_context(ExitStack())
        s0 = Scope(nc, first_weights, "w0")
        w1, w3, w2 = (s0.sb(n, sh) for n, sh in (("w1", [P, E0, 512]), ("w3", [P, E0, 512]), ("w2", [P, E0, 4, P])))
        gate = s0.sb("gate", [P, E0])
        g.weights_loaded = s.sem("weights_loaded")

        def load_weights(sp):
            for dst, src in ((gate[:], a["L0_ffn_gate"]), (w1[:], a["L0_ffn_experts_w1"].rearrange("e h i -> h e i")),
                             (w3[:], a["L0_ffn_experts_w3"].rearrange("e h i -> h e i")),
                             (w2[:], a["L0_ffn_experts_w2"].rearrange("e (b i) h -> i e b h", i=P))):
                sp.dma_start(dst, src).then_inc(g.weights_loaded, 16)
            sp.wait_ge(g.weights_loaded, 16 * 4)
        g.load_weights = load_weights
        later = {}

        def load_later_weights():
            s1 = Scope(nc, later_weights, "w1")
            wv, wp, router = (s1.sb(n, sh) for n, sh in (("wv", [P, E1, 1024]), ("wproj", [P, E1, 4, P]), ("router", [P, E1])))
            later.update(wv=wv, wp=wp, router=router)
            with nc.Block() as block:
                @block.sync
                def _(sp):
                    for dst, src in ((router[:], a["L1_ffn_w_router"]), (wv[:], a["L1_ffn_w_v"].rearrange("e d h -> d e h")),
                                     (wp[:], a["L1_ffn_w_proj"].rearrange("e (b i) d -> i e b d", i=P))):
                        sp.dma_start(dst, src).then_inc(g.weights_loaded, 16)
                    sp.wait_ge(g.weights_loaded, 16 * 7)

        load_and_constants(nc, g, a["L0_attn_a_x"])

        def l0_experts(name):
            expert_layer(nc, g, name, E0, 2, gate, lambda e, j: w1[:, e, j * P:j * P + P], lambda e, j: w3[:, e, j * P:j * P + P], lambda e, j: w2[:, e, j, :])

        def l1_experts(name):
            if not later:
                load_later_weights()
            wv, wp, router = later["wv"], later["wp"], later["router"]
            expert_layer(nc, g, name, E1, 1, router, lambda e, j: wv[:, e, j * P:j * P + P], lambda e, j: wv[:, e, 512 + j * P:512 + j * P + P], lambda e, j: wp[:, e, j, :])

        layers = [
            lambda: ssm_layer(nc, g, *(a["L0_attn_a_" + n] for n in ("W_in", "b_in", "log_A", "B_p", "C_p", "W_out", "b_out", "gamma", "beta"))),
            lambda: l0_experts("ffn0"),
            lambda: landmark_layer(nc, g, *(a["L0_attn_b_" + n] for n in ("Wq", "bq", "Wk", "bk", "Wv", "bv"))),
            lambda: l0_experts("ffn1"),
            lambda: causal_layer(nc, g, *(a["L1_attn_a_" + n] for n in ("Wq", "bq", "Wk", "bk", "Wv", "bv", "Wp", "bp", "rel_bias_table", "Wq_swapped", "bq_swapped", "Wk_swapped", "bk_swapped")), a["rope_a"], a["buckets"]),
            lambda: l1_experts("ffn2"),
            lambda: memory_layer(nc, g, a["wq_halves"], a["wq_swapped"], a["wk_halves"], a["wk_swapped"], a["wv"], *(a["L1_attn_b_" + n] for n in ("w_out", "ln_g", "ln_b", "mem_beta")), a["rope_b"]),
            lambda: l1_experts("ffn3"),
        ]
        for n in STAGES:
            if n == 4:
                first_weights.close()
            layers[n]()
        later_weights.close()
        with nc.Block() as block:
            @block.sync
            def _(sp):
                sp.dma_start(out.rearrange("b (n p) d -> p (b n) d", p=P), g.X[:]).then_inc(g.stored, 16)
                sp.wait_ge(g.stored, 16)


def shape_constants():
    import math

    import numpy as np

    T, D = 1024, 8
    inv = (1.0 / 10000.0 ** (np.arange(0, D, 2, dtype=np.float32) / D)).astype(np.float32)
    ang = (np.arange(T, dtype=np.float32)[None, :] * inv[:, None]).astype(np.float32)
    cos, sin = np.cos(ang), np.sin(ang)
    rope = np.stack([np.tile(np.concatenate([cos, cos]), (16, 1)), np.tile(np.concatenate([-sin, sin]), (16, 1))], 1)

    def bucket(n):
        if n < 16:
            return n
        big = np.log(np.float32(n) / np.float32(16)) / np.float32(math.log(8.0)) * np.float32(16)
        return min(16 + int(big), 31)

    pick = np.zeros((33, 2, 384), np.float32)
    for u in range(384):
        for side, n in ((0, u - 128), (1, 255 - u)):
            if n < 0:
                pick[32, side, u] = -1.0e30
            else:
                pick[bucket(n), side, u] += 1.0
                pick[31, side, u] -= 1.0
    freq = 10000.0 ** (-np.arange(0, 64, 2, dtype=np.float64) / 64)
    ang = freq[:, None] * np.arange(32)[None, :]
    cos, sin = np.cos(ang), np.sin(ang)
    rope_b = np.stack([np.tile(np.concatenate([cos, cos]), (2, 1)), np.tile(np.concatenate([-sin, sin]), (2, 1))], 1)
    return rope.astype(np.float32), pick.reshape(33, 768), rope_b.astype(np.float32)


_INS = ['L0_attn_a_x', 'L0_attn_a_W_in', 'L0_attn_a_b_in', 'L0_attn_a_log_A', 'L0_attn_a_B_p', 'L0_attn_a_C_p', 'L0_attn_a_W_out', 'L0_attn_a_b_out', 'L0_attn_a_gamma', 'L0_attn_a_beta', 'L0_attn_b_Wq', 'L0_attn_b_bq', 'L0_attn_b_Wk', 'L0_attn_b_bk', 'L0_attn_b_Wv', 'L0_attn_b_bv', 'L0_ffn_gate', 'L0_ffn_experts_w1', 'L0_ffn_experts_w2', 'L0_ffn_experts_w3', 'L1_attn_a_Wq', 'L1_attn_a_bq', 'L1_attn_a_Wk', 'L1_attn_a_bk', 'L1_attn_a_Wv', 'L1_attn_a_bv', 'L1_attn_a_Wp', 'L1_attn_a_bp', 'L1_attn_a_rel_bias_table', 'L1_attn_b_w_qkv', 'L1_attn_b_w_out', 'L1_attn_b_ln_g', 'L1_attn_b_ln_b', 'L1_attn_b_mem_beta', 'L1_ffn_w_router', 'L1_ffn_w_v', 'L1_ffn_w_proj']


def kernel(**inputs):
    import numpy as _np
    import concourse.bacc as _bacc
    from concourse import mybir as _mybir
    from concourse.bass_utils import run_bass_kernel_spmd as _run

    laid = dict(inputs)
    for name in ("L0_attn_a_W_in", "L0_attn_a_W_out"):
        laid[name] = _np.asarray(inputs[name]).T
    for name in ("Wq", "bq", "Wk", "bk"):
        m = _np.asarray(inputs["L1_attn_a_" + name])
        laid["L1_attn_a_" + name + "_swapped"] = m.reshape(m.shape[:-1] + (16, 2, 4))[..., ::-1, :].reshape(m.shape)
    qkv = _np.asarray(inputs["L1_attn_b_w_qkv"])
    for i, side in enumerate("qk"):
        m = qkv[:, i * 1024:i * 1024 + 1024].reshape(128, 16, 32, 2)
        laid["w" + side + "_halves"] = m.transpose(0, 1, 3, 2).reshape(128, 1024)
        laid["w" + side + "_swapped"] = m[..., ::-1].transpose(0, 1, 3, 2).reshape(128, 1024)
    laid["wv"] = qkv[:, 2048:]
    del laid["L1_attn_b_w_qkv"]
    laid["rope_a"], laid["buckets"], laid["rope_b"] = shape_constants()
    nc = _bacc.Bacc("TRN2", target_bir_lowering=False, num_devices=1)
    arrays, aps = {}, {}
    for name in laid:
        arr = _np.ascontiguousarray(laid[name])
        arrays[f"in_{name}_dram"] = arr
        aps[name] = nc.dram_tensor(f"in_{name}_dram", arr.shape, _mybir.dt.from_np(arr.dtype), kind="ExternalInput").ap()
    out = nc.dram_tensor("out_0_dram", (4, 1024, 128), _mybir.dt.float32, kind="ExternalOutput").ap()
    build(nc, aps, out)
    r = _run(nc, [arrays], core_ids=[0])
    return r.results[0]["out_0_dram"]
```

```python
from contextlib import ExitStack

import concourse.bass as bass
from concourse import mybir

F32 = mybir.dt.float32
U32 = mybir.dt.uint32
I32 = mybir.dt.int32
ALU = mybir.AluOpType
ACT = mybir.ActivationFunctionType
AX_X = mybir.AxisListType.X

P = 128
BATCH, SEQ = 4, 1024
NT = BATCH * SEQ // P
CT = 4
CHUNK = CT * P
NC_ = NT // CT
EPS = 1e-5


class Scope:

    def __init__(self, nc, ctx, prefix):
        self.nc, self.ctx, self.prefix, self.sems = nc, ctx, prefix, []

    def sb(self, name, shape, dt=F32):
        return self.ctx.enter_context(self.nc.sbuf_tensor(f"{self.prefix}_{name}", shape, dt))

    def ps(self, name, shape, dt=F32):
        return self.ctx.enter_context(self.nc.psum_tensor(f"{self.prefix}_{name}", shape, dt))

    def sem(self, name):
        self.sems.append(self.nc.alloc_semaphore(f"{self.prefix}_{name}"))
        return self.sems[-1]

    def clear(self):
        self.nc.clear_and_free_semaphores(self.sems)
        self.nc.all_engine_barrier()


class Chain:

    def __init__(self, eng, sem, base=0):
        self.eng, self.sem, self.base, self.n = eng, sem, base, 0

    def mark(self, ins):
        self.n += 1
        return ins.then_inc(self.sem, 1)

    def wait(self):
        hold(self.eng, self.sem, self.base + self.n)

    def link(self, ins):
        self.mark(ins)
        self.wait()


def hold(eng, sem, value):
    eng.wait_ge(sem, value)
    eng.nop(nofuse=True)


def bc(ap, k):
    return ap.unsqueeze(1).to_broadcast([ap.shape[0], k, ap.shape[1]])


def bl(ap, n):
    return ap.unsqueeze(2).to_broadcast([ap.shape[0], ap.shape[1], n])


def tile_of(t, n):
    return t[:, bass.ds(n, 1), :].rearrange("p a d -> p (a d)")


def some(k):
    return not isinstance(k, int) or k > 0


def load_and_constants(nc, g, x):
    with ExitStack() as ctx:
        s = Scope(nc, ctx, "init")
        raw = s.sb("raw", [P, NT, 6])
        x_loaded, zeroed = s.sem("x_loaded"), s.sem("zeroed")
        stats_done = s.sem("stats_done")
        with nc.Block() as block:
            @block.sync
            def _(sp):
                xs = x.rearrange("b (n p) d -> p (b n) d", p=P)
                for c in range(NC_):
                    sp.dma_start(g.X[:, CT * c:CT * c + CT, :], xs[:, CT * c:CT * c + CT, :]).then_inc(x_loaded, 16)
                g.load_weights(sp)

            @block.gpsimd
            def _(pool):
                nc.gpsimd.memset(g.ident[:], 0.0).then_inc(zeroed, 1)
                nc.gpsimd.memset(g.eps[:], EPS)
                nc.gpsimd.memset(g.ones[:], 1.0)
                nc.gpsimd.iota(g.iota8[:], pattern=[[1, 8]], base=0, channel_multiplier=0,
                               allow_small_or_imprecise_dtypes=True)
                pool.wait_ge(zeroed, 1)
                nc.gpsimd.affine_select(out=g.ident[:], in_=g.ident[:], compare_op=ALU.not_equal, fill=1.0,
                                        base=0, pattern=[[-1, P]], channel_multiplier=1)

            @block.vector
            def _(dve):
                dve.wait_ge(x_loaded, 16 * NC_)
                for n in range(NT):
                    last = nc.vector.bn_stats(raw[:, n, :], g.X[:, n, :])
                last.then_inc(stats_done, 1)
                dve.wait_ge(stats_done, 1)
                for n in range(NT):
                    nc.vector.bn_aggr(g.MV[:, n, :], raw[:, n, :])
        s.clear()


class Norm:

    def __init__(self, nc, g, s, bufs=1):
        self.nc, self.g = nc, g
        self.std = s.sb("std", [P, NT])
        self.RS = s.sb("rstd", [P, NT])
        self.xn = s.sb("xn", [P, CT, P])
        self.std_ready, self.rs_ready = s.sem("std_ready"), s.sem("rs_ready")

    def act_std(self, act):
        self.nc.scalar.activation(self.std[:], self.g.MV[:, :, 1], ACT.Sqrt, bias=self.g.eps[:, 0:1]).then_inc(self.std_ready, 1)

    def dve_rstd(self, dve):
        dve.wait_ge(self.std_ready, 1)
        self.nc.vector.reciprocal(self.RS[:], self.std[:]).then_inc(self.rs_ready, 1)
        dve.wait_ge(self.rs_ready, 1)

    def dve_rows(self, c):
        for k in range(CT):
            n = c * CT + k
            last = self.nc.vector.tensor_scalar(self.xn[:, k, :], tile_of(self.g.X, n),
                                                tile_of(self.g.MV, n)[:, 0:1], self.RS[:, bass.ds(n, 1)],
                                                ALU.subtract, ALU.mult)
        return last


def dve_new_stats(nc, dve, g, raw, c, ch):
    for k in range(CT):
        last = nc.vector.bn_stats(raw[:, k, :], tile_of(g.X, c * CT + k))
    ch.link(last)
    for k in range(CT):
        last = nc.vector.bn_aggr(g.mv4[:, k, :], raw[:, k, :])
    ch.link(last)
    return nc.vector.tensor_copy(g.MV[:, bass.ds(c * CT, CT), :], g.mv4[:])


def ssm_layer(nc, g, w_in_t, b_in, log_a, b_p, c_p, w_out_t, b_out, gamma, beta):
    with ExitStack() as ctx:
        s = Scope(nc, ctx, "ssm")
        norm = Norm(nc, g, s)
        win, wout, woc = s.sb("win", [P, P]), s.sb("wout", [P, P]), s.sb("woc", [P, P])
        cols = s.sb("cols", [P, 8])
        decay = s.sb("decay", [P, CHUNK])
        rows = s.sb("rows", [P, 2, P])
        bo4 = s.sb("bo4", [1, CT, P])
        xt = s.sb("xt", [P, CHUNK])
        bh = s.sb("bh", [P, CHUNK])
        y = s.sb("y", [P, 2, CHUNK])
        t = s.sb("t", [P, CT, P])
        raw, mv = s.sb("raw", [P, CT, 6]), s.sb("mv", [P, CT, 2])
        so, ro = s.sb("so", [P, CT]), s.sb("ro", [P, CT])
        ps_t, ps_h, ps_o = s.ps("ps_t", [P, CHUNK]), s.ps("ps_h", [P, CHUNK]), s.ps("ps_o", [P, CT, P])
        loaded = s.sem("loaded")
        setup, chain, e_ready = s.sem("setup"), s.sem("chain"), s.sem("e_ready")
        consts_ready = s.sem("consts_ready")
        xn_ready, xn_turned, xt_ready = s.sem("xn_ready"), s.sem("xn_turned"), s.sem("xt_ready")
        h_ready, bh_ready, y_ready, o_ready = s.sem("h_ready"), s.sem("bh_ready"), s.sem("y_ready"), s.sem("o_ready")
        mv_ready, so_ready, o_used = s.sem("mv_ready"), s.sem("so_ready"), s.sem("o_used")
        STEPS = 8

        with nc.Block() as block:
            @block.sync
            def _(sp):
                for dst, src in ((win[:], w_in_t), (wout[:], w_out_t),
                                 (cols[:, 0:1], b_in.rearrange("(p a) -> p a", a=1)),
                                 (cols[:, 1:2], log_a.rearrange("h (d a) -> (h d) a", a=1)),
                                 (cols[:, 2:3], b_p.rearrange("h (d a) -> (h d) a", a=1)),
                                 (cols[:, 3:4], c_p.rearrange("h (d a) -> (h d) a", a=1)),
                                 (rows[:, 0, :], gamma.partition_broadcast(P)),
                                 (rows[:, 1, :], beta.partition_broadcast(P))):
                    sp.dma_start(dst, src).then_inc(loaded, 16)
                for k in range(CT):
                    sp.dma_start(bo4[:, k, :], b_out.rearrange("(a n) -> a n", a=1)).then_inc(loaded, 16)

            @block.scalar
            def _(act):
                norm.act_std(act)
                act.wait_ge(loaded, 16 * 12)
                nc.scalar.activation(cols[:, 6:7], cols[:, 1:2], ACT.Exp).then_inc(e_ready, 1)
                act.wait_ge(consts_ready, 1)
                with act.Fori(0, NC_) as c:
                    act.wait_ge(xn_turned, c + 1)
                    nc.scalar.activation(xt[:], ps_t[:], ACT.Copy).then_inc(xt_ready, 1)
                    act.wait_ge(h_ready, c + 1)
                    act.wait_ge(y_ready, c + 1)
                    nc.scalar.activation(bh[:], ps_h[:], ACT.Identity, bias=cols[:, 5:6], scale=cols[:, 2:3]).then_inc(bh_ready, 1)
                    act.wait_ge(mv_ready, c + 1)
                    nc.scalar.activation(so[:], mv[:, :, 1], ACT.Sqrt, bias=g.eps[:, 0:1]).then_inc(so_ready, 1)

            @block.tensor
            def _(pe):
                pe.wait_ge(consts_ready, 1)
                with pe.Fori(0, NC_ // 2) as i:
                    for u in range(2):
                        c = i * 2 + u
                        pe.wait_ge(xn_ready, c + 1)
                        for k in range(CT):
                            last = nc.tensor.transpose(ps_t[:, k * P:k * P + P], norm.xn[:, k, :], g.ident[:])
                        last.then_inc(xn_turned, 1)
                        pe.wait_ge(xt_ready, c + 1)
                        pe.wait_ge(y_ready, c + 1)
                        nc.tensor.matmul(ps_h[:], win[:], xt[:], start=True, stop=True).then_inc(h_ready, 1)
                        pe.wait_ge(y_ready, c + 2)
                        pe.wait_ge(o_used, c + 1)
                        nc.tensor.matmul(ps_o[:].rearrange("p a b -> p (a b)"), g.ones[0:1, :], bo4[:].rearrange("p a b -> p (a b)"), start=True, stop=False, skip_group_check=True)
                        for k in range(CT):
                            last = nc.tensor.matmul(ps_o[:, k, :], y[:, u, k * P:k * P + P], woc[:], start=False, stop=True, skip_group_check=True)
                        last.then_inc(o_ready, 1)

            @block.vector
            def _(dve):
                norm.dve_rstd(dve)
                st = Chain(dve, setup)
                dve.wait_ge(e_ready, 1)
                st.link(nc.vector.tensor_scalar_add(cols[:, 6:7], cols[:, 6:7], 1.0))
                st.link(nc.vector.reciprocal(cols[:, 4:5], cols[:, 6:7]))
                nc.vector.tensor_copy(decay[:], cols[:, 4:5].to_broadcast([P, CHUNK]))
                nc.vector.tensor_tensor(cols[:, 5:6], cols[:, 2:3], cols[:, 0:1], ALU.mult)
                st.link(nc.vector.tensor_scalar(woc[:], wout[:], cols[:, 3:4], None, ALU.mult))
                dve.sem_inc(y_ready, 1)
                dve.sem_inc(o_used, 1)
                dve.sem_inc(consts_ready, 1)
                with dve.Fori(0, NC_ // 2) as i:
                    for u in range(2):
                        c = i * 2 + u
                        ch = Chain(dve, chain, c * STEPS)
                        norm.dve_rows(c).then_inc(xn_ready, 1)
                        dve.wait_ge(bh_ready, c + 1)
                        first = 0.0 if u == 0 else y[:, 0, CHUNK - 1:CHUNK]
                        nc.vector.tensor_tensor_scan(y[:, u, :], decay[:], bh[:], first, ALU.mult, ALU.add).then_inc(y_ready, 1)
                        hold(dve, o_ready, c + 1)
                        for k in range(CT):
                            last = nc.vector.bn_stats(raw[:, k, :], ps_o[:, k, :])
                        ch.link(last)
                        for k in range(CT):
                            last = nc.vector.bn_aggr(mv[:, k, :], raw[:, k, :])
                        last.then_inc(mv_ready, 1)
                        dve.wait_ge(so_ready, c + 1)
                        ch.link(nc.vector.reciprocal(ro[:], so[:]))
                        for k in range(CT):
                            last = nc.vector.tensor_scalar(t[:, k, :], ps_o[:, k, :], mv[:, k, 0:1], ro[:, k:k + 1], ALU.subtract, ALU.mult)
                        last.then_inc(o_used, 1)
                        dve.wait_ge(o_used, c + 2)
                        ch.link(nc.vector.tensor_tensor(t[:], t[:], bc(rows[:, 0, :], CT), ALU.mult))
                        ch.link(nc.vector.tensor_tensor(t[:], t[:], bc(rows[:, 1, :], CT), ALU.add))
                        xc = g.X[:, bass.ds(c * CT, CT), :]
                        ch.link(nc.vector.tensor_tensor(xc, xc, t[:], ALU.add))
                        ch.link(dve_new_stats(nc, dve, g, raw, c, ch))
                        assert ch.n == STEPS, ch.n
        s.clear()


STRIDE = NT * P + P


def expert_layer(nc, g, name, experts, top, gate_w, up_g, up_u, down):
    IB = 4
    SLOTS = top * NT + experts
    SPARE = experts * STRIDE
    STEPS = 15 if top == 2 else 11
    with ExitStack() as ctx:
        s = Scope(nc, ctx, name)
        std, rstd = s.sb("std", [P, NT]), s.sb("rstd", [P, NT])
        xn = s.sb("xn", [P, 2, CT, P])
        xt = s.sb("xt", [P, CHUNK])
        lg = s.sb("logits", [P, CT, 8])
        ex, wgap = s.sb("ex", [P, CT]), s.sb("wgap", [P, CT])
        top8, idx = s.sb("top8", [P, CT, 8]), s.sb("idx", [P, CT, 8], U32)
        idf = s.sb("idf", [P, CT, 8])
        hot = s.sb("hot", [P, 2, CT, 8])
        hot5 = s.sb("hot5", [P, CT + 1, 8])
        wsum, w2 = s.sb("wsum", [P, CT]), s.sb("w2", [P, 2, CT])
        earlier = s.sb("earlier", [P, P])
        base = s.sb("base", [P, 8])
        starts = s.sb("starts", [P, 8])
        pos, place = s.sb("pos", [P, CT, 8]), s.sb("place", [P, 2, CT, 8])
        destf = s.sb("destf", [P, 2, CT])
        dest = s.sb("dest", [P, 2, 2 * CT], U32)
        dest_all = s.sb("dest_all", [P, NC_, 2 * CT])
        hot_all = s.sb("hot_all", [P, NC_, 2 * CT * 8])
        shift, shifts, from_row = s.sb("shift", [P, 8]), s.sb("shifts", [P, 2 * CT, 8]), s.sb("from_row", [P, 2 * CT])
        w_all = s.sb("w_all", [P, NC_, 2 * CT])
        row_id, padf = s.sb("row_id", [P, 1]), s.sb("padf", [P, 8])
        pad = s.sb("pad", [P, 8], U32)
        zeros = s.sb("zeros", [P, P])
        t128, held, tiles = s.sb("t128", [P, NT]), s.sb("held", [P, 8, NT]), s.sb("tiles", [P, 8])
        until, jump = s.sb("until", [P, 8]), s.sb("jump", [1, 8])
        slot_id, past = s.sb("slot_id", [1, SLOTS]), s.sb("past", [1, SLOTS, 8])
        moved, slot_row, slot_e = s.sb("moved", [1, SLOTS, 8]), s.sb("slot_row", [1, SLOTS]), s.sb("slot_e", [1, SLOTS])
        table_row, table_e = s.sb("table_row", [1, SLOTS], I32), s.sb("table_e", [1, SLOTS], I32)
        xs = s.sb("xs", [P, 2, P])
        xst = s.sb("xst", [P, P])
        sg, hid = s.sb("sg", [P, 2, CHUNK]), s.sb("hid", [P, 2, CHUNK])
        hid_t = s.sb("hid_t", [P, 2, IB, P])
        ys = s.sb("ys", [P, 2, P])
        got = s.sb("got", [P, 2, top, CT, P])
        raw = s.sb("raw", [P, CT, 6])
        sorted_x = nc.dram_tensor(f"{name}_x", (experts * (STRIDE + P), P), F32).ap()
        sorted_y = nc.dram_tensor(f"{name}_y", (SLOTS, P, P), F32).ap()
        ps = s.ps("ps", [P, 8, 512])
        ps_t, ps_l, ps_r = ps[:, 4, :], ps[:, 6, 0:CT * 8].rearrange("p (k e) -> p k e", e=8), ps[:, 7, 0:(CT + 1) * 8].rearrange("p (k e) -> p k e", e=8)
        names = ("std_ready", "rs_ready", "made", "xn_ready", "xn_turned", "xt_ready", "lg_cleared", "lg_ready", "lg_copied", "gap_ready", "ex_ready",
                 "hot_ready", "rank_ready", "dest_ready", "scattered0", "scattered1", "pad_ready", "spare_ready", "padded", "table_ready", "chain", "combine_chain",
                 "xs_loaded0", "xs_loaded1", "x_turned", "xst_ready", "gu_ready", "silu_ready", "hid_ready", "h_turned", "ht_ready",
                 "y_ready", "y_copied", "y_stored0", "y_stored1", "idx_ready", "gathered0", "gathered1", "combined")
        S = {n: s.sem(n) for n in names}

        with nc.Block() as block:
            @block.sync
            def _(sp):
                sp.wait_ge(S["made"], 5)
                for e in range(experts):
                    sp.dma_start(sorted_x[SPARE + e * P:SPARE + e * P + P, :], zeros[:]).then_inc(S["spare_ready"], 16)
                sp.wait_ge(S["table_ready"], 1)
                sp.wait_ge(S["spare_ready"], 16 * experts)
                sp.wait_ge(S["padded"], 16 * experts)
                for par in range(2):
                    sp.wait_ge(S[f"scattered{par}"], NC_ // 2 * top * CT * 16)

                def load(n, par, half):
                    row = sp.value_load(table_row[0:1, bass.ds(n, 1)], min_val=0, max_val=SPARE + (experts - 1) * P)
                    sp.dma_start(xs[:, par, :], sorted_x[bass.ds(row, P), :]).then_inc(S[f"xs_loaded{par}"], 16)

                load(0, 0, 0)
                load(1, 1, 0)
                with sp.Fori(0, SLOTS // 2 - 1) as i:
                    for par in range(2):
                        hold(sp, S["x_turned"], i * 2 + (par + 1))
                        load(i * 2 + (par + 2), par, None)

            @block.gpsimd
            def _(pool):
                nc.gpsimd.memset(earlier[:], 1.0).then_inc(S["made"], 1)
                nc.gpsimd.memset(zeros[:], 0.0).then_inc(S["made"], 1)
                nc.gpsimd.memset(hot5[:], 0.0).then_inc(S["made"], 1)
                nc.gpsimd.iota(row_id[:], pattern=[[0, 1]], base=0, channel_multiplier=1, allow_small_or_imprecise_dtypes=True).then_inc(S["made"], 1)
                pool.wait_ge(S["made"], 4)
                nc.gpsimd.affine_select(out=earlier[:], in_=earlier[:], compare_op=ALU.is_gt, fill=0.0,
                                        base=0, pattern=[[1, P]], channel_multiplier=-1).then_inc(S["made"], 1)
                nc.gpsimd.iota(t128[:], pattern=[[P, NT]], base=0, channel_multiplier=0, allow_small_or_imprecise_dtypes=True).then_inc(S["made"], 1)
                nc.gpsimd.iota(slot_id[:], pattern=[[1, SLOTS]], base=0, channel_multiplier=0, allow_small_or_imprecise_dtypes=True).then_inc(S["made"], 1)
                nc.gpsimd.iota(starts[:], pattern=[[STRIDE, 8]], base=0, channel_multiplier=0, allow_small_or_imprecise_dtypes=True).then_inc(S["made"], 1)
                with pool.Fori(0, NC_ // 2) as i:
                    for par in range(2):
                        hold(pool, S["dest_ready"], i * 2 + (par + 1))
                        for n in range(top * CT):
                            nc.gpsimd.indirect_dma_start(out=sorted_x[:, :], out_offset=bass.IndirectOffsetOnAxis(ap=dest[:, par, n:n + 1], axis=0),
                                                         in_=xn[:, par, n % CT, :], in_offset=None).then_inc(S[f"scattered{par}"], 16)
                pool.wait_ge(S["pad_ready"], 1)
                for e in range(experts):
                    nc.gpsimd.indirect_dma_start(out=sorted_x[:, :], out_offset=bass.IndirectOffsetOnAxis(ap=pad[:, e:e + 1], axis=0),
                                                 in_=zeros[:], in_offset=None).then_inc(S["padded"], 16)
                pool.wait_ge(S["table_ready"], 1)

                with pool.Fori(0, SLOTS // 2) as i:
                    for par in range(2):
                        hold(pool, S["y_copied"], i * 2 + (par + 1))
                        nc.gpsimd.dma_start(sorted_y[bass.ds(i * 2 + par, 1), :, :].rearrange("a p d -> (a p) d"), ys[:, par, :]).then_inc(S[f"y_stored{par}"], 16)
                for par in range(2):
                    pool.wait_ge(S[f"y_stored{par}"], SLOTS // 2 * 16)
                with pool.Fori(0, NC_ // 2) as i:
                    for par in range(2):
                        hold(pool, S["idx_ready"], i * 2 + (par + 1))
                        for n in range(top * CT):
                            nc.gpsimd.indirect_dma_start(out=got[:, par, n // CT, n % CT, :], out_offset=None, in_=sorted_y.rearrange("a p d -> (a p) d"),
                                                         in_offset=bass.IndirectOffsetOnAxis(ap=dest[:, par, n:n + 1], axis=0)).then_inc(S[f"gathered{par}"], 16)

            @block.scalar
            def _(act):
                nc.scalar.activation(std[:], g.MV[:, :, 1], ACT.Sqrt, bias=g.eps[:, 0:1]).then_inc(S["std_ready"], 1)
                with act.Fori(0, NC_) as c:
                    act.wait_ge(S["xn_turned"], c + 1)
                    nc.scalar.activation(xt[:], ps_t, ACT.Copy).then_inc(S["xt_ready"], 1)
                    if top == 2:
                        act.wait_ge(S["gap_ready"], c + 1)
                        nc.scalar.activation(ex[:], wgap[:], ACT.Exp).then_inc(S["ex_ready"], 1)

                def turned_rows(n):
                    act.wait_ge(S["x_turned"], n + 1)
                    nc.scalar.activation(xst[:], ps[:, 6, 0:P], ACT.Copy).then_inc(S["xst_ready"], 1)

                def silu(n, par):
                    act.wait_ge(S["gu_ready"], n + 1)
                    if some(n - 1):
                        act.wait_ge(S["hid_ready"], n - 1)
                    nc.scalar.activation(sg[:, par, :], ps[:, par, :], ACT.Silu).then_inc(S["silu_ready"], 1)

                def turned_hidden(n, par):
                    act.wait_ge(S["h_turned"], n + 1)
                    nc.scalar.activation(hid_t[:, par].rearrange("p j t -> p (j t)"), ps[:, 4 + par, :], ACT.Copy).then_inc(S["ht_ready"], 1)

                turned_rows(0)
                silu(0, 0)
                turned_rows(1)
                with act.Fori(0, SLOTS // 2 - 1) as i:
                    for j in range(2):
                        n = i * 2 + (j + 1)
                        silu(n, 1 - j)
                        turned_rows(n + 1)
                        turned_hidden(n - 1, j)
                silu(SLOTS - 1, 1)
                turned_hidden(SLOTS - 2, 0)
                turned_hidden(SLOTS - 1, 1)

            @block.tensor
            def _(pe):
                pe.wait_ge(S["made"], 8)
                with pe.Fori(0, NC_ // 2) as i:
                    for par in range(2):
                        c = i * 2 + par
                        pe.wait_ge(S["xn_ready"], c + 1)
                        for k in range(CT):
                            last = nc.tensor.transpose(ps_t[:, k * P:k * P + P], xn[:, par, k, :], g.ident[:])
                        last.then_inc(S["xn_turned"], 1)
                        pe.wait_ge(S["xt_ready"], c + 1)
                        for k in range(CT):
                            last = nc.tensor.matmul(ps_l[:, k, 0:experts], xt[:, k * P:k * P + P], gate_w[:], start=True, stop=True)
                        last.then_inc(S["lg_ready"], 1)
                        pe.wait_ge(S["hot_ready"], c + 1)
                        h5 = hot5[:].rearrange("p k e -> p (k e)")
                        nc.tensor.matmul(ps_r.rearrange("p k e -> p (k e)"), earlier[:], h5, start=True, stop=False, skip_group_check=True)
                        for k in range(CT):
                            last = nc.tensor.matmul(ps_r[:, k + 1:CT + 1, :], g.ones[:], bc(hot5[:, k, :], CT - k), start=False, stop=(k == CT - 1), skip_group_check=True)
                        last.then_inc(S["rank_ready"], 1)

                def turn_rows(n, par, loads):
                    pe.wait_ge(S[f"xs_loaded{par}"], loads)
                    if some(n):
                        pe.wait_ge(S["xst_ready"], n)
                    nc.tensor.transpose(ps[:, 6, 0:P], xs[:, par, :], g.ident[:]).then_inc(S["x_turned"], 1)

                def up(n, par):
                    e = pe.value_load(table_e[0:1, bass.ds(n, 1)], min_val=0, max_val=experts - 1)
                    pe.wait_ge(S["xst_ready"], n + 1)
                    if some(n - 1):
                        pe.wait_ge(S["hid_ready"], n - 1)
                    nc.tensor.matmul(ps[:, par, :], xst[:], up_g(e), start=True, stop=True)
                    nc.tensor.matmul(ps[:, 2 + par, :], xst[:], up_u(e), start=True, stop=True).then_inc(S["gu_ready"], 1)

                def turn_hidden(n, par):
                    pe.wait_ge(S["hid_ready"], n + 1)
                    for j in range(IB):
                        last = nc.tensor.transpose(ps[:, 4 + par, j * P:j * P + P], hid[:, par, j * P:j * P + P], g.ident[:])
                    last.then_inc(S["h_turned"], 1)

                def rows(n, par):
                    e = pe.value_load(table_e[0:1, bass.ds(n, 1)], min_val=0, max_val=experts - 1)
                    pe.wait_ge(S["ht_ready"], n + 1)
                    if some(n):
                        pe.wait_ge(S["y_copied"], n)
                    for j in range(IB):
                        last = nc.tensor.matmul(ps[:, 7, 0:P], hid_t[:, par, j, :], down(e, j), start=(j == 0), stop=(j == IB - 1))
                    last.then_inc(S["y_ready"], 1)

                pe.wait_ge(S["table_ready"], 1)
                turn_rows(0, 0, 16)
                up(0, 0)
                turn_rows(1, 1, 16)
                up(1, 1)
                turn_rows(2, 0, 32)
                turn_hidden(0, 0)
                with pe.Fori(0, SLOTS // 2 - 2) as i:
                    for par in range(2):
                        n = i * 2 + (par + 2)
                        up(n, par)
                        turn_rows(n + 1, 1 - par, (i + (2 + par)) * 16)
                        turn_hidden(n - 1, 1 - par)
                        rows(n - 2, par)
                n = SLOTS - 2
                up(n, 0)
                turn_rows(n + 1, 1, SLOTS // 2 * 16)
                turn_hidden(n - 1, 1)
                rows(n - 2, 0)
                up(n + 1, 1)
                turn_hidden(n, 0)
                rows(n - 1, 1)
                turn_hidden(n + 1, 1)
                rows(n, 0)
                rows(n + 1, 1)

            @block.vector
            def _(dve):
                def weights(c, ch):
                    dve.wait_ge(S["lg_ready"], c + 1)
                    nc.vector.tensor_copy(lg[:, :, 0:experts], ps_l[:, :, 0:experts]).then_inc(S["lg_copied"], 1)
                    hold(dve, S["lg_copied"], c + 1)
                    for k in range(CT):
                        last = nc.vector.max(top8[:, k, :], lg[:, k, :])
                    ch.link(last)
                    for k in range(CT):
                        last = nc.vector.max_index(idx[:, k, :], top8[:, k, :], lg[:, k, :])
                    ch.link(last)
                    ch.link(nc.vector.tensor_copy(idf[:, :, 0:2], idx[:, :, 0:2]))
                    for r in range(top):
                        last = nc.vector.tensor_tensor(hot[:, r], bc(g.iota8[:], CT), bl(idf[:, :, r], 8), ALU.is_equal)
                    ch.link(last)
                    if top == 1:
                        nc.vector.tensor_copy(hot5[:, 0:CT, :], hot[:, 0]).then_inc(S["hot_ready"], 1)
                        return
                    nc.vector.tensor_tensor(hot5[:, 0:CT, :], hot[:, 0], hot[:, 1], ALU.add).then_inc(S["hot_ready"], 1)
                    nc.vector.tensor_tensor(wgap[:], top8[:, :, 1], top8[:, :, 0], ALU.subtract).then_inc(S["gap_ready"], 1)
                    dve.wait_ge(S["ex_ready"], c + 1)
                    ch.link(nc.vector.tensor_scalar_add(wsum[:], ex[:], 1.0))
                    ch.link(nc.vector.reciprocal(w2[:, 0, :], wsum[:]))
                    ch.link(nc.vector.tensor_tensor(w2[:, 1, :], w2[:, 0, :], ex[:], ALU.mult))
                    ch.link(nc.vector.tensor_copy(w_all[:, bass.ds(c, 1), :].rearrange("p a n -> p (a n)"), w2[:].rearrange("p r k -> p (r k)")))

                def places(c, par, ch):
                    dve.wait_ge(S["rank_ready"], c + 1)
                    ch.link(nc.vector.tensor_tensor(pos[:], ps_r[:, 0:CT, :], bc(base[:], CT), ALU.add))
                    ch.link(nc.vector.tensor_tensor(base[:], ps_r[:, CT, :], base[:], ALU.add))
                    for r in range(top):
                        last = nc.vector.tensor_tensor(place[:, r], hot[:, r], pos[:], ALU.mult)
                    ch.link(last)
                    ch.link(nc.vector.tensor_reduce(destf[:, 0:top], place[:, 0:top], AX_X, ALU.add))
                    ch.link(nc.vector.tensor_copy(hot_all[:, bass.ds(c, 1), 0:top * CT * 8].rearrange("p a n -> p (a n)"), hot[:, 0:top].rearrange("p r k e -> p (r k e)")))
                    ch.link(nc.vector.tensor_copy(dest_all[:, bass.ds(c, 1), 0:top * CT].rearrange("p a n -> p (a n)"), destf[:, 0:top].rearrange("p r k -> p (r k)")))
                    nc.vector.tensor_copy(dest[:, par, 0:top * CT], destf[:, 0:top].rearrange("p r k -> p (r k)")).then_inc(S["dest_ready"], 1)

                dve.wait_ge(S["std_ready"], 1)
                nc.vector.reciprocal(rstd[:], std[:]).then_inc(S["rs_ready"], 1)
                nc.vector.memset(lg[:], -3.0e38).then_inc(S["lg_cleared"], 1)
                dve.wait_ge(S["made"], 8)
                nc.vector.tensor_copy(base[:], starts[:]).then_inc(S["rs_ready"], 1)
                dve.wait_ge(S["lg_cleared"], 1)
                dve.wait_ge(S["rs_ready"], 2)

                def chunk(c, par, first=None, i=None):
                    ch = Chain(dve, S["chain"], c * STEPS)
                    if not first:
                        hold(dve, S[f"scattered{par}"], i * (top * CT * 16))
                    for k in range(CT):
                        n = c * CT + k
                        last = nc.vector.tensor_scalar(xn[:, par, k, :], tile_of(g.X, n), tile_of(g.MV, n)[:, 0:1], rstd[:, bass.ds(n, 1)], ALU.subtract, ALU.mult)
                    last.then_inc(S["xn_ready"], 1)
                    weights(c, ch)
                    places(c, par, ch)
                    while ch.n < STEPS:
                        ch.link(nc.vector.tensor_copy(padf[:, 0:1], row_id[:]))
                    assert ch.n == STEPS, ch.n

                for par in range(2):
                    chunk(par, par, first=True)
                with dve.Fori(1, NC_ // 2) as i:
                    for par in range(2):
                        chunk(i * 2 + par, par, i=i)

                ch = Chain(dve, S["chain"], NC_ * STEPS)
                ch.link(nc.vector.tensor_scalar(padf[:], base[:], row_id[:, 0:1], None, ALU.add))
                nc.vector.tensor_copy(pad[:], padf[:]).then_inc(S["pad_ready"], 1)
                ch.link(nc.vector.tensor_tensor(tiles[:], base[:], starts[:], ALU.subtract))
                ch.link(nc.vector.tensor_tensor(held[:], bl(tiles[:], NT), bc(t128[:], 8), ALU.is_gt))
                ch.link(nc.vector.tensor_reduce(tiles[:], held[:], AX_X, ALU.add))
                ch.link(nc.vector.tensor_copy(until[:], tiles[:]))
                for e in range(1, 8):
                    ch.link(nc.vector.tensor_tensor(until[:, e:e + 1], until[:, e - 1:e], until[:, e:e + 1], ALU.add))
                ch.link(nc.vector.tensor_tensor(shift[:], until[:], tiles[:], ALU.subtract))
                ch.link(nc.vector.scalar_tensor_tensor(shift[:], shift[:], float(P), starts[:], ALU.mult, ALU.subtract))
                ch.link(nc.vector.tensor_scalar(jump[:], tiles[0:1, :], -float(P), float(STRIDE), ALU.mult, ALU.add))
                ch.link(nc.vector.tensor_tensor(past[:], bl(slot_id[:], 8), bc(until[0:1, :], SLOTS), ALU.is_ge))
                ch.link(nc.vector.tensor_tensor(moved[:], past[:], bc(jump[:], SLOTS), ALU.mult))
                ch.link(nc.vector.tensor_reduce(slot_row[:], moved[:, :, 0:experts], AX_X, ALU.add))
                ch.link(nc.vector.scalar_tensor_tensor(slot_row[:], slot_id[:], float(P), slot_row[:], ALU.mult, ALU.add))
                ch.link(nc.vector.tensor_reduce(slot_e[:], past[:, :, 0:experts], AX_X, ALU.add))
                ch.link(nc.vector.tensor_copy(table_row[:], slot_row[:]))
                nc.vector.tensor_scalar(table_e[:], slot_e[:], float(experts - 1), None, ALU.min).then_inc(S["table_ready"], 1)

                def hidden(n, par):
                    dve.wait_ge(S["silu_ready"], n + 1)
                    if some(n - 1):
                        dve.wait_ge(S["h_turned"], n - 1)
                    nc.vector.tensor_tensor(hid[:, par, :], sg[:, par, :], ps[:, 2 + par, :], ALU.mult).then_inc(S["hid_ready"], 1)

                def rows(n, par, stores):
                    dve.wait_ge(S["y_ready"], n + 1)
                    if some(stores):
                        hold(dve, S[f"y_stored{par}"], stores)
                    nc.vector.tensor_copy(ys[:, par, :], ps[:, 7, 0:P]).then_inc(S["y_copied"], 1)

                hidden(0, 0)
                hidden(1, 1)
                hidden(2, 0)
                rows(0, 0, 0)
                hidden(3, 1)
                rows(1, 1, 0)
                with dve.Fori(1, SLOTS // 2 - 1) as i:
                    for par in range(2):
                        n = i * 2 + par
                        hidden(n + 2, par)
                        rows(n, par, i * 16)
                rows(SLOTS - 2, 0, (SLOTS // 2 - 1) * 16)
                rows(SLOTS - 1, 1, (SLOTS // 2 - 1) * 16)

                def order(c, par, ch):
                    ch.link(nc.vector.tensor_tensor(shifts[:, 0:top * CT], hot_all[:, bass.ds(c, 1), 0:top * CT * 8].rearrange("p a (n e) -> p (a n) e", e=8), bc(shift[:], top * CT), ALU.mult))
                    ch.link(nc.vector.tensor_reduce(from_row[:, 0:top * CT], shifts[:, 0:top * CT], AX_X, ALU.add))
                    ch.link(nc.vector.tensor_tensor(from_row[:, 0:top * CT], from_row[:, 0:top * CT], dest_all[:, bass.ds(c, 1), 0:top * CT].rearrange("p a n -> p (a n)"), ALU.add))
                    nc.vector.tensor_copy(dest[:, par, 0:top * CT], from_row[:, 0:top * CT]).then_inc(S["idx_ready"], 1)

                CSTEPS = 6 + top
                order(0, 0, ch)
                dve.wait_ge(S["idx_ready"], 1)
                order(1, 1, ch)

                def combine(c, par, gathers, more, ch):
                    dve.wait_ge(S[f"gathered{par}"], gathers)
                    for r in range(top):
                        for k in range(CT):
                            x = tile_of(g.X, c * CT + k)
                            if top == 1:
                                last = nc.vector.tensor_tensor(x, got[:, par, r, k, :], x, ALU.add)
                            else:
                                w = w_all[:, bass.ds(c, 1), r * CT + k:r * CT + k + 1].rearrange("p a n -> p (a n)")
                                last = nc.vector.scalar_tensor_tensor(x, got[:, par, r, k, :], w, x, ALU.mult, ALU.add)
                        ch.link(last)
                    if more:
                        order(c + 2, par, ch)
                    ch.link(dve_new_stats(nc, dve, g, raw, c, ch))
                    assert not more or ch.n == CSTEPS, ch.n

                with dve.Fori(0, NC_ // 2 - 1) as i:
                    for par in range(2):
                        c = i * 2 + par
                        combine(c, par, (i + 1) * (top * CT * 16), True, Chain(dve, S["combine_chain"], c * CSTEPS))
                ch = Chain(dve, S["combine_chain"], (NC_ - 2) * CSTEPS)
                for par in range(2):
                    combine(NC_ - 2 + par, par, NC_ // 2 * top * CT * 16, False, ch)
        s.clear()


def landmark_layer(nc, g, wq, bq, wk, bk, wv, bv):
    TB = SEQ // P
    LM = 64
    RUN = SEQ // LM
    PER = P // RUN
    WIN = LM - PER
    with ExitStack() as ctx:
        s = Scope(nc, ctx, "lm")
        norm = Norm(nc, g, s)
        w = s.sb("w", [P, 3, P])
        brow = s.sb("brow", [1, 3, P])
        avg = s.sb("avg", [P, WIN + LM])
        xt = s.sb("xt", [P, 2, CHUNK])
        nmx, sums, rs = s.sb("nmx", [P, TB, 2]), s.sb("sums", [P, TB, 2]), s.sb("rs", [P, TB, 2])
        eq, ek = s.sb("eq", [P, 2, P]), s.sb("ek", [P, 2, P])
        kk, k3 = s.sb("kk", [P, 2, P]), s.sb("k3", [P, 2, P])
        eqt = s.sb("eqt", [P, TB, P])
        lm, mm, aa, nn = s.sb("lm", [LM, P]), s.sb("mm", [P, P]), s.sb("aa", [P, P]), s.sb("nn", [P, P])
        raw = s.sb("raw", [P, CT, 6])
        ps_t, ps_qkv, ps_o = s.ps("ps_t", [P, CT, P]), s.ps("ps_qkv", [P, 4, 512]), s.ps("ps_o", [P, CT, P])
        ps_m, ps_lm = s.ps("ps_m", [P, 512]), s.ps("ps_lm", [P, 512])
        loaded, made, chain = s.sem("loaded"), s.sem("made"), s.sem("chain")
        xn_ready, turned, copied = s.sem("xn_ready"), s.sem("turned"), s.sem("copied")
        qkv_ready, mx_ready, exp_ready = s.sem("qkv_ready"), s.sem("mx_ready"), s.sem("exp_ready")
        k3_ready, acc_done = s.sem("k3_ready"), s.sem("acc_done")
        mm_ready, a_done, a_ready, n_done, n_ready = (s.sem(n) for n in ("mm_ready", "a_done", "a_ready", "n_done", "n_ready"))
        o_ready, o_used = s.sem("o_ready"), s.sem("o_used")
        STEPS = TB + 6

        with nc.Block() as block:
            @block.sync
            def _(sp):
                for i, (m, b) in enumerate(((wq, bq), (wk, bk), (wv, bv))):
                    sp.dma_start(w[:, i, :], m).then_inc(loaded, 16)
                    sp.dma_start(brow[:, i, :], b.rearrange("(a n) -> a n", a=1)).then_inc(loaded, 16)

            @block.gpsimd
            def _(pool):
                nc.gpsimd.memset(avg[:], 1.0 / RUN).then_inc(made, 1)
                pool.wait_ge(made, 1)
                nc.gpsimd.affine_select(out=avg[:], in_=avg[:], compare_op=ALU.is_ge, fill=0.0, base=RUN * WIN,
                                        pattern=[[-RUN, WIN + LM]], channel_multiplier=1).then_inc(made, 1)
                pool.wait_ge(made, 2)
                nc.gpsimd.affine_select(out=avg[:], in_=avg[:], compare_op=ALU.is_ge, fill=0.0, base=RUN - 1 - RUN * WIN,
                                        pattern=[[RUN, WIN + LM]], channel_multiplier=-1).then_inc(made, 1)

            @block.scalar
            def _(act):
                norm.act_std(act)
                with act.Fori(0, BATCH) as b:
                    for h in range(2):
                        act.wait_ge(turned, b * 2 + h + 1)
                        nc.scalar.activation(xt[:, h, :], ps_t[:].rearrange("p a b -> p (a b)"), ACT.Copy).then_inc(copied, 1)
                    for t in range(TB + 1):
                        n = b * TB + t
                        if t < TB:
                            act.wait_ge(mx_ready, n + 1)
                            act.wait_ge(k3_ready, n + 3)
                            act.wait_ge(acc_done, n + 1)
                            nc.scalar.activation(ek[:, t % 2, :], ps_qkv[:, t % 4, P:2 * P], ACT.Exp, bias=nmx[:, t, 1:2], accum_out=sums[:, t, 1:2])
                            nc.scalar.activation(eq[:, t % 2, :], ps_qkv[:, t % 4, 0:P], ACT.Exp, bias=nmx[:, t, 0:1], accum_out=sums[:, t, 0:1]).then_inc(exp_ready, 1)
                        if t in (4, 8):
                            act.wait_ge(acc_done, n + 2)
                            nc.scalar.activation(eqt[:, t - 4:t, :], ps_t[:], ACT.Copy).then_inc(copied, 1)

            @block.tensor
            def _(pe):
                pe.wait_ge(loaded, 16 * 6)
                pe.wait_ge(made, 3)
                pe.sem_inc(acc_done, 2)
                with pe.Fori(0, BATCH) as b:
                    for h in range(2):
                        pe.wait_ge(xn_ready, b * 2 + h + 1)
                        pe.wait_ge(copied, b * 4 + h + 1)
                        for k in range(CT):
                            last = nc.tensor.transpose(ps_t[:, k, :], norm.xn[:, k, :], g.ident[:])
                        last.then_inc(turned, 1)
                    for t in range(TB + 1):
                        n = b * TB + t
                        if t < TB:
                            if t % CT == 0:
                                pe.wait_ge(copied, b * 4 + 2 + t // CT)
                            pe.wait_ge(k3_ready, n + 1)
                            if t >= 4:
                                pe.wait_ge(exp_ready, n - 3)
                            out = ps_qkv[:, t % 4, 0:3 * P]
                            nc.tensor.matmul(out, g.ones[0:1, :], brow[:].rearrange("p a b -> p (a b)"), start=True, stop=False)
                            nc.tensor.matmul(out, xt[:, t // CT, t % CT * P:t % CT * P + P], w[:].rearrange("p a b -> p (a b)"),
                                             start=False, stop=True).then_inc(qkv_ready, 1)
                        if t >= 1:
                            r = t - 1
                            pe.wait_ge(k3_ready, n + 4)
                            nc.tensor.matmul(ps_m[:, 0:P], kk[:, r % 2, :], k3[:, r % 2, :], start=(r == 0), stop=(r == TB - 1))
                            nc.tensor.matmul(ps_lm[0:LM, 0:P], avg[:, WIN - PER * r:WIN - PER * r + LM], kk[:, r % 2, :],
                                             start=(r == 0), stop=(r == TB - 1))
                            pe.wait_ge(exp_ready, n)
                            if r % 4 == 0:
                                pe.wait_ge(copied, b * 4 + 3 + r // 4)
                            nc.tensor.transpose(ps_t[:, r % 4, :], eq[:, r % 2, :], g.ident[:]).then_inc(acc_done, 1)
                    pe.wait_ge(mm_ready, b + 1)
                    nc.tensor.matmul(ps_o[:, 0, :], lm[:], lm[:], start=True, stop=True).then_inc(a_done, 1)
                    pe.wait_ge(a_ready, b + 1)
                    nc.tensor.matmul(ps_o[:, 1, :], aa[:], mm[:], start=True, stop=True).then_inc(n_done, 1)
                    pe.wait_ge(n_ready, b + 1)
                    pe.wait_ge(copied, b * 4 + 5)
                    for h in range(2):
                        if h:
                            pe.wait_ge(o_used, b * 2 + 1)
                        for k in range(CT):
                            last = nc.tensor.matmul(ps_o[:, k, :], eqt[:, h * CT + k, :], nn[:], start=True, stop=True)
                        last.then_inc(o_ready, 1)

            @block.vector
            def _(dve):
                norm.dve_rstd(dve)
                dve.sem_inc(k3_ready, 4)
                dve.sem_inc(copied, 1)
                with dve.Fori(0, BATCH) as b:
                    ch = Chain(dve, chain, b * STEPS)
                    for h in range(2):
                        if h:
                            dve.wait_ge(turned, b * 2 + 1)
                        norm.dve_rows(b * 2 + h).then_inc(xn_ready, 1)
                    for t in range(TB + 1):
                        n = b * TB + t
                        if t < TB:
                            dve.wait_ge(qkv_ready, n + 1)
                            nc.vector.tensor_reduce(nmx[:, t, :], ps_qkv[:, t % 4, 0:2 * P].rearrange("p (a b) -> p a b", a=2),
                                                    AX_X, ALU.max, negate=True).then_inc(mx_ready, 1)
                        if t >= 1:
                            r = t - 1
                            dve.wait_ge(exp_ready, n)
                            ch.link(nc.vector.reciprocal(rs[:, r, :], sums[:, r, :]))
                            dve.wait_ge(acc_done, n)
                            nc.vector.tensor_scalar(kk[:, r % 2, :], ek[:, r % 2, :], rs[:, r, 1:2], None, ALU.mult)
                            nc.vector.scalar_tensor_tensor(k3[:, r % 2, :], ek[:, r % 2, :], rs[:, r, 1:2], ps_qkv[:, r % 4, 2 * P:3 * P],
                                                           ALU.mult, ALU.mult).then_inc(k3_ready, 1)
                    dve.wait_ge(acc_done, b * TB + TB + 2)
                    nc.vector.tensor_copy(lm[:], ps_lm[0:LM, 0:P])
                    nc.vector.tensor_copy(mm[:], ps_m[:, 0:P]).then_inc(mm_ready, 1)
                    dve.wait_ge(a_done, b + 1)
                    nc.vector.tensor_copy(aa[:], ps_o[:, 0, :]).then_inc(a_ready, 1)
                    dve.wait_ge(n_done, b + 1)
                    nc.vector.tensor_copy(nn[:], ps_o[:, 1, :]).then_inc(n_ready, 1)
                    for h in range(2):
                        c = b * 2 + h
                        dve.wait_ge(o_ready, c + 1)
                        for k in range(CT):
                            t = h * CT + k
                            xk = tile_of(g.X, b * TB + t)
                            last = nc.vector.scalar_tensor_tensor(xk, ps_o[:, k, :], rs[:, t, 0:1], xk, ALU.mult, ALU.add)
                        last.then_inc(o_used, 1)
                        hold(dve, o_used, c + 1)
                        ch.link(dve_new_stats(nc, dve, g, raw, c, ch))
                    assert ch.n == STEPS, ch.n
        s.clear()


def causal_layer(nc, g, wq, bq, wk, bk, wv, bv, wp, bp, table, wq_sw, bq_sw, wk_sw, bk_sw, rope, onehot):
    H, D = 16, 8
    TB = SEQ // P
    NP = 3
    KD = NP * NP * D
    KM = KD + NP
    G4 = 4
    NG = H // G4
    SCALE = 1.0 / D ** 0.5
    NEG = -1.0e30
    W2 = 2 * P
    blocks = [(q4, kt) for q4 in range(2) for kt in range(4 * q4 + 4)]
    NS = NG * len(blocks) * G4
    BF = mybir.dt.bfloat16

    def span(q4, kt):
        lo, hi = max(kt * P, q4 * CHUNK), q4 * CHUNK + CHUNK
        return lo, min(max(kt * P + W2, lo), hi), hi

    near_of, last_of = {}, []
    i = 0
    for _ in range(NG):
        for q4, kt in blocks:
            for _ in range(G4):
                if span(q4, kt)[0] < span(q4, kt)[1]:
                    near_of[i] = len(near_of)
                i += 1
            if kt == 4 * q4 + 3:
                last_of.append(i - 1)
    NN = len(near_of)
    STEPS = 3 + 2 * NG + 2 * 4

    with ExitStack() as ctx:
        s = Scope(nc, ctx, "ca")
        norm = Norm(nc, g, s)
        w = s.sb("w", [P, 6, P])
        bcol = s.sb("bcol", [P, 4])
        brow = s.sb("brow", [1, 2, CT, P])
        cs = s.sb("cs", [P, 2, SEQ])
        bias_q = s.sb("bias_q", [P, H, W2])
        bias_k = s.sb("bias_k", [P, H, W2])
        xt = s.sb("xt", [P, 2, CHUNK])
        t1, t2 = s.sb("t1", [P, 2, CHUNK]), s.sb("t2", [P, 2, CHUNK])
        full = s.sb("full", [P, 2, SEQ])
        piece = s.sb("piece", [P, NP, SEQ], BF)
        qst, kst = s.sb("qst", [KM, H, SEQ], BF), s.sb("kst", [KM, H, SEQ], BF)
        vp = s.sb("vp", [P, TB, H, D + 1])
        m_near, m_far, m_all = s.sb("m_near", [P, H * TB]), s.sb("m_far", [P, H * TB]), s.sb("m_all", [P, H * TB])
        m_rest, m_piece = s.sb("m_rest", [P, P]), s.sb("m_piece", [P, NP, P], BF)
        near = s.sb("near", [P, 4, W2])
        pt = s.sb("pt", [P, 8, CHUNK])
        ysb, yrs = s.sb("ysb", [P, CHUNK]), s.sb("yrs", [P, CT, G4])
        yy = s.sb("yy", [P, TB, P])
        zero_row = s.sb("zero_row", [1, CHUNK])
        raw = s.sb("raw", [P, CT, 6])
        ps = s.ps("ps", [P, 8, 512])
        dram_bias = nc.dram_tensor("scratch_bias", (2, H, 384), F32).ap()
        dram_toeplitz = nc.dram_tensor("scratch_toeplitz", (2, H, P, W2), F32).ap()
        dram_piece = nc.dram_tensor("scratch_piece", (2, NP, P, SEQ), BF).ap()
        dram_max = nc.dram_tensor("scratch_max", (NP, H * TB, P), BF).ap()

        loaded, bias_made, bias_stored, bias_loaded = (s.sem(n) for n in ("loaded", "bias_made", "bias_stored", "bias_loaded"))
        filled, buckets_ready, bias_ready = s.sem("filled"), s.sem("buckets_ready"), s.sem("bias_ready")
        chain = s.sem("chain")
        xn_ready, turned, xt_ready = s.sem("xn_ready"), s.sem("turned"), s.sem("xt_ready")
        proj_ready, proj_used, v_ready, v_used = (s.sem(n) for n in ("proj_ready", "proj_used", "v_ready", "v_used"))
        full_ready, piece1, rest1, piece2, piece3 = (s.sem(n) for n in ("full_ready", "piece1", "rest1", "piece2", "piece3"))
        pieces_stored, stacks_loaded = s.sem("pieces_stored"), s.sem("stacks_loaded")
        sq_ready, sq_used = s.sem("sq_ready"), s.sem("sq_used")
        m_ready, mt_ready, mp_ready, mp_stored, mp_loaded = (s.sem(n) for n in ("m_ready", "mt_ready", "mp_ready", "mp_stored", "mp_loaded"))
        st_ready, near_ready, p_ready, pv_done = (s.sem(n) for n in ("st_ready", "near_ready", "p_ready", "pv_done"))
        y_copied, yt_ready, yy_ready = (s.sem(n) for n in ("y_copied", "yt_ready", "yy_ready"))
        t_ready, t_copied, o_ready = (s.sem(n) for n in ("t_ready", "t_copied", "o_ready"))
        YB = NG * 2

        with nc.Block() as block:
            @block.sync
            def _(sp):
                for i, m in enumerate((wq, wq_sw, wk, wk_sw, wv, wp)):
                    sp.dma_start(w[:, i, :], m).then_inc(loaded, 16)
                for i, m in enumerate((bq, bq_sw, bk, bk_sw)):
                    sp.dma_start(bcol[:, i:i + 1], m.rearrange("(p a) -> p a", a=1)).then_inc(loaded, 16)
                for i, m in enumerate((bv, bp)):
                    for k in range(CT):
                        sp.dma_start(brow[:, i, k, :], m.rearrange("(a n) -> a n", a=1)).then_inc(loaded, 16)
                sp.dma_start(cs[:], rope).then_inc(loaded, 16)
                sp.dma_start(m_near[0:32, 0:H], table).then_inc(loaded, 16)
                sp.dma_start(near[0:33, 0:3, :].rearrange("p a b -> p (a b)"), onehot).then_inc(loaded, 16)
                sp.wait_ge(bias_made, 2)
                sp.dma_start(dram_bias.rearrange("a h n -> h a n"), full[0:H, :, 0:384]).then_inc(bias_stored, 16)
                sp.wait_ge(bias_stored, 16)
                for side, offset in ((1, P - 1), (0, P)):
                    sp.dma_start(dram_toeplitz[side], bass.AP(dram_bias.tensor, side * H * 384 + offset, [[384, H], [-1, P], [1, W2]])).then_inc(bias_stored, 16)
                sp.wait_ge(bias_stored, 48)
                for bias, side in ((bias_q, 1), (bias_k, 0)):
                    sp.dma_start(bias[:], dram_toeplitz[side].rearrange("h p w -> p h w")).then_inc(bias_loaded, 16)
                with sp.Fori(0, BATCH) as b:
                    for side in range(2):
                        hold(sp, piece3, b * 2 + side + 1)
                        sp.dma_start(dram_piece[side].rearrange("n p t -> p n t"), piece[:]).then_inc(pieces_stored, 16)
                        hold(sp, pieces_stored, b * 32 + side * 16 + 16)
                        for a in range(NP):
                            for c in range(NP):
                                r = (a * NP + c) * D
                                dst = (qst, kst)[side]
                                src = dram_piece[side, (a, c)[side]].rearrange("(h d) t -> d h t", d=D)
                                sp.dma_start(dst[r:r + D], src).then_inc(stacks_loaded, 16)
                    hold(sp, stacks_loaded, b * 288 + 288)
                    hold(sp, mp_ready, b + 1)
                    sp.dma_start(dram_max.rearrange("n p t -> p n t"), m_piece[:]).then_inc(mp_stored, 16)
                    hold(sp, mp_stored, b * 16 + 16)
                    sp.dma_start(qst[KD:KM].rearrange("p h t -> p (h t)"), dram_max.rearrange("n p t -> n (p t)")).then_inc(mp_loaded, 16)
                    hold(sp, mp_loaded, b * 16 + 16)
                    hold(sp, o_ready, b * 2 + 2)

            @block.gpsimd
            def _(pool):
                nc.gpsimd.memset(vp[:, :, :, D:D + 1], 1.0).then_inc(filled, 1)
                pool.wait_ge(filled, 1)
                nc.gpsimd.memset(zero_row[:], 0.0).then_inc(filled, 1)
                pool.wait_ge(filled, 2)
                nc.gpsimd.memset(m_near[32:33, 0:H], 1.0).then_inc(filled, 1)
                pool.wait_ge(filled, 3)
                nc.gpsimd.memset(m_far[:], NEG).then_inc(filled, 1)
                pool.wait_ge(filled, 4)
                nc.gpsimd.memset(kst[64:KM], 1.0).then_inc(filled, 1)
                with pool.Fori(0, BATCH) as b:
                    for side in range(2):
                        pool.wait_ge(piece1, b * 2 + side + 1)
                        nc.gpsimd.tensor_tensor(full[:, side], full[:, side], piece[:, 0, :], ALU.subtract).then_inc(rest1, 1)
                        pool.wait_ge(piece2, b * 2 + side + 1)
                        nc.gpsimd.tensor_tensor(piece[:, 2, :], full[:, side], piece[:, 1, :], ALU.subtract).then_inc(piece3, 1)

            @block.scalar
            def _(act):
                norm.act_std(act)
                act.sem_inc(p_ready, 4)
                act.wait_ge(bias_ready, 1)
                with act.Fori(0, BATCH) as b:
                    for h in range(2):
                        act.wait_ge(turned, b * 2 + h + 1)
                        nc.scalar.activation(xt[:, h, :], ps[:, 4, :], ACT.Copy).then_inc(xt_ready, 1)
                    for side in range(2):
                        n = b * 2 + side
                        act.wait_ge(full_ready, b * 2 + 2)
                        if side:
                            act.wait_ge(pieces_stored, b * 32 + 16)
                        nc.scalar.activation(piece[:, 0, :], full[:, side], ACT.Copy).then_inc(piece1, 1)
                        act.wait_ge(rest1, n + 1)
                        nc.scalar.activation(piece[:, 1, :], full[:, side], ACT.Copy).then_inc(piece2, 1)

                    def copy_y(n):
                        act.wait_ge(pv_done, b * NS + last_of[n] + 9)
                        nc.scalar.activation(ysb[:], ps[:, 6, :], ACT.Copy).then_inc(y_copied, 1)

                    i = 0
                    for gr in range(NG):
                        for q4, kt in blocks:
                            lo, mid, hi = span(q4, kt)
                            c0 = q4 * CHUNK
                            for j in range(G4):
                                act.wait_ge(st_ready, b * NS + i + 1)
                                act.wait_ge(pv_done, b * NS + i + 1)
                                out, src = pt[:, i % 8, :], ps[:, i % 6, :]
                                if lo < mid:
                                    act.wait_ge(near_ready, b * NN + near_of[i] + 1)
                                nc.scalar.activation(out[:, lo - c0:hi - c0], src[:, lo - c0:hi - c0], ACT.Exp, scale=SCALE).then_inc(p_ready, 1)
                                i += 1
                            if kt == 0 and (gr, q4) != (0, 0):
                                copy_y(gr * 2 + q4 - 1)
                    copy_y(YB - 1)
                    for h in range(2):
                        act.wait_ge(t_ready, b * 2 + h + 1)
                        nc.scalar.activation(pt[:, h, :], ps[:, h, :], ACT.Copy).then_inc(t_copied, 1)

            @block.tensor
            def _(pe):
                pe.wait_ge(loaded, 16 * 21)
                pe.wait_ge(filled, 5)
                for a in range(2):
                    nc.tensor.matmul(ps[0:H, a, 0:384], m_near[0:33, 0:H],
                                     near[0:33, 0:3, :].rearrange("p a b -> p (a b)")[:, a * 384:a * 384 + 384],
                                     start=True, stop=True).then_inc(buckets_ready, 1)
                nc.tensor.matmul(ps[:, 6, :], g.ones[0:1, :], zero_row[:], start=True, stop=True)
                pe.sem_inc(pv_done, 8)
                pe.wait_ge(bias_ready, 1)
                with pe.Fori(0, BATCH) as b:
                    for h in range(2):
                        pe.wait_ge(xn_ready, b * 2 + h + 1)
                        if h:
                            pe.wait_ge(xt_ready, b * 2 + 1)
                        for k in range(CT):
                            last = nc.tensor.transpose(ps[:, 4, k * P:k * P + P], norm.xn[:, k, :], g.ident[:])
                        last.then_inc(turned, 1)
                    for h in range(2):
                        n = b * 2 + h
                        pe.wait_ge(xt_ready, n + 1)
                        pe.wait_ge(proj_used, n + 1)
                        for i in range(4):
                            last = nc.tensor.matmul(ps[:, i, :], w[:, i, :], xt[:, h, :], start=True, stop=True)
                        last.then_inc(proj_ready, 1)
                        pe.wait_ge(v_used, n + 1)
                        nc.tensor.matmul(ps[:, 5, :], g.ones[0:1, :], brow[:, 0].rearrange("p a b -> p (a b)"), start=True, stop=False, skip_group_check=True)
                        for k in range(CT):
                            last = nc.tensor.matmul(ps[:, 5, k * P:k * P + P], xt[:, h, k * P:k * P + P], w[:, 4, :], start=False, stop=True, skip_group_check=True)
                        last.then_inc(v_ready, 1)

                    pe.wait_ge(proj_used, b * 2 + 3)
                    pe.wait_ge(v_used, b * 2 + 3)
                    pe.wait_ge(stacks_loaded, b * 288 + 288)
                    for h in range(H):
                        for qt in range(TB):
                            i = h * TB + qt
                            pe.wait_ge(sq_used, b * H * TB + i + 1)
                            r = 2 * (i % 3)
                            end = (qt + 1) * P
                            for c in range(0, end, 512):
                                e = min(c + 512, end)
                                last = nc.tensor.matmul(ps[:, r + c // 512, 0:e - c], qst[0:KD, h, qt * P:qt * P + P], kst[0:KD, h, c:e], start=True, stop=True)
                            last.then_inc(sq_ready, 1)
                    pe.wait_ge(m_ready, b + 1)
                    nc.tensor.transpose(ps[:, 7, 0:P], m_all[:], g.ident[:]).then_inc(mt_ready, 1)
                    pe.wait_ge(mp_loaded, b * 16 + 16)

                    def products(gr, q4, kt, i):
                        lo, _, hi = span(q4, kt)
                        c0 = q4 * CHUNK
                        if kt == 0:
                            pe.wait_ge(y_copied, b * YB + gr * 2 + q4 + 1)
                        for j in range(G4):
                            pe.wait_ge(p_ready, b * NS + i + j + 5)
                            nc.tensor.matmul(ps[32 * j:32 * j + D + 1, 6, lo - c0:hi - c0], vp[:, kt, gr * G4 + j, :], pt[:, (i + j) % 8, lo - c0:hi - c0],
                                             start=(kt == 0), stop=(kt == 4 * q4 + 3), skip_group_check=True).then_inc(pv_done, 1)

                    def turn_y(n):
                        pe.wait_ge(y_copied, b * YB + n + 2)
                        pe.wait_ge(yy_ready, b * YB + n + 1)
                        for k in range(CT):
                            last = nc.tensor.transpose(ps[:, 7, k * P:k * P + P], ysb[:, k * P:k * P + P], g.ident[:])
                        last.then_inc(yt_ready, 1)

                    i = 0
                    before = None
                    for gr in range(NG):
                        for q4, kt in blocks:
                            lo, _, hi = span(q4, kt)
                            c0 = q4 * CHUNK
                            for j in range(G4):
                                if i + j >= 6:
                                    pe.wait_ge(p_ready, b * NS + i + j - 1)
                                nc.tensor.matmul(ps[:, (i + j) % 6, lo - c0:hi - c0], kst[:, gr * G4 + j, kt * P:kt * P + P], qst[:, gr * G4 + j, lo:hi],
                                                 start=True, stop=True).then_inc(st_ready, 1)
                            if before:
                                products(*before)
                            if kt == 3 and (gr, q4) != (0, 0):
                                turn_y(gr * 2 + q4 - 1)
                            before = (gr, q4, kt, i)
                            i += G4
                    products(*before)
                    turn_y(YB - 1)
                    for h in range(2):
                        pe.wait_ge(yy_ready, b * YB + YB + 1)
                        pe.wait_ge(p_ready, b * NS + NS + 4)
                        for k in range(CT):
                            last = nc.tensor.transpose(ps[:, h, k * P:k * P + P], yy[:, h * CT + k, :], g.ident[:])
                        last.then_inc(t_ready, 1)
                    for h in range(2):
                        pe.wait_ge(t_copied, b * 2 + h + 1)
                        nc.tensor.matmul(ps[:, 2 + h, :], g.ones[0:1, :], brow[:, 1].rearrange("p a b -> p (a b)"), start=True, stop=False, skip_group_check=True)
                        for k in range(CT):
                            last = nc.tensor.matmul(ps[:, 2 + h, k * P:k * P + P], pt[:, h, k * P:k * P + P], w[:, 5, :], start=False, stop=True, skip_group_check=True)
                        last.then_inc(o_ready, 1)

            @block.vector
            def _(dve):
                norm.dve_rstd(dve)
                dve.wait_ge(buckets_ready, 2)
                dve.wait_ge(filled, 4)
                nc.vector.tensor_copy(full[0:H, 0, 0:384], ps[0:H, 0, 0:384]).then_inc(bias_made, 1)
                nc.vector.tensor_copy(full[0:H, 1, 0:384], ps[0:H, 1, 0:384]).then_inc(bias_made, 1)
                dve.sem_inc(proj_used, 1)
                dve.sem_inc(v_used, 1)
                dve.sem_inc(sq_used, 3)
                dve.sem_inc(y_copied, 1)
                dve.sem_inc(yy_ready, 1)
                dve.wait_ge(bias_loaded, 32)
                dve.sem_inc(bias_ready, 2)
                with dve.Fori(0, BATCH) as b:
                    ch = Chain(dve, chain, b * STEPS)
                    for h in range(2):
                        if h:
                            dve.wait_ge(turned, b * 2 + 1)
                        norm.dve_rows(b * 2 + h).then_inc(xn_ready, 1)
                    for h in range(2):
                        n = b * 2 + h
                        tt = slice(h * CHUNK, h * CHUNK + CHUNK)
                        dve.wait_ge(proj_ready, n + 1)
                        for side in range(2):
                            i = 2 * side
                            nc.vector.scalar_tensor_tensor(t1[:, side], ps[:, i, :], bcol[:, i:i + 1], cs[:, 0, tt], ALU.add, ALU.mult)
                            last = nc.vector.scalar_tensor_tensor(t2[:, side], ps[:, i + 1, :], bcol[:, i + 1:i + 2], cs[:, 1, tt], ALU.add, ALU.mult)
                        last.then_inc(proj_used, 1)
                        dve.wait_ge(proj_used, n + 2)
                        nc.vector.tensor_tensor(full[:, :, tt], t1[:], t2[:], ALU.add).then_inc(full_ready, 1)
                        dve.wait_ge(full_ready, n + 1)
                        dve.wait_ge(v_ready, n + 1)
                        nc.vector.tensor_copy(vp[:, h * CT:h * CT + CT, :, 0:D], ps[:, 5, :].rearrange("p (t h d) -> p t h d", t=CT, d=D)).then_inc(v_used, 1)

                    for h in range(H):
                        for qt in range(TB):
                            i = h * TB + qt
                            hold(dve, sq_ready, b * H * TB + i + 1)
                            r = 2 * (i % 3)
                            rows = ps[:, r:r + 2, :].rearrange("p a b -> p (a b)")
                            lo = max(qt - 1, 0) * P
                            hi = qt * P + P
                            if lo:
                                nc.vector.tensor_reduce(m_far[:, i:i + 1], rows[:, 0:lo], AX_X, ALU.max)
                            nc.vector.tensor_tensor_reduce(near[:, i % 4, 0:hi - lo], rows[:, lo:hi], bias_q[:, h, W2 - (hi - lo):W2], 1.0, NEG,
                                                           ALU.add, ALU.max, m_near[:, i:i + 1]).then_inc(sq_used, 1)
                    dve.wait_ge(sq_used, b * H * TB + H * TB + 3)
                    nc.vector.tensor_tensor(m_all[:], m_near[:], m_far[:], ALU.max).then_inc(m_ready, 1)
                    dve.wait_ge(mt_ready, b + 1)
                    ch.link(nc.vector.tensor_scalar(m_piece[:, 0, :], ps[:, 7, 0:P], -1.0, None, ALU.mult))
                    ch.link(nc.vector.scalar_tensor_tensor(m_rest[:], ps[:, 7, 0:P], -1.0, m_piece[:, 0, :], ALU.mult, ALU.subtract))
                    ch.link(nc.vector.tensor_copy(m_piece[:, 1, :], m_rest[:]))
                    nc.vector.tensor_tensor(m_piece[:, 2, :], m_rest[:], m_piece[:, 1, :], ALU.subtract).then_inc(mp_ready, 1)

                    def norm_y(n):
                        gr, q4 = n // 2, n % 2
                        dve.wait_ge(yt_ready, b * YB + n + 1)
                        turned_y = ps[:, 7, :].rearrange("p (t j d) -> p t j d", t=CT, j=G4)
                        ch.link(nc.vector.reciprocal(yrs[:], turned_y[:, :, :, D]))
                        nc.vector.tensor_tensor(yy[:, q4 * CT:q4 * CT + CT, gr * G4 * D:gr * G4 * D + G4 * D].rearrange("p t (j d) -> p t j d", d=D),
                                                turned_y[:, :, :, 0:D], yrs[:].unsqueeze(3).to_broadcast([P, CT, G4, D]), ALU.mult).then_inc(yy_ready, 1)

                    i = 0
                    for gr in range(NG):
                        for q4, kt in blocks:
                            lo, mid, hi = span(q4, kt)
                            c0 = q4 * CHUNK
                            for j in range(G4):
                                if lo < mid:
                                    dve.wait_ge(st_ready, b * NS + i + 1)
                                    nc.vector.tensor_tensor(ps[:, i % 6, lo - c0:mid - c0], ps[:, i % 6, lo - c0:mid - c0],
                                                            bias_k[:, gr * G4 + j, lo - kt * P:mid - kt * P], ALU.add).then_inc(near_ready, 1)
                                i += 1
                            if kt == 3 and (gr, q4) != (0, 0):
                                norm_y(gr * 2 + q4 - 1)
                    norm_y(YB - 1)
                    for h in range(2):
                        c = b * 2 + h
                        dve.wait_ge(o_ready, c + 1)
                        xc = g.X[:, bass.ds(c * CT, CT), :]
                        ch.link(nc.vector.tensor_tensor(xc, ps[:, 2 + h, :].rearrange("p (t d) -> p t d", t=CT), xc, ALU.add))
                        ch.link(dve_new_stats(nc, dve, g, raw, c, ch))
                    assert ch.n == STEPS, ch.n
        s.clear()


def memory_layer(nc, g, wq, wq_sw, wk, wk_sw, wv, w_out, ln_g, ln_b, mem_beta, rope):
    H, D, SEG = 16, 64, 32
    W = SEQ // SEG
    QH = 4
    NQ = H // QH
    PB = QH // 2
    SCALE = D ** -0.5
    E1 = D + 1
    STEPS = NQ * 8
    with ExitStack() as ctx:
        s = Scope(nc, ctx, "im")
        norm = Norm(nc, g, s)
        w4 = s.sb("w4", [P, 4, H // 2, P])
        wv_s = s.sb("wv", [P, H * D])
        wo = s.sb("wo", [P, H // 2, P])
        lncol = s.sb("lncol", [P, 2])
        cs = s.sb("cs", [P, 2, SEG])
        mask = s.sb("mask", [P, SEG])
        gate = s.sb("gate", [P, 3, H])
        XT = s.sb("xt_all", [P, W, BATCH * SEG])
        xw = s.sb("xw", [P, P])
        ee, rr = s.sb("ee", [P, 4 * P]), s.sb("rr", [P, 4 * P])
        t1, t2 = s.sb("t1", [P, 4 * P]), s.sb("t2", [P, 4 * P])
        rope_qk = s.sb("rope_qk", [P, 2, 2 * PB, P])
        el = s.sb("el", [P, 2, 2 * PB, P])
        mem = s.sb("mem", [P, NQ, PB, BATCH, E1])
        zinc = s.sb("zinc", [P, NQ, PB, BATCH])
        vt = s.sb("vt", [P, NQ, QH, D])
        skt = s.sb("skt", [P, NQ, PB, P])
        u1, uu = s.sb("u1", [P, QH, D]), s.sb("uu", [P, 2, QH, D])
        rd = s.sb("rd", [P, QH])
        s1, s2 = s.sb("s1", [P, QH, SEG]), s.sb("s2", [P, QH, SEG])
        pe_, pt = s.sb("pe_", [P, QH, SEG]), s.sb("pt", [P, 2, QH, SEG])
        uu_e, pt_e = s.sb("uu_e", [P, 2, QH, BATCH, D]), s.sb("pt_e", [P, 2, QH, BATCH, SEG])
        own = s.sb("own", [P, BATCH, SEG])
        mx, sm, rs = s.sb("mx", [P, QH]), s.sb("sm", [P, 2, QH]), s.sb("rs", [P, QH])
        dn = s.sb("dn", [P, QH])
        m1, m2 = s.sb("m1", [P, 2, QH, D]), s.sb("m2", [P, QH, D])
        oo = s.sb("oo", [P, H * D])
        ot = s.sb("ot", [P, H // 2, P])
        raw = s.sb("raw", [P, CT, 6])
        b_a, b_s, b_v, b_sc, b_pv, b_pr, b_nu, b_up = (s.ps(n, [P, 512]) for n in ("b_a", "b_s", "b_v", "b_sc", "b_pv", "b_pr", "b_nu", "b_up"))

        names = ("loaded", "made", "g_ready", "setup", "chain", "xn_ready", "turned", "xt_ready", "xw_ready", "proj_ready", "v_ready",
                 "er_ready", "v_copied", "ab_used", "el_ready", "rope_ready", "sk_turned", "sk_copied", "prev_ready", "num_ready", "s_ready",
                 "s1_ready", "s2_ready", "p_ready", "pt_ready", "u_ready", "m1_ready", "pv_ready", "upd_ready", "m2_ready",
                 "mem_ready", "prev_even", "s_even", "num_even", "ue_ready", "pte_ready", "o_ready", "ot_ready", "ot_copied", "out_ready", "x_ready", "stats")
        S = {n: s.sem(n) for n in names}

        def score_view(ap):
            return ap[:, 0:QH * SEG].rearrange("p (h k) -> p h k", h=QH)

        def head_view(ap, width):
            return ap[:, 0:QH * width].rearrange("p (h d) -> p h d", h=QH)

        def segment(w, project, recall, update, turn, add, first=False, last=False):
            for slot in range(NQ):
                k = w * NQ + slot
                if slot != 2 and not last:
                    project(w, slot, k)
                if not (first and slot < 1 or last and slot > 0):
                    recall(w, (slot - 1) % NQ, k - 1)
                if slot == 2 and not first:
                    turn(w)
                if not (first and slot < 2 or last and slot > 1):
                    update(w, (slot - 2) % NQ, k - 2)
                if slot == 2 and not last:
                    project(w, slot, k)
                if slot == 2 and not first:
                    add(w)

        def idle(*_):
            pass

        with nc.Block() as block:
            @block.sync
            def _(sp):
                for i, m in enumerate((wq, wq_sw, wk, wk_sw)):
                    sp.dma_start(w4[:, i], m.rearrange("d (n f) -> d n f", f=P)).then_inc(S["loaded"], 16)
                sp.dma_start(wv_s[:], wv).then_inc(S["loaded"], 16)
                sp.dma_start(wo[:], w_out.rearrange("(n f) d -> f n d", f=P)).then_inc(S["loaded"], 16)
                sp.dma_start(lncol[:, 0:1], ln_g.rearrange("(p a) -> p a", a=1)).then_inc(S["loaded"], 16)
                sp.dma_start(lncol[:, 1:2], ln_b.rearrange("(p a) -> p a", a=1)).then_inc(S["loaded"], 16)
                sp.dma_start(cs[:], rope).then_inc(S["loaded"], 16)
                sp.dma_start(gate[:, 0, :], mem_beta.rearrange("a h b c -> (a h b c)").partition_broadcast(P)).then_inc(S["loaded"], 16)

            @block.gpsimd
            def _(pool):
                nc.gpsimd.memset(mask[:], 0.0).then_inc(S["made"], 1)
                for b in range(BATCH):
                    pool.wait_ge(S["made"], b + 1)
                    nc.gpsimd.affine_select(out=mask[32 * b:32 * b + 32, :], in_=mask[32 * b:32 * b + 32, :], compare_op=ALU.is_ge, fill=-1.0e30,
                                            base=0, pattern=[[-1, SEG]], channel_multiplier=1).then_inc(S["made"], 1)
                pool.wait_ge(S["made"], 5)
                nc.gpsimd.memset(mem[:], 0.0).then_inc(S["made"], 1)
                pool.wait_ge(S["made"], 6)
                nc.gpsimd.memset(mem[:, :, :, :, D], 1.0e-6).then_inc(S["made"], 1)
                nc.gpsimd.memset(uu_e[:], 0.0).then_inc(S["made"], 1)
                nc.gpsimd.memset(own[:], 0.0).then_inc(S["made"], 1)
                for b in range(BATCH):
                    pool.wait_ge(S["made"], 9 + b)
                    nc.gpsimd.memset(own[SEG * b:SEG * b + SEG, b, :], 1.0).then_inc(S["made"], 1)
                pool.wait_ge(S["made"], 13)

                def project(w, q, k):
                    if some(k - 1):
                        pool.wait_ge(S["s_ready"], k - 1)
                    pool.wait_ge(S["ab_used"], k + 2)
                    nc.gpsimd.tensor_tensor(rope_qk[:, q % 2].rearrange("p a b -> p (a b)"), t1[:], t2[:], ALU.add).then_inc(S["rope_ready"], 1)

                def recall(w, q, k):
                    r = q % 2
                    pool.wait_ge(S["pt_ready"], k + 1)
                    if some(k - 1):
                        pool.wait_ge(S["pv_ready"], k - 1)
                    shape = [P, QH, BATCH, SEG]
                    nc.gpsimd.tensor_tensor(pt_e[:, r], pt[:, r].unsqueeze(2).to_broadcast(shape), own[:].unsqueeze(1).to_broadcast(shape), ALU.mult).then_inc(S["pte_ready"], 1)

                def update(w, q, k):
                    if q == 0 and some(w):
                        pool.wait_ge(S["ot_ready"], w)
                    pool.wait_ge(S["m2_ready"], k + 1)
                    nc.gpsimd.tensor_tensor(oo[:, q * QH * D:(q + 1) * QH * D].rearrange("p (h d) -> p h d", h=QH), m1[:, q % 2], m2[:], ALU.add).then_inc(S["o_ready"], 1)

                stages = (project, recall, update, idle, idle)
                segment(0, *stages, first=True)
                with pool.Fori(1, W) as w:
                    segment(w, *stages)
                segment(W, *stages, last=True)

            @block.scalar
            def _(act):
                norm.act_std(act)
                act.wait_ge(S["loaded"], 160)
                nc.scalar.activation(gate[:, 1, :], gate[:, 0, :], ACT.Exp, scale=-1.0)
                nc.scalar.activation(gate[:, 2, :], gate[:, 0, :], ACT.Exp).then_inc(S["g_ready"], 1)
                with act.Fori(0, BATCH) as b:
                    for h in range(2):
                        act.wait_ge(S["turned"], b * 2 + h + 1)
                        out = XT[:, h * 16:h * 16 + 16, bass.ds(b * SEG, SEG)]
                        nc.scalar.activation(out, b_a[:].rearrange("p (w t) -> p w t", t=SEG), ACT.Identity, scale=lncol[:, 0:1], bias=lncol[:, 1:2]).then_inc(S["xt_ready"], 1)
                act.wait_ge(S["xt_ready"], 8)

                def project(w, q, k):
                    if q == 0:
                        if some(k):
                            act.wait_ge(S["v_ready"], k)
                        nc.scalar.activation(xw[:], XT[:, bass.ds(w, 1), :].rearrange("p a b -> p (a b)"), ACT.Copy).then_inc(S["xw_ready"], 1)
                    act.wait_ge(S["proj_ready"], k + 1)
                    act.wait_ge(S["el_ready"], k + 1)
                    nc.scalar.activation(ee[:], b_a[:], ACT.Exp)
                    nc.scalar.activation(rr[:], b_a[:], ACT.Relu).then_inc(S["er_ready"], 1)
                    act.wait_ge(S["v_ready"], k + 1)
                    nc.scalar.activation(vt[:, q].rearrange("p a b -> p (a b)"), b_v[:, 0:QH * D], ACT.Copy).then_inc(S["v_copied"], 1)

                def recall(w, q, k):
                    act.wait_ge(S["sk_turned"], k + 1)
                    nc.scalar.activation(skt[:, q].rearrange("p a b -> p (a b)"), b_up[:, 0:PB * P], ACT.Copy).then_inc(S["sk_copied"], 1)
                    act.wait_ge(S["u_ready"], k + 2)
                    for b in range(BATCH):
                        tok = slice(SEG * b, SEG * b + SEG)
                        last = nc.scalar.activation(uu_e[tok, q % 2, :, b, :], uu[tok, q % 2], ACT.Copy)
                    last.then_inc(S["ue_ready"], 1)
                    act.wait_ge(S["s2_ready"], k + 1)
                    nc.scalar.activation(pe_[:], s2[:], ACT.Exp, scale=SCALE).then_inc(S["p_ready"], 1)

                def turn(w):
                    act.wait_ge(S["ot_ready"], w)
                    nc.scalar.activation(ot[:, 0:4].rearrange("p a b -> p (a b)"), b_a[:], ACT.Copy)
                    nc.scalar.activation(ot[:, 4:8].rearrange("p a b -> p (a b)"), b_s[:], ACT.Copy).then_inc(S["ot_copied"], 1)

                stages = (project, recall, idle, turn, idle)
                segment(0, *stages, first=True)
                with act.Fori(1, W) as w:
                    segment(w, *stages)
                segment(W, *stages, last=True)

            @block.tensor
            def _(pe):
                def project(w, q, k):
                    pe.wait_ge(S["ab_used"], k + 1)
                    if q == 2 and some(w):
                        pe.wait_ge(S["ot_copied"], w)
                    x = XT[:, bass.ds(w, 1), :].rearrange("p a b -> p (a b)")
                    for i in range(2):
                        for n in range(PB):
                            c = (i * PB + n) * P
                            nc.tensor.matmul(b_a[:, c:c + P], w4[:, 2 * i, q * PB + n, :], x, start=True, stop=True)
                            last = nc.tensor.matmul(b_s[:, c:c + P], w4[:, 2 * i + 1, q * PB + n, :], x, start=True, stop=True)
                    last.then_inc(S["proj_ready"], 1)
                    pe.wait_ge(S["v_copied"], k + 1)
                    if q == 0:
                        pe.wait_ge(S["xw_ready"], w + 1)
                    if q == NQ - 1 and some(w):
                        pe.wait_ge(S["x_ready"], w)
                    nc.tensor.matmul(b_v[:, 0:QH * D], xw[:], wv_s[:, q * QH * D:(q + 1) * QH * D], start=True, stop=True).then_inc(S["v_ready"], 1)

                def for_heads(parity, fn):
                    half = slice(D * parity, D * parity + D)
                    for blk in range(PB):
                        for b in range(BATCH):
                            last = fn(2 * blk + parity, half, blk, b, slice(SEG * b, SEG * b + SEG))
                    return last

                def recall(w, q, k):
                    r = q % 2
                    pe.wait_ge(S["el_ready"], k + 2)
                    if some(k - 1):
                        pe.wait_ge(S["mem_ready"], k - 1)
                    elif k == 1:
                        pe.wait_ge(S["sk_copied"], k)
                    for n in range(PB):
                        last = nc.tensor.transpose(b_up[:, n * P:n * P + P], el[:, r, PB + n, :], g.ident[:])
                    last.then_inc(S["sk_turned"], 1)
                    prev = lambda h, half, blk, b, tok: nc.tensor.matmul(b_pr[tok, h * E1:h * E1 + E1], el[half, r, PB + blk, tok], mem[half, q, blk, b, :], start=True, stop=True, skip_group_check=True)
                    score = lambda h, half, blk, b, tok: nc.tensor.matmul(b_sc[tok, h * SEG:h * SEG + SEG], rope_qk[half, r, blk, tok], rope_qk[half, r, PB + blk, tok], start=True, stop=True, skip_group_check=True)
                    num = lambda h, half, blk, b, tok: nc.tensor.matmul(b_nu[tok, h * E1:h * E1 + E1], el[half, r, blk, tok], mem[half, q, blk, b, :], start=True, stop=True, skip_group_check=True)
                    hold(pe, S["u_ready"], k + 1)
                    for_heads(0, prev).then_inc(S["prev_even"], 1)
                    hold(pe, S["rope_ready"], k + 1)
                    hold(pe, S["s1_ready"], k + 1)
                    for_heads(0, score).then_inc(S["s_even"], 1)
                    hold(pe, S["prev_even"], k + 1)
                    for_heads(1, prev).then_inc(S["prev_ready"], 1)
                    hold(pe, S["m1_ready"], k + 1)
                    for_heads(0, num).then_inc(S["num_even"], 1)
                    hold(pe, S["s_even"], k + 1)
                    for_heads(1, score).then_inc(S["s_ready"], 1)
                    hold(pe, S["num_even"], k + 1)
                    for_heads(1, num).then_inc(S["num_ready"], 1)

                def update(w, q, k):
                    r = q % 2
                    if isinstance(k, int) and k == W * NQ - 1:
                        pe.wait_ge(S["mem_ready"], k)
                    else:
                        pe.wait_ge(S["sk_copied"], k + 2)
                    pe.wait_ge(S["ue_ready"], k + 1)
                    for h in range(QH):
                        half, c = slice(D * (h % 2), D * (h % 2) + D), h // 2 * BATCH * D
                        last = nc.tensor.matmul(b_up[half, c:c + BATCH * D], skt[:, q, h // 2, half], uu_e[:, r, h].rearrange("p b d -> p (b d)"), start=True, stop=True, skip_group_check=True)
                    last.then_inc(S["upd_ready"], 1)
                    pe.wait_ge(S["pte_ready"], k + 1)
                    if some(k):
                        pe.wait_ge(S["m2_ready"], k)
                    for h in range(QH):
                        last = nc.tensor.matmul(b_pv[:, h * D:h * D + D], pt_e[:, r, h].rearrange("p b t -> p (b t)"), vt[:, q, h, :], start=True, stop=True)
                    last.then_inc(S["pv_ready"], 1)

                def turn(w):
                    pe.wait_ge(S["o_ready"], w * NQ)
                    pe.wait_ge(S["ab_used"], w * NQ + 1 if isinstance(w, int) and w == W else w * NQ + 3)
                    for n in range(H // 2):
                        last = nc.tensor.transpose((b_a, b_s)[n // 4][:, n % 4 * P:n % 4 * P + P], oo[:, n * P:n * P + P], g.ident[:])
                    last.then_inc(S["ot_ready"], 1)

                def add(w):
                    pe.wait_ge(S["ot_copied"], w)
                    pe.wait_ge(S["v_copied"], w * NQ + 1 if isinstance(w, int) and w == W else w * NQ + 4)
                    for n in range(H // 2):
                        last = nc.tensor.matmul(b_v[:, 0:P], ot[:, n, :], wo[:, n, :], start=(n == 0), stop=(n == H // 2 - 1))
                    last.then_inc(S["out_ready"], 1)

                pe.wait_ge(S["loaded"], 160)
                pe.wait_ge(S["made"], 13)
                with pe.Fori(0, 2 * BATCH) as c:
                    pe.wait_ge(S["xn_ready"], c + 1)
                    for n in range(CT):
                        last = nc.tensor.transpose(b_a[:, n * P:n * P + P], norm.xn[:, n, :], g.ident[:])
                    last.then_inc(S["turned"], 1)
                pe.wait_ge(S["xt_ready"], 2 * BATCH)
                stages = (project, recall, update, turn, add)
                segment(0, *stages, first=True)
                with pe.Fori(1, W) as w:
                    segment(w, *stages)
                segment(W, *stages, last=True)

            @block.vector
            def _(dve):
                norm.dve_rstd(dve)
                st = Chain(dve, S["setup"])
                dve.wait_ge(S["g_ready"], 1)
                dve.wait_ge(S["made"], 13)
                st.link(nc.vector.tensor_scalar_add(gate[:, 1:3, :], gate[:, 1:3, :], 1.0))
                for n, credit in (("ab_used", 1), ("v_copied", 1), ("el_ready", 1), ("u_ready", 1), ("s1_ready", 1), ("m1_ready", 1)):
                    dve.sem_inc(S[n], credit)
                with dve.Fori(0, 2 * BATCH) as c:
                    norm.dve_rows(c).then_inc(S["xn_ready"], 1)
                    dve.wait_ge(S["xt_ready"], c + 1)

                def project(w, q, k, ch):
                    dve.wait_ge(S["proj_ready"], k + 1)
                    if some(k):
                        dve.wait_ge(S["rope_ready"], k)
                    seg = lambda ap: ap.rearrange("p (n t) -> p n t", t=SEG)
                    tab = lambda i: bc(cs[:, i, :], 4 * P // SEG)
                    nc.vector.tensor_tensor(seg(t2[:]), seg(b_s[:]), tab(1), ALU.mult)
                    dve.wait_ge(S["er_ready"], k + 1)
                    nc.vector.tensor_tensor(seg(t1[:]), seg(b_a[:]), tab(0), ALU.mult).then_inc(S["ab_used"], 1)
                    e2 = el[:, q % 2].rearrange("p a b -> p (a b)")
                    nc.vector.scalar_tensor_tensor(e2, ee[:], 1.0, rr[:], ALU.min, ALU.add).then_inc(S["el_ready"], 1)
                    dve.wait_ge(S["el_ready"], k + 2)
                    nc.vector.tensor_reduce(zinc[:, q].rearrange("p a b -> p (a b)"), el[:, q % 2, PB:2 * PB].rearrange("p a (b t) -> p (a b) t", t=SEG), AX_X, ALU.add)

                def recall_and_update(w, q, k, ch, recalls=True, updates=True):
                    r, kw, qw = q % 2, k - 1, (q - 1) % NQ
                    rw = qw % 2
                    pr, nu = head_view(b_pr, E1), head_view(b_nu, E1)
                    m = mem[:, qw].rearrange("p a b e -> p (a b) e")
                    done = {}

                    def mark(name, ins):
                        ch.mark(ins)
                        done[name] = ch.n

                    def after(name):
                        dve.wait_ge(S["chain"], ch.base + done[name])

                    if recalls:
                        dve.wait_ge(S["prev_ready"], k + 1)
                        mark("rd", nc.vector.reciprocal(rd[:], pr[:, :, D]))
                    if updates:
                        dve.wait_ge(S["pt_ready"], kw + 1)
                        if some(kw):
                            dve.wait_ge(S["m2_ready"], kw)
                        mark("rsum", nc.vector.tensor_tensor(rs[:], sm[:, rw], gate[:, 2, qw * QH:qw * QH + QH], ALU.mult))
                    if recalls:
                        after("rd")
                        mark("u1", nc.vector.tensor_tensor(u1[:], pr[:, :, 0:D], bl(rd[:], D), ALU.mult))
                    if updates:
                        after("rsum")
                        mark("rs", nc.vector.reciprocal(rs[:], rs[:]))
                    if recalls:
                        dve.wait_ge(S["s_ready"], k + 1)
                        nc.vector.tensor_tensor(s1[:], score_view(b_sc), bc(mask[:], QH), ALU.add).then_inc(S["s1_ready"], 1)
                        dve.wait_ge(S["v_copied"], k + 2)
                        after("u1")
                        nc.vector.tensor_tensor(uu[:, r], vt[:, q], u1[:], ALU.subtract).then_inc(S["u_ready"], 1)
                        dve.wait_ge(S["s1_ready"], k + 2)
                        mark("mx", nc.vector.tensor_reduce(mx[:], s1[:], AX_X, ALU.max))
                        dve.wait_ge(S["num_ready"], k + 1)
                        mark("den", nc.vector.scalar_tensor_tensor(dn[:], nu[:, :, D], 1.0e-6, gate[:, 1, q * QH:q * QH + QH], ALU.add, ALU.mult))
                        after("mx")
                        nc.vector.tensor_tensor(s2[:], s1[:], bl(mx[:], SEG), ALU.subtract).then_inc(S["s2_ready"], 1)
                        after("den")
                        mark("dn", nc.vector.reciprocal(dn[:], dn[:]))
                    if updates:
                        dve.wait_ge(S["upd_ready"], kw + 1)
                        mark("mem", nc.vector.tensor_tensor(m[:, :, 0:D], m[:, :, 0:D], b_up[:].rearrange("p (n d) -> p n d", d=D), ALU.add))
                    if recalls:
                        after("dn")
                        if some(k - 1):
                            dve.wait_ge(S["o_ready"], k - 1)
                        nc.vector.tensor_tensor(m1[:, r], nu[:, :, 0:D], bl(dn[:], D), ALU.mult).then_inc(S["m1_ready"], 1)
                    if updates:
                        after("mem")
                        nc.vector.tensor_tensor(m[:, :, D], m[:, :, D], zinc[:, qw].rearrange("p a b -> p (a b)"), ALU.add).then_inc(S["mem_ready"], 1)
                    if recalls:
                        dve.wait_ge(S["p_ready"], k + 1)
                        nc.vector.tensor_reduce(sm[:, r], pe_[:], AX_X, ALU.add)
                        nc.vector.transpose(pt[:, r].rearrange("p a b -> p (a b)"), pe_[:].rearrange("p a b -> p (a b)")).then_inc(S["pt_ready"], 1)
                    if updates:
                        after("rs")
                        if some(kw):
                            dve.wait_ge(S["o_ready"], kw)
                        dve.wait_ge(S["pv_ready"], kw + 1)
                        nc.vector.tensor_tensor(m2[:], head_view(b_pv, D), bl(rs[:], D), ALU.mult).then_inc(S["m2_ready"], 1)

                first_links = []

                def step(w, n, j, tile):
                    ch = Chain(dve, S["chain"], first_links[0] + (w - 1) * STEPS if first_links else 0)

                    def add(w):
                        dve.wait_ge(S["out_ready"], w)
                        for b in range(BATCH):
                            rows = g.X[SEG * j:SEG * j + SEG, bass.ds(tile + b * (SEQ // P), 1), :].rearrange("p a d -> p (a d)")
                            last = nc.vector.tensor_tensor(rows, b_v[SEG * b:SEG * b + SEG, 0:P], rows, ALU.add)
                        last.then_inc(S["x_ready"], 1)

                    first, last = n == "first", n == "last"
                    for slot in range(NQ):
                        k = w * NQ + slot
                        if slot != 2 and not last:
                            project(w, slot, k, ch)
                        recalls, updates = not (first and slot < 1 or last and slot > 0), not (first and slot < 2 or last and slot > 1)
                        if recalls or updates:
                            recall_and_update(w, (slot - 1) % NQ, k - 1, ch, recalls, updates)
                        if slot == 2 and not last:
                            project(w, slot, k, ch)
                        if slot == 2 and not first:
                            add(w)
                    assert n != "inner" or ch.n == STEPS, ch.n
                    first_links.append(ch.n)

                step(0, "first", None, None)
                with dve.Fori(0, W // 4 - 1) as i:
                    for j in range(4):
                        step(i * 4 + (j + 1), "inner", j, i)
                for j in range(4):
                    w = W - 3 + j
                    step(w, "last" if w == W else "inner", j, W // 4 - 1)
                dve.wait_ge(S["x_ready"], W)
                with dve.Fori(0, NC_) as c:
                    ch = Chain(dve, S["stats"], c * 3)
                    ch.link(dve_new_stats(nc, dve, g, raw, c, ch))
        s.clear()


class Globals:
    pass


STAGES = list(range(8))


def build(nc, a, out):
    with ExitStack() as ctx:
        s = Scope(nc, ctx, "g")
        g = Globals()
        g.X = s.sb("x", [P, NT, P])
        g.MV, g.mv4 = s.sb("mv", [P, NT, 2]), s.sb("mv4", [P, CT, 2])
        g.ident, g.ones = s.sb("ident", [P, P]), s.sb("ones", [P, P])
        g.eps, g.iota8 = s.sb("eps", [P, 1]), s.sb("iota8", [P, 8])
        g.stored = s.sem("stored")
        E0, E1 = a["L0_ffn_gate"].shape[1], a["L1_ffn_w_router"].shape[1]
        first_weights, later_weights = ctx.enter_context(ExitStack()), ctx.enter_context(ExitStack())
        s0 = Scope(nc, first_weights, "w0")
        w1, w3, w2 = (s0.sb(n, sh) for n, sh in (("w1", [P, E0, 512]), ("w3", [P, E0, 512]), ("w2", [P, E0, 4, P])))
        gate = s0.sb("gate", [P, E0])
        g.weights_loaded = s.sem("weights_loaded")

        def load_weights(sp):
            for dst, src in ((gate[:], a["L0_ffn_gate"]), (w1[:], a["L0_ffn_experts_w1"].rearrange("e h i -> h e i")),
                             (w3[:], a["L0_ffn_experts_w3"].rearrange("e h i -> h e i")),
                             (w2[:], a["L0_ffn_experts_w2"].rearrange("e (b i) h -> i e b h", i=P))):
                sp.dma_start(dst, src).then_inc(g.weights_loaded, 16)
            sp.wait_ge(g.weights_loaded, 16 * 4)
        g.load_weights = load_weights
        later = {}

        def load_later_weights():
            s1 = Scope(nc, later_weights, "w1")
            wv, wp, router = (s1.sb(n, sh) for n, sh in (("wv", [P, E1, 1024]), ("wproj", [P, E1, 4, P]), ("router", [P, E1])))
            later.update(wv=wv, wp=wp, router=router)
            with nc.Block() as block:
                @block.sync
                def _(sp):
                    for dst, src in ((router[:], a["L1_ffn_w_router"]), (wv[:], a["L1_ffn_w_v"].rearrange("e d h -> d e h")),
                                     (wp[:], a["L1_ffn_w_proj"].rearrange("e (b i) d -> i e b d", i=P))):
                        sp.dma_start(dst, src).then_inc(g.weights_loaded, 16)
                    sp.wait_ge(g.weights_loaded, 16 * 7)

        load_and_constants(nc, g, a["L0_attn_a_x"])

        def l0_experts(name):
            expert_layer(nc, g, name, E0, 2, gate, lambda e: tile_of(w1, e), lambda e: tile_of(w3, e), lambda e, j: tile_of(w2[:, :, j, :], e))

        def l1_experts(name):
            if not later:
                load_later_weights()
            wv, wp, router = later["wv"], later["wp"], later["router"]
            expert_layer(nc, g, name, E1, 1, router, lambda e: tile_of(wv[:, :, 0:512], e), lambda e: tile_of(wv[:, :, 512:1024], e), lambda e, j: tile_of(wp[:, :, j, :], e))

        layers = [
            lambda: ssm_layer(nc, g, *(a["L0_attn_a_" + n] for n in ("W_in", "b_in", "log_A", "B_p", "C_p", "W_out", "b_out", "gamma", "beta"))),
            lambda: l0_experts("ffn0"),
            lambda: landmark_layer(nc, g, *(a["L0_attn_b_" + n] for n in ("Wq", "bq", "Wk", "bk", "Wv", "bv"))),
            lambda: l0_experts("ffn1"),
            lambda: causal_layer(nc, g, *(a["L1_attn_a_" + n] for n in ("Wq", "bq", "Wk", "bk", "Wv", "bv", "Wp", "bp", "rel_bias_table", "Wq_swapped", "bq_swapped", "Wk_swapped", "bk_swapped")), a["rope_a"], a["buckets"]),
            lambda: l1_experts("ffn2"),
            lambda: memory_layer(nc, g, a["wq_halves"], a["wq_swapped"], a["wk_halves"], a["wk_swapped"], a["wv"], *(a["L1_attn_b_" + n] for n in ("w_out", "ln_g", "ln_b", "mem_beta")), a["rope_b"]),
            lambda: l1_experts("ffn3"),
        ]
        for n in STAGES:
            if n == 4:
                first_weights.close()
            layers[n]()
        later_weights.close()
        with nc.Block() as block:
            @block.sync
            def _(sp):
                sp.dma_start(out.rearrange("b (n p) d -> p (b n) d", p=P), g.X[:]).then_inc(g.stored, 16)
                sp.wait_ge(g.stored, 16)


def shape_constants():
    import math

    import numpy as np

    T, D = 1024, 8
    inv = (1.0 / 10000.0 ** (np.arange(0, D, 2, dtype=np.float32) / D)).astype(np.float32)
    ang = (np.arange(T, dtype=np.float32)[None, :] * inv[:, None]).astype(np.float32)
    cos, sin = np.cos(ang), np.sin(ang)
    rope = np.stack([np.tile(np.concatenate([cos, cos]), (16, 1)), np.tile(np.concatenate([-sin, sin]), (16, 1))], 1)

    def bucket(n):
        if n < 16:
            return n
        big = np.log(np.float32(n) / np.float32(16)) / np.float32(math.log(8.0)) * np.float32(16)
        return min(16 + int(big), 31)

    pick = np.zeros((33, 2, 384), np.float32)
    for u in range(384):
        for side, n in ((0, u - 128), (1, 255 - u)):
            if n < 0:
                pick[32, side, u] = -1.0e30
            else:
                pick[bucket(n), side, u] += 1.0
                pick[31, side, u] -= 1.0
    freq = 10000.0 ** (-np.arange(0, 64, 2, dtype=np.float64) / 64)
    ang = freq[:, None] * np.arange(32)[None, :]
    cos, sin = np.cos(ang), np.sin(ang)
    rope_b = np.stack([np.tile(np.concatenate([cos, cos]), (2, 1)), np.tile(np.concatenate([-sin, sin]), (2, 1))], 1)
    return rope.astype(np.float32), pick.reshape(33, 768), rope_b.astype(np.float32)


_INS = ['L0_attn_a_x', 'L0_attn_a_W_in', 'L0_attn_a_b_in', 'L0_attn_a_log_A', 'L0_attn_a_B_p', 'L0_attn_a_C_p', 'L0_attn_a_W_out', 'L0_attn_a_b_out', 'L0_attn_a_gamma', 'L0_attn_a_beta', 'L0_attn_b_Wq', 'L0_attn_b_bq', 'L0_attn_b_Wk', 'L0_attn_b_bk', 'L0_attn_b_Wv', 'L0_attn_b_bv', 'L0_ffn_gate', 'L0_ffn_experts_w1', 'L0_ffn_experts_w2', 'L0_ffn_experts_w3', 'L1_attn_a_Wq', 'L1_attn_a_bq', 'L1_attn_a_Wk', 'L1_attn_a_bk', 'L1_attn_a_Wv', 'L1_attn_a_bv', 'L1_attn_a_Wp', 'L1_attn_a_bp', 'L1_attn_a_rel_bias_table', 'L1_attn_b_w_qkv', 'L1_attn_b_w_out', 'L1_attn_b_ln_g', 'L1_attn_b_ln_b', 'L1_attn_b_mem_beta', 'L1_ffn_w_router', 'L1_ffn_w_v', 'L1_ffn_w_proj']


def kernel(**inputs):
    import numpy as _np
    import concourse.bacc as _bacc
    from concourse import mybir as _mybir
    from concourse.bass_utils import run_bass_kernel_spmd as _run

    laid = dict(inputs)
    for name in ("L0_attn_a_W_in", "L0_attn_a_W_out"):
        laid[name] = _np.asarray(inputs[name]).T
    for name in ("Wq", "bq", "Wk", "bk"):
        m = _np.asarray(inputs["L1_attn_a_" + name])
        laid["L1_attn_a_" + name + "_swapped"] = m.reshape(m.shape[:-1] + (16, 2, 4))[..., ::-1, :].reshape(m.shape)
    qkv = _np.asarray(inputs["L1_attn_b_w_qkv"])
    for i, side in enumerate("qk"):
        m = qkv[:, i * 1024:i * 1024 + 1024].reshape(128, 16, 32, 2)
        laid["w" + side + "_halves"] = m.transpose(0, 1, 3, 2).reshape(128, 1024)
        laid["w" + side + "_swapped"] = m[..., ::-1].transpose(0, 1, 3, 2).reshape(128, 1024)
    laid["wv"] = qkv[:, 2048:]
    del laid["L1_attn_b_w_qkv"]
    laid["rope_a"], laid["buckets"], laid["rope_b"] = shape_constants()
    nc = _bacc.Bacc("TRN2", target_bir_lowering=False, num_devices=1)
    arrays, aps = {}, {}
    for name in laid:
        arr = _np.ascontiguousarray(laid[name])
        arrays[f"in_{name}_dram"] = arr
        aps[name] = nc.dram_tensor(f"in_{name}_dram", arr.shape, _mybir.dt.from_np(arr.dtype), kind="ExternalInput").ap()
    out = nc.dram_tensor("out_0_dram", (4, 1024, 128), _mybir.dt.float32, kind="ExternalOutput").ap()
    build(nc, aps, out)
    r = _run(nc, [arrays], core_ids=[0])
    return r.results[0]["out_0_dram"]
```

```python
from contextlib import ExitStack

import concourse.bass as bass
from concourse import mybir

F32 = mybir.dt.float32
U32 = mybir.dt.uint32
I32 = mybir.dt.int32
ALU = mybir.AluOpType
ACT = mybir.ActivationFunctionType
AX_X = mybir.AxisListType.X

P = 128
BATCH, SEQ = 4, 1024
NT = BATCH * SEQ // P
CT = 4
CHUNK = CT * P
NC_ = NT // CT
EPS = 1e-5


class Scope:

    def __init__(self, nc, ctx, prefix):
        self.nc, self.ctx, self.prefix, self.sems = nc, ctx, prefix, []

    def sb(self, name, shape, dt=F32):
        return self.ctx.enter_context(self.nc.sbuf_tensor(f"{self.prefix}_{name}", shape, dt))

    def ps(self, name, shape, dt=F32):
        return self.ctx.enter_context(self.nc.psum_tensor(f"{self.prefix}_{name}", shape, dt))

    def sem(self, name):
        self.sems.append(self.nc.alloc_semaphore(f"{self.prefix}_{name}"))
        return self.sems[-1]

    def clear(self):
        self.nc.clear_and_free_semaphores(self.sems)
        self.nc.all_engine_barrier()


class Chain:

    def __init__(self, eng, sem, base=0):
        self.eng, self.sem, self.base, self.n = eng, sem, base, 0

    def mark(self, ins):
        self.n += 1
        return ins.then_inc(self.sem, 1)

    def wait(self):
        hold(self.eng, self.sem, self.base + self.n)

    def link(self, ins):
        self.mark(ins)
        self.wait()


def hold(eng, sem, value):
    eng.wait_ge(sem, value)
    eng.nop(nofuse=True)


def bc(ap, k):
    return ap.unsqueeze(1).to_broadcast([ap.shape[0], k, ap.shape[1]])


def bl(ap, n):
    return ap.unsqueeze(2).to_broadcast([ap.shape[0], ap.shape[1], n])


def tile_of(t, n):
    return t[:, bass.ds(n, 1), :].rearrange("p a d -> p (a d)")


def some(k):
    return not isinstance(k, int) or k > 0


def load_and_constants(nc, g, x):
    with ExitStack() as ctx:
        s = Scope(nc, ctx, "init")
        raw = s.sb("raw", [P, NT, 6])
        x_loaded, zeroed = s.sem("x_loaded"), s.sem("zeroed")
        stats_done = s.sem("stats_done")
        with nc.Block() as block:
            @block.sync
            def _(sp):
                xs = x.rearrange("b (n p) d -> p (b n) d", p=P)
                for c in range(NC_):
                    sp.dma_start(g.X[:, CT * c:CT * c + CT, :], xs[:, CT * c:CT * c + CT, :]).then_inc(x_loaded, 16)
                g.load_weights(sp)

            @block.gpsimd
            def _(pool):
                nc.gpsimd.memset(g.ident[:], 0.0).then_inc(zeroed, 1)
                nc.gpsimd.memset(g.eps[:], EPS)
                nc.gpsimd.memset(g.ones[:], 1.0)
                nc.gpsimd.iota(g.iota8[:], pattern=[[1, 8]], base=0, channel_multiplier=0,
                               allow_small_or_imprecise_dtypes=True)
                pool.wait_ge(zeroed, 1)
                nc.gpsimd.affine_select(out=g.ident[:], in_=g.ident[:], compare_op=ALU.not_equal, fill=1.0,
                                        base=0, pattern=[[-1, P]], channel_multiplier=1)

            @block.vector
            def _(dve):
                dve.wait_ge(x_loaded, 16 * NC_)
                for n in range(NT):
                    last = nc.vector.bn_stats(raw[:, n, :], g.X[:, n, :])
                last.then_inc(stats_done, 1)
                dve.wait_ge(stats_done, 1)
                for n in range(NT):
                    nc.vector.bn_aggr(g.MV[:, n, :], raw[:, n, :])
        s.clear()


class Norm:

    def __init__(self, nc, g, s, bufs=1):
        self.nc, self.g = nc, g
        self.std = s.sb("std", [P, NT])
        self.RS = s.sb("rstd", [P, NT])
        self.xn = s.sb("xn", [P, CT, P])
        self.std_ready, self.rs_ready = s.sem("std_ready"), s.sem("rs_ready")

    def act_std(self, act):
        self.nc.scalar.activation(self.std[:], self.g.MV[:, :, 1], ACT.Sqrt, bias=self.g.eps[:, 0:1]).then_inc(self.std_ready, 1)

    def dve_rstd(self, dve):
        dve.wait_ge(self.std_ready, 1)
        self.nc.vector.reciprocal(self.RS[:], self.std[:]).then_inc(self.rs_ready, 1)
        dve.wait_ge(self.rs_ready, 1)

    def dve_rows(self, c):
        for k in range(CT):
            n = c * CT + k
            last = self.nc.vector.tensor_scalar(self.xn[:, k, :], tile_of(self.g.X, n),
                                                tile_of(self.g.MV, n)[:, 0:1], self.RS[:, bass.ds(n, 1)],
                                                ALU.subtract, ALU.mult)
        return last


def dve_new_stats(nc, dve, g, raw, c, ch):
    for k in range(CT):
        last = nc.vector.bn_stats(raw[:, k, :], tile_of(g.X, c * CT + k))
    ch.link(last)
    for k in range(CT):
        last = nc.vector.bn_aggr(g.mv4[:, k, :], raw[:, k, :])
    ch.link(last)
    return nc.vector.tensor_copy(g.MV[:, bass.ds(c * CT, CT), :], g.mv4[:])


def ssm_layer(nc, g, w_in_t, b_in, log_a, b_p, c_p, w_out_t, b_out, gamma, beta):
    with ExitStack() as ctx:
        s = Scope(nc, ctx, "ssm")
        norm = Norm(nc, g, s)
        win, wout, woc = s.sb("win", [P, P]), s.sb("wout", [P, P]), s.sb("woc", [P, P])
        cols = s.sb("cols", [P, 8])
        decay = s.sb("decay", [P, CHUNK])
        rows = s.sb("rows", [P, 2, P])
        bo4 = s.sb("bo4", [1, CT, P])
        xt = s.sb("xt", [P, CHUNK])
        bh = s.sb("bh", [P, CHUNK])
        y = s.sb("y", [P, 2, CHUNK])
        t = s.sb("t", [P, CT, P])
        raw, mv = s.sb("raw", [P, CT, 6]), s.sb("mv", [P, CT, 2])
        so, ro = s.sb("so", [P, CT]), s.sb("ro", [P, CT])
        ps_t, ps_h, ps_o = s.ps("ps_t", [P, CHUNK]), s.ps("ps_h", [P, CHUNK]), s.ps("ps_o", [P, CT, P])
        loaded = s.sem("loaded")
        setup, chain, e_ready = s.sem("setup"), s.sem("chain"), s.sem("e_ready")
        consts_ready = s.sem("consts_ready")
        xn_ready, xn_turned, xt_ready = s.sem("xn_ready"), s.sem("xn_turned"), s.sem("xt_ready")
        h_ready, bh_ready, y_ready, o_ready = s.sem("h_ready"), s.sem("bh_ready"), s.sem("y_ready"), s.sem("o_ready")
        mv_ready, so_ready, o_used = s.sem("mv_ready"), s.sem("so_ready"), s.sem("o_used")
        STEPS = 8

        with nc.Block() as block:
            @block.sync
            def _(sp):
                for dst, src in ((win[:], w_in_t), (wout[:], w_out_t),
                                 (cols[:, 0:1], b_in.rearrange("(p a) -> p a", a=1)),
                                 (cols[:, 1:2], log_a.rearrange("h (d a) -> (h d) a", a=1)),
                                 (cols[:, 2:3], b_p.rearrange("h (d a) -> (h d) a", a=1)),
                                 (cols[:, 3:4], c_p.rearrange("h (d a) -> (h d) a", a=1)),
                                 (rows[:, 0, :], gamma.partition_broadcast(P)),
                                 (rows[:, 1, :], beta.partition_broadcast(P))):
                    sp.dma_start(dst, src).then_inc(loaded, 16)
                for k in range(CT):
                    sp.dma_start(bo4[:, k, :], b_out.rearrange("(a n) -> a n", a=1)).then_inc(loaded, 16)

            @block.scalar
            def _(act):
                norm.act_std(act)
                act.wait_ge(loaded, 16 * 12)
                nc.scalar.activation(cols[:, 6:7], cols[:, 1:2], ACT.Exp).then_inc(e_ready, 1)
                act.wait_ge(consts_ready, 1)

                def incoming(c):
                    act.wait_ge(xn_turned, c + 1)
                    nc.scalar.activation(xt[:], ps_t[:], ACT.Copy).then_inc(xt_ready, 1)
                    act.wait_ge(h_ready, c + 1)
                    act.wait_ge(y_ready, c + 1)
                    nc.scalar.activation(bh[:], ps_h[:], ACT.Identity, bias=cols[:, 5:6], scale=cols[:, 2:3]).then_inc(bh_ready, 1)

                def outgoing(c):
                    act.wait_ge(mv_ready, c + 1)
                    nc.scalar.activation(so[:], mv[:, :, 1], ACT.Sqrt, bias=g.eps[:, 0:1]).then_inc(so_ready, 1)

                incoming(0)
                with act.Fori(1, NC_) as c:
                    incoming(c)
                    outgoing(c - 1)
                outgoing(NC_ - 1)

            @block.tensor
            def _(pe):
                pe.wait_ge(consts_ready, 1)
                with pe.Fori(0, NC_ // 2) as i:
                    for u in range(2):
                        c = i * 2 + u
                        pe.wait_ge(xn_ready, c + 1)
                        for k in range(CT):
                            last = nc.tensor.transpose(ps_t[:, k * P:k * P + P], norm.xn[:, k, :], g.ident[:])
                        last.then_inc(xn_turned, 1)
                        pe.wait_ge(xt_ready, c + 1)
                        pe.wait_ge(y_ready, c + 1)
                        nc.tensor.matmul(ps_h[:], win[:], xt[:], start=True, stop=True).then_inc(h_ready, 1)
                        pe.wait_ge(y_ready, c + 2)
                        pe.wait_ge(o_used, c + 1)
                        nc.tensor.matmul(ps_o[:].rearrange("p a b -> p (a b)"), g.ones[0:1, :], bo4[:].rearrange("p a b -> p (a b)"), start=True, stop=False, skip_group_check=True)
                        for k in range(CT):
                            last = nc.tensor.matmul(ps_o[:, k, :], y[:, u, k * P:k * P + P], woc[:], start=False, stop=True, skip_group_check=True)
                        last.then_inc(o_ready, 1)

            @block.vector
            def _(dve):
                norm.dve_rstd(dve)
                st = Chain(dve, setup)
                dve.wait_ge(e_ready, 1)
                st.link(nc.vector.tensor_scalar_add(cols[:, 6:7], cols[:, 6:7], 1.0))
                st.link(nc.vector.reciprocal(cols[:, 4:5], cols[:, 6:7]))
                nc.vector.tensor_copy(decay[:], cols[:, 4:5].to_broadcast([P, CHUNK]))
                nc.vector.tensor_tensor(cols[:, 5:6], cols[:, 2:3], cols[:, 0:1], ALU.mult)
                st.link(nc.vector.tensor_scalar(woc[:], wout[:], cols[:, 3:4], None, ALU.mult))
                dve.sem_inc(y_ready, 1)
                dve.sem_inc(o_used, 1)
                dve.sem_inc(consts_ready, 1)

                def scan(c, u):
                    dve.wait_ge(bh_ready, c + 1)
                    first = 0.0 if u == 0 else y[:, 0, CHUNK - 1:CHUNK]
                    nc.vector.tensor_tensor_scan(y[:, u, :], decay[:], bh[:], first, ALU.mult, ALU.add).then_inc(y_ready, 1)

                def outgoing(c):
                    ch = Chain(dve, chain, c * STEPS)
                    hold(dve, o_ready, c + 1)
                    for k in range(CT):
                        last = nc.vector.bn_stats(raw[:, k, :], ps_o[:, k, :])
                    ch.link(last)
                    for k in range(CT):
                        last = nc.vector.bn_aggr(mv[:, k, :], raw[:, k, :])
                    last.then_inc(mv_ready, 1)
                    dve.wait_ge(so_ready, c + 1)
                    ch.link(nc.vector.reciprocal(ro[:], so[:]))
                    for k in range(CT):
                        last = nc.vector.tensor_scalar(t[:, k, :], ps_o[:, k, :], mv[:, k, 0:1], ro[:, k:k + 1], ALU.subtract, ALU.mult)
                    last.then_inc(o_used, 1)
                    dve.wait_ge(o_used, c + 2)
                    ch.link(nc.vector.tensor_tensor(t[:], t[:], bc(rows[:, 0, :], CT), ALU.mult))
                    ch.link(nc.vector.tensor_tensor(t[:], t[:], bc(rows[:, 1, :], CT), ALU.add))
                    xc = g.X[:, bass.ds(c * CT, CT), :]
                    ch.link(nc.vector.tensor_tensor(xc, xc, t[:], ALU.add))
                    ch.link(dve_new_stats(nc, dve, g, raw, c, ch))
                    assert ch.n == STEPS, ch.n

                norm.dve_rows(0).then_inc(xn_ready, 1)
                scan(0, 0)
                with dve.Fori(0, NC_ // 2 - 1) as i:
                    for u in range(2):
                        c = i * 2 + (u + 1)
                        norm.dve_rows(c).then_inc(xn_ready, 1)
                        outgoing(c - 1)
                        scan(c, 1 - u)
                norm.dve_rows(NC_ - 1).then_inc(xn_ready, 1)
                outgoing(NC_ - 2)
                scan(NC_ - 1, 1)
                outgoing(NC_ - 1)
        s.clear()


def expert_layer(nc, g, name, experts, top, weights, gate_w, up_g, up_u, down):
    IB = 4
    E = experts
    SLOTS = top * NT + E
    TOKENS = NT * P
    HALF = 12582912.0
    with ExitStack() as ctx:
        s = Scope(nc, ctx, name)
        std, rstd = s.sb("std", [P, NT]), s.sb("rstd", [P, NT])
        xn = s.sb("xn", [P, 2, CT, P])
        xt = s.sb("xt", [P, 2, CHUNK])
        lg = s.sb("logits", [P, 2, NT, E])
        best, is_best = s.sb("best", [P, 2, NT]), s.sb("is_best", [P, NT, E])
        first = s.sb("first", [P, NT])
        hot, hots = s.sb("hot", [P, 2, NT, E]), s.sb("hots", [P, NT, E])
        w_all = s.sb("w_all", [P, 2, NT])
        ex, wsum = s.sb("ex", [P, NT]), s.sb("wsum", [P, NT])
        countdown = s.sb("countdown", [P, E])
        earlier = s.sb("earlier", [P, P])
        pad_t = NT // 2
        upto = s.sb("upto", [P, 2, pad_t + NT, E])
        rank, place = s.sb("rank", [P, NT, E]), s.sb("place", [P, 2, NT, E])
        t128, held = s.sb("t128", [P, NT]), s.sb("held", [P, E, NT])
        tiles, until = s.sb("tiles", [P, E]), s.sb("until", [P, 2, 4 + E])
        start = s.sb("start", [P, E])
        dest, value = s.sb("dest", [P, 2, NT]), s.sb("value", [P, 2, NT])
        tile_no, row_no = s.sb("tile_no", [P, 2, NT]), s.sb("row_no", [P, 2, NT])
        col_id, slot_id, token_id = s.sb("col_id", [P, P]), s.sb("slot_id", [P, SLOTS]), s.sb("token_id", [P, NT])
        oh_row, oh_slot = s.sb("oh_row", [P, 4, CT, P]), s.sb("oh_slot", [P, 4, CT, SLOTS])
        zero_row = s.sb("zero_row", [1, SLOTS])
        spare_row, row_at = s.sb("spare_row", [P, SLOTS]), s.sb("row_at", [P, SLOTS])
        second, token = s.sb("second", [P, SLOTS]), s.sb("token", [P, SLOTS])
        token_at, result_at = s.sb("token_at", [P, SLOTS], U32), s.sb("result_at", [P, SLOTS], U32)
        past, slot_e = s.sb("past", [1, SLOTS, E]), s.sb("slot_e", [1, SLOTS])
        table_e = s.sb("table_e", [1, SLOTS], I32)
        now, then = s.sb("now", [P, 2, 1], U32), s.sb("then", [P, 2, 1], U32)
        xs = s.sb("xs", [P, 2, P])
        xst = s.sb("xst", [P, P])
        sg, hid = s.sb("sg", [P, 2, CHUNK]), s.sb("hid", [P, 2, CHUNK])
        hid_t = s.sb("hid_t", [P, 2, IB, P])
        ys = s.sb("ys", [P, 2, P])
        got = s.sb("got", [P, 4, top, CT, P])
        raw, stats = s.sb("raw", [P, 4 * CT, 6]), s.sb("stats", [P, 4 * CT, 2])
        xn_rows = nc.dram_tensor(f"{name}_x", (NT * P, P), F32).ap()
        y_rows = nc.dram_tensor(f"{name}_y", (top * TOKENS + SLOTS * P, P), F32).ap()
        ps = s.ps("ps", [P, 8, 512])
        ps_l = ps[:, 6, 0:NT * E].rearrange("p (t e) -> p t e", e=E)
        ps_rank, ps_count = (ps[:, i, 0:NT * E].rearrange("p (t e) -> p t e", e=E) for i in (0, 1))
        names = ("std_ready", "ready", "made", "xn_ready", "xn_stored0", "xn_stored1", "xn_turned", "xt_ready", "lg_ready",
                 "gap_ready", "ex_ready", "hots_ready", "ranks_ready", "oh_ready", "ohs_ready", "values_ready", "oh_used", "table_ready", "chain", "combine_chain",
                 "picked", "xs_loaded0", "xs_loaded1", "x_turned", "xst_ready", "gu_ready", "silu_ready", "hid_ready", "h_turned", "ht_ready",
                 "y_ready", "y_copied", "y_stored0", "y_stored1", "y_loaded0", "y_loaded1", "y_loaded2", "y_loaded3", "weighted", "combined")
        S = {n: s.sem(n) for n in names}

        with nc.Block() as block:
            @block.sync
            def _(sp):
                with sp.Fori(0, NC_ // 2) as i:
                    for par in range(2):
                        hold(sp, S["xn_ready"], i * 2 + (par + 1))
                        sp.dma_start(xn_rows[bass.ds((i * 2 + par) * CHUNK, CHUNK), :].rearrange("(k p) d -> p k d", p=P), xn[:, par]).then_inc(S[f"xn_stored{par}"], 16)
                for par in range(2):
                    sp.wait_ge(S[f"y_stored{par}"], SLOTS // 2 * 16)

                def load(c, buf):
                    for r in range(top):
                        sp.dma_start(got[:, buf, r], y_rows[bass.ds(c * CHUNK + r * TOKENS, CHUNK), :].rearrange("(k p) d -> p k d", p=P)).then_inc(S[f"y_loaded{buf}"], 16)

                for buf in range(4):
                    load(buf, buf)
                for buf in range(4):
                    sp.wait_ge(S["combined"], buf + 1)
                    load(4 + buf, buf)

            @block.gpsimd
            def _(pool):
                approx = dict(allow_small_or_imprecise_dtypes=True)
                nc.gpsimd.memset(earlier[:], 1.0).then_inc(S["made"], 1)
                pool.wait_ge(S["made"], 1)
                nc.gpsimd.affine_select(out=earlier[:], in_=earlier[:], compare_op=ALU.is_gt, fill=0.0,
                                        base=0, pattern=[[1, P]], channel_multiplier=-1).then_inc(S["made"], 1)
                nc.gpsimd.iota(countdown[:], pattern=[[-1, E]], base=E, channel_multiplier=0, **approx).then_inc(S["made"], 1)
                nc.gpsimd.iota(t128[:], pattern=[[P, NT]], base=0, channel_multiplier=0, **approx).then_inc(S["made"], 1)
                nc.gpsimd.iota(token_id[:], pattern=[[P, NT]], base=0, channel_multiplier=1, **approx).then_inc(S["made"], 1)
                nc.gpsimd.iota(col_id[:], pattern=[[1, P]], base=0, channel_multiplier=0, **approx).then_inc(S["made"], 1)
                nc.gpsimd.iota(slot_id[:], pattern=[[1, SLOTS]], base=0, channel_multiplier=0, **approx).then_inc(S["made"], 1)
                nc.gpsimd.iota(spare_row[:], pattern=[[P, SLOTS]], base=top * TOKENS, channel_multiplier=1, **approx).then_inc(S["made"], 1)
                nc.gpsimd.memset(upto[:, :, 0:pad_t, :], 0.0).then_inc(S["made"], 1)
                nc.gpsimd.memset(until[:], 0.0).then_inc(S["made"], 1)
                nc.gpsimd.memset(zero_row[:], 0.0).then_inc(S["made"], 1)
                value_all = value[:].rearrange("p r t -> p (r t)")
                with pool.Fori(0, top * NT // CT // 4) as i:
                    for par in range(4):
                        hold(pool, S["oh_ready"], i * 4 + (par + 1))
                        nc.gpsimd.tensor_tensor(oh_slot[:, par], oh_slot[:, par], bl(value_all[:, bass.ds((i * 4 + par) * CT, CT)], SLOTS), ALU.mult).then_inc(S["ohs_ready"], 1)
                for par in range(2):
                    pool.wait_ge(S[f"xn_stored{par}"], NC_ // 2 * 16)

                def gather(n, par):
                    hold(pool, S["picked"], n + 1)
                    nc.gpsimd.indirect_dma_start(out=xs[:, par, :], out_offset=None, in_=xn_rows[:, :],
                                                 in_offset=bass.IndirectOffsetOnAxis(ap=now[:, par, :], axis=0)).then_inc(S[f"xs_loaded{par}"], 16)

                def scatter(n, par):
                    hold(pool, S["y_copied"], n + 1)
                    nc.gpsimd.indirect_dma_start(out=y_rows[:, :], out_offset=bass.IndirectOffsetOnAxis(ap=then[:, par, :], axis=0),
                                                 in_=ys[:, par, :], in_offset=None).then_inc(S[f"y_stored{par}"], 16)

                for n in range(5):
                    gather(n, n % 2)
                scatter(0, 0)
                with pool.Fori(0, SLOTS // 2 - 3) as i:
                    for par in range(2):
                        gather(i * 2 + (par + 5), 1 - par)
                        scatter(i * 2 + (par + 1), 1 - par)
                gather(SLOTS - 1, 1)
                for n in range(SLOTS - 5, SLOTS):
                    scatter(n, n % 2)

            @block.scalar
            def _(act):
                nc.scalar.activation(std[:], g.MV[:, :, 1], ACT.Sqrt, bias=g.eps[:, 0:1]).then_inc(S["std_ready"], 1)
                with act.Fori(0, NC_ // 2) as i:
                    for par in range(2):
                        act.wait_ge(S["xn_turned"], i * 2 + (par + 1))
                        nc.scalar.activation(xt[:, par, :], ps[:, 4 + par, :], ACT.Copy).then_inc(S["xt_ready"], 1)
                if top == 2:
                    act.wait_ge(S["gap_ready"], 1)
                    nc.scalar.activation(ex[:], wsum[:], ACT.Exp).then_inc(S["ex_ready"], 1)

                def turned_rows(n):
                    act.wait_ge(S["x_turned"], n + 1)
                    nc.scalar.activation(xst[:], ps[:, 6, 0:P], ACT.Copy).then_inc(S["xst_ready"], 1)

                def silu(n, par):
                    act.wait_ge(S["gu_ready"], n + 1)
                    if some(n - 1):
                        act.wait_ge(S["hid_ready"], n - 1)
                    nc.scalar.activation(sg[:, par, :], ps[:, par, :], ACT.Silu).then_inc(S["silu_ready"], 1)

                def turned_hidden(n, par):
                    act.wait_ge(S["h_turned"], n + 1)
                    nc.scalar.activation(hid_t[:, par].rearrange("p j t -> p (j t)"), ps[:, 4 + par, :], ACT.Copy).then_inc(S["ht_ready"], 1)

                turned_rows(0)
                silu(0, 0)
                turned_rows(1)
                with act.Fori(0, SLOTS // 2 - 1) as i:
                    for j in range(2):
                        n = i * 2 + (j + 1)
                        silu(n, 1 - j)
                        turned_rows(n + 1)
                        turned_hidden(n - 1, j)
                silu(SLOTS - 1, 1)
                turned_hidden(SLOTS - 2, 0)
                turned_hidden(SLOTS - 1, 1)
                if top == 2:
                    with act.Fori(0, NC_ // 4) as i:
                        for buf in range(4):
                            act.wait_ge(S[f"y_loaded{buf}"], (i + 1) * (top * 16))
                            for k in range(CT):
                                last = nc.scalar.activation(got[:, buf, 1, k, :], got[:, buf, 1, k, :], ACT.Copy, scale=w_all[:, 1, bass.ds(i * NT // 2 + (buf * CT + k), 1)])
                            last.then_inc(S["weighted"], 1)

            @block.tensor
            def _(pe):
                pe.wait_ge(g.weights_loaded, weights)
                pe.wait_ge(S["made"], 11)

                def turn(c, par):
                    pe.wait_ge(S["xn_ready"], c + 1)
                    if some(c - 1):
                        pe.wait_ge(S["xt_ready"], c - 1)
                    for k in range(CT):
                        last = nc.tensor.transpose(ps[:, 4 + par, k * P:k * P + P], xn[:, par, k, :], g.ident[:])
                    last.then_inc(S["xn_turned"], 1)

                def logits(c, par):
                    pe.wait_ge(S["xt_ready"], c + 1)
                    for k in range(CT):
                        last = nc.tensor.matmul(ps[:, 6, bass.ds(c * (CT * E) + k * E, E)], xt[:, par, k * P:k * P + P], gate_w[:], start=True, stop=True)
                    last.then_inc(S["lg_ready"], 1)

                turn(0, 0)
                turn(1, 1)
                with pe.Fori(0, NC_ // 2 - 1) as i:
                    for par in range(2):
                        logits(i * 2 + par, par)
                        turn(i * 2 + (par + 2), par)
                logits(NC_ - 2, 0)
                logits(NC_ - 1, 1)
                pe.wait_ge(S["hots_ready"], 1)
                nc.tensor.matmul(ps[:, 0, 0:NT * E], earlier[:], hots[:].rearrange("p t e -> p (t e)"), start=True, stop=True)
                nc.tensor.matmul(ps[:, 1, 0:NT * E], g.ones[:], hots[:].rearrange("p t e -> p (t e)"), start=True, stop=True).then_inc(S["ranks_ready"], 1)
                nc.tensor.matmul(ps[:, 2, 0:SLOTS], g.ones[0:1, :], zero_row[:], start=True, stop=False, skip_group_check=True)
                pe.sem_inc(S["oh_used"], 4)
                with pe.Fori(0, top * NT // CT // 4) as i:
                    for par in range(4):
                        pe.wait_ge(S["ohs_ready"], i * 4 + (par + 1))
                        for k in range(CT):
                            last = nc.tensor.matmul(ps[:, 2, 0:SLOTS], oh_row[:, par, k, :], oh_slot[:, par, k, :], start=False, stop=True, skip_group_check=True)
                        last.then_inc(S["oh_used"], 1)

                def turn_rows(n, par, loads):
                    pe.wait_ge(S[f"xs_loaded{par}"], loads)
                    if some(n):
                        pe.wait_ge(S["xst_ready"], n)
                    nc.tensor.transpose(ps[:, 6, 0:P], xs[:, par, :], g.ident[:]).then_inc(S["x_turned"], 1)

                def expert_of(n):
                    return pe.value_load(table_e[0:1, bass.ds(n, 1)], min_val=0, max_val=E - 1)

                def up(n, par, e):
                    pe.wait_ge(S["xst_ready"], n + 1)
                    if some(n - 1):
                        pe.wait_ge(S["hid_ready"], n - 1)
                    nc.tensor.matmul(ps[:, par, :], xst[:], up_g(e), start=True, stop=True)
                    nc.tensor.matmul(ps[:, 2 + par, :], xst[:], up_u(e), start=True, stop=True).then_inc(S["gu_ready"], 1)

                def turn_hidden(n, par):
                    pe.wait_ge(S["hid_ready"], n + 1)
                    for j in range(IB):
                        last = nc.tensor.transpose(ps[:, 4 + par, j * P:j * P + P], hid[:, par, j * P:j * P + P], g.ident[:])
                    last.then_inc(S["h_turned"], 1)

                def rows(n, par, e):
                    pe.wait_ge(S["ht_ready"], n + 1)
                    if some(n):
                        pe.wait_ge(S["y_copied"], n)
                    for j in range(IB):
                        last = nc.tensor.matmul(ps[:, 7, 0:P], hid_t[:, par, j, :], down(e, j), start=(j == 0), stop=(j == IB - 1))
                    last.then_inc(S["y_ready"], 1)

                pe.wait_ge(S["table_ready"], 1)
                turn_rows(0, 0, 16)
                up(0, 0, expert_of(0))
                turn_rows(1, 1, 16)
                up(1, 1, expert_of(1))
                turn_rows(2, 0, 32)
                turn_hidden(0, 0)
                def two_slots(n, pair):
                    e0, e1 = expert_of(n), expert_of(n + 1)
                    up(n, 0, e0)
                    before0, before1 = expert_of(n - 2), expert_of(n - 1)
                    turn_rows(n + 1, 1, pair * 16 + 32)
                    turn_hidden(n - 1, 1)
                    rows(n - 2, 0, before0)
                    up(n + 1, 1, e1)
                    turn_rows(n + 2, 0, pair * 16 + 48)
                    turn_hidden(n, 0)
                    rows(n - 1, 1, before1)

                PAIRS = SLOTS // 2 - 2
                with pe.Fori(0, PAIRS // 4) as i:
                    for j in range(4):
                        two_slots(i * 8 + (j * 2 + 2), i * 4 + j)
                for j in range(PAIRS // 4 * 4, PAIRS):
                    two_slots(j * 2 + 2, j)
                n = SLOTS - 2
                up(n, 0, expert_of(n))
                turn_rows(n + 1, 1, SLOTS // 2 * 16)
                turn_hidden(n - 1, 1)
                rows(n - 2, 0, expert_of(n - 2))
                up(n + 1, 1, expert_of(n + 1))
                turn_hidden(n, 0)
                rows(n - 1, 1, expert_of(n - 1))
                turn_hidden(n + 1, 1)
                rows(n, 0, expert_of(n))
                rows(n + 1, 1, expert_of(n + 1))

            @block.vector
            def _(dve):
                ch = Chain(dve, S["chain"])
                dve.wait_ge(S["std_ready"], 1)
                ch.link(nc.vector.reciprocal(rstd[:], std[:]))

                def rows_of(c, par):
                    for k in range(CT):
                        n = c * CT + k
                        last = nc.vector.tensor_scalar(xn[:, par, k, :], tile_of(g.X, n), tile_of(g.MV, n)[:, 0:1], rstd[:, bass.ds(n, 1)], ALU.subtract, ALU.mult)
                    last.then_inc(S["xn_ready"], 1)

                rows_of(0, 0)
                rows_of(1, 1)
                with dve.Fori(1, NC_ // 2) as i:
                    for par in range(2):
                        hold(dve, S[f"xn_stored{par}"], i * 16)
                        hold(dve, S["xn_turned"], i * 2 + (par - 1))
                        rows_of(i * 2 + par, par)

                dve.wait_ge(S["made"], 11)
                dve.wait_ge(S["lg_ready"], NC_)
                ch.link(nc.vector.tensor_copy(lg[:, 0], ps_l))
                for r in range(top):
                    if r:
                        ch.link(nc.vector.scalar_tensor_tensor(lg[:, 1], hot[:, 0], -3.0e38, lg[:, 0], ALU.mult, ALU.add))
                    ch.link(nc.vector.tensor_reduce(best[:, r], lg[:, r], AX_X, ALU.max))
                    ch.link(nc.vector.tensor_tensor(is_best[:], lg[:, r], bl(best[:, r], E), ALU.is_equal))
                    ch.link(nc.vector.tensor_tensor(is_best[:], is_best[:], bc(countdown[:], NT), ALU.mult))
                    ch.link(nc.vector.tensor_reduce(first[:], is_best[:], AX_X, ALU.max))
                    ch.link(nc.vector.tensor_tensor(hot[:, r], bc(countdown[:], NT), bl(first[:], E), ALU.is_equal))
                if top == 2:
                    nc.vector.tensor_tensor(hots[:], hot[:, 0], hot[:, 1], ALU.add).then_inc(S["hots_ready"], 1)
                    nc.vector.tensor_tensor(wsum[:], best[:, 1], best[:, 0], ALU.subtract).then_inc(S["gap_ready"], 1)
                else:
                    nc.vector.tensor_copy(hots[:], hot[:, 0]).then_inc(S["hots_ready"], 1)

                dve.wait_ge(S["ranks_ready"], 1)
                body = slice(pad_t, pad_t + NT)
                ch.link(nc.vector.tensor_copy(upto[:, 0, body], ps_count))
                side, step = 0, 1
                while step < NT:
                    ch.link(nc.vector.tensor_tensor(upto[:, 1 - side, body], upto[:, side, body], upto[:, side, pad_t - step:pad_t - step + NT], ALU.add))
                    side, step = 1 - side, 2 * step
                total = upto[:, side, pad_t + NT - 1, :]
                ch.link(nc.vector.tensor_tensor(rank[:], upto[:, side, body], ps_count, ALU.subtract))
                ch.link(nc.vector.tensor_tensor(rank[:], rank[:], ps_rank, ALU.add))
                ch.link(nc.vector.tensor_tensor(held[:], bl(total, NT), bc(t128[:], E), ALU.is_gt))
                ch.link(nc.vector.tensor_reduce(tiles[:], held[:], AX_X, ALU.add))
                ch.link(nc.vector.tensor_copy(until[:, 0, 4:4 + E], tiles[:]))
                side, step = 0, 1
                while step < E:
                    ch.link(nc.vector.tensor_tensor(until[:, 1 - side, 4:4 + E], until[:, side, 4:4 + E], until[:, side, 4 - step:4 - step + E], ALU.add))
                    side, step = 1 - side, 2 * step
                done = until[:, side, 4:4 + E]
                ch.link(nc.vector.tensor_tensor(start[:], done, tiles[:], ALU.subtract))
                ch.link(nc.vector.tensor_scalar(start[:], start[:], float(P), None, ALU.mult))
                ch.link(nc.vector.tensor_tensor(rank[:], rank[:], bc(start[:], NT), ALU.add))
                for r in range(top):
                    last = nc.vector.tensor_tensor(place[:, r], hot[:, r], rank[:], ALU.mult)
                ch.link(last)
                ch.link(nc.vector.tensor_reduce(dest[:, 0:top], place[:, 0:top], AX_X, ALU.add))
                ch.link(nc.vector.tensor_scalar(tile_no[:, 0:top], dest[:, 0:top], -63.5, 1.0 / P, ALU.add, ALU.mult))
                ch.link(nc.vector.tensor_scalar(tile_no[:, 0:top], tile_no[:, 0:top], HALF, None, ALU.add))
                ch.link(nc.vector.tensor_scalar(tile_no[:, 0:top], tile_no[:, 0:top], HALF, None, ALU.subtract))
                ch.link(nc.vector.scalar_tensor_tensor(row_no[:, 0:top], tile_no[:, 0:top], -float(P), dest[:, 0:top], ALU.mult, ALU.add))
                for r in range(top):
                    last = nc.vector.scalar_tensor_tensor(value[:, r], token_id[:], float((r - top) * TOKENS), dest[:, r], ALU.add, ALU.subtract)
                last.then_inc(S["values_ready"], 1)
                dve.wait_ge(S["values_ready"], 1)
                row_all, tile_all = (t[:].rearrange("p r t -> p (r t)") for t in (row_no, tile_no))
                with dve.Fori(0, top * NT // CT // 4) as i:
                    for par in range(4):
                        group = bass.ds((i * 4 + par) * CT, CT)
                        hold(dve, S["oh_used"], i * 4 + (par + 1))
                        nc.vector.tensor_tensor(oh_slot[:, par], bc(slot_id[:], CT), bl(tile_all[:, group], SLOTS), ALU.is_equal)
                        nc.vector.tensor_tensor(oh_row[:, par], bc(col_id[:], CT), bl(row_all[:, group], P), ALU.is_equal).then_inc(S["oh_ready"], 1)
                if top == 2:
                    dve.wait_ge(S["ex_ready"], 1)
                    ch.link(nc.vector.tensor_scalar_add(wsum[:], ex[:], 1.0))
                    ch.link(nc.vector.reciprocal(w_all[:, 0, :], wsum[:]))
                    ch.link(nc.vector.tensor_tensor(w_all[:, 1, :], w_all[:, 0, :], ex[:], ALU.mult))
                ch.link(nc.vector.tensor_tensor(past[:], bl(slot_id[0:1, :], E), bc(done[0:1], SLOTS), ALU.is_ge))
                ch.link(nc.vector.tensor_reduce(slot_e[:], past[:], AX_X, ALU.add))
                ch.link(nc.vector.tensor_scalar(table_e[:], slot_e[:], float(E - 1), None, ALU.min))
                dve.wait_ge(S["oh_used"], top * NT // CT + 4)
                ch.link(nc.vector.tensor_tensor(row_at[:], ps[:, 2, 0:SLOTS], spare_row[:], ALU.add))
                ch.link(nc.vector.tensor_scalar(second[:], row_at[:], float(TOKENS), -float((top - 1) * TOKENS), ALU.is_ge, ALU.mult))
                ch.link(nc.vector.tensor_tensor(token[:], row_at[:], second[:], ALU.add))
                ch.link(nc.vector.tensor_scalar(token_at[:], token[:], float(TOKENS - 1), None, ALU.min))
                nc.vector.tensor_copy(result_at[:], row_at[:]).then_inc(S["table_ready"], 1)
                dve.wait_ge(S["table_ready"], 1)

                def pick(n, par):
                    if some(n - 1):
                        hold(dve, S["x_turned"], n - 1)
                    nc.vector.tensor_copy(now[:, par, :], token_at[:, bass.ds(n, 1)]).then_inc(S["picked"], 1)

                def hidden(n, par):
                    dve.wait_ge(S["silu_ready"], n + 1)
                    if some(n - 1):
                        dve.wait_ge(S["h_turned"], n - 1)
                    nc.vector.tensor_tensor(hid[:, par, :], sg[:, par, :], ps[:, 2 + par, :], ALU.mult).then_inc(S["hid_ready"], 1)

                def rows(n, par, stores):
                    dve.wait_ge(S["y_ready"], n + 1)
                    if some(stores):
                        hold(dve, S[f"y_stored{par}"], stores)
                    nc.vector.tensor_copy(then[:, par, :], result_at[:, bass.ds(n, 1)])
                    nc.vector.tensor_copy(ys[:, par, :], ps[:, 7, 0:P]).then_inc(S["y_copied"], 1)

                AHEAD = 3
                for n in range(AHEAD):
                    pick(n, n % 2)
                for n in range(2):
                    hidden(n, n)
                    pick(n + AHEAD, (n + AHEAD) % 2)
                for n in range(2, 4):
                    hidden(n, n % 2)
                    pick(n + AHEAD, (n + AHEAD) % 2)
                    rows(n - 2, n % 2, 0)
                with dve.Fori(1, SLOTS // 2 - 3) as i:
                    for par in range(2):
                        n = i * 2 + par
                        hidden(n + 2, par)
                        pick(n + 5, 1 - par)
                        rows(n, par, i * 16)
                for n in range(SLOTS - 6, SLOTS):
                    if n + 2 < SLOTS:
                        hidden(n + 2, n % 2)
                    if n + 5 < SLOTS:
                        pick(n + 5, (n + 5) % 2)
                    rows(n, n % 2, n // 2 * 16)

                CSTEPS = 1 + top
                with dve.Fori(0, NC_ // 4) as i:
                    ch = Chain(dve, S["combine_chain"], i * CSTEPS)
                    if top == 2:
                        for buf in range(4):
                            dve.wait_ge(S[f"y_loaded{buf}"], (i + 1) * (top * 16))
                            for k in range(CT):
                                x = tile_of(g.X, i * (4 * CT) + (buf * CT + k))
                                last = nc.vector.scalar_tensor_tensor(x, got[:, buf, 0, k, :], w_all[:, 0, bass.ds(i * (4 * CT) + (buf * CT + k), 1)], x,
                                                                      ALU.mult, ALU.add)
                        ch.link(last)
                    for buf in range(4):
                        if top == 2:
                            hold(dve, S["weighted"], i * 4 + (buf + 1))
                        else:
                            dve.wait_ge(S[f"y_loaded{buf}"], (i + 1) * (top * 16))
                        xc = g.X[:, bass.ds(i * (4 * CT) + buf * CT, CT), :]
                        nc.vector.tensor_tensor(xc, got[:, buf, top - 1], xc, ALU.add).then_inc(S["combined"], 1)
                    hold(dve, S["combined"], (i + 1) * 4)
                    for k in range(4 * CT):
                        last = nc.vector.bn_stats(raw[:, k, :], tile_of(g.X, i * (4 * CT) + k))
                    ch.link(last)
                    for k in range(4 * CT):
                        last = nc.vector.bn_aggr(stats[:, k, :], raw[:, k, :])
                    ch.link(last)
                    nc.vector.tensor_copy(g.MV[:, bass.ds(i * (4 * CT), 4 * CT), :], stats[:]).then_inc(S["ready"], 1)
                    hold(dve, S["ready"], i + 1)
        s.clear()


def landmark_layer(nc, g, wq, bq, wk, bk, wv, bv):
    TB = SEQ // P
    LM = 64
    RUN = SEQ // LM
    PER = P // RUN
    WIN = LM - PER
    with ExitStack() as ctx:
        s = Scope(nc, ctx, "lm")
        norm = Norm(nc, g, s)
        w = s.sb("w", [P, 3, P])
        brow = s.sb("brow", [1, 3, P])
        avg = s.sb("avg", [P, WIN + LM])
        xt = s.sb("xt", [P, 2, CHUNK])
        nmx, sums, rs = s.sb("nmx", [P, TB, 2]), s.sb("sums", [P, TB, 2]), s.sb("rs", [P, TB, 2])
        eq, ek = s.sb("eq", [P, 4, P]), s.sb("ek", [P, 4, P])
        kk, k3 = s.sb("kk", [P, 4, P]), s.sb("k3", [P, 4, P])
        bias = s.sb("bias", [P, 3 * P])
        eqt = s.sb("eqt", [P, TB, P])
        lm, mm, aa, nn = s.sb("lm", [LM, P]), s.sb("mm", [P, P]), s.sb("aa", [P, P]), s.sb("nn", [P, P])
        raw = s.sb("raw", [P, CT, 6])
        ps_t, ps_qkv, ps_o = s.ps("ps_t", [P, CT, P]), s.ps("ps_qkv", [P, 4, 512]), s.ps("ps_o", [P, CT, P])
        ps_m, ps_lm = s.ps("ps_m", [P, 512]), s.ps("ps_lm", [P, 512])
        loaded, made, chain, spread = (s.sem(n) for n in ("loaded", "made", "chain", "spread"))
        xn_ready, turned, copied = s.sem("xn_ready"), s.sem("turned"), s.sem("copied")
        qkv_ready, mx_ready, exp_ready = s.sem("qkv_ready"), s.sem("mx_ready"), s.sem("exp_ready")
        k3_ready, acc_done = s.sem("k3_ready"), s.sem("acc_done")
        mm_ready, a_done, a_ready, n_done, n_ready = (s.sem(n) for n in ("mm_ready", "a_done", "a_ready", "n_done", "n_ready"))
        o_ready, x_added = s.sem("o_ready"), s.sem("x_added")
        STEPS = TB * 2 + 6

        def out_bank(h, k):
            return ps_o[:, k, :] if h == 0 else ps_m[:, k * P:k * P + P]

        with nc.Block() as block:
            @block.sync
            def _(sp):
                for i, (m, b) in enumerate(((wq, bq), (wk, bk), (wv, bv))):
                    sp.dma_start(w[:, i, :], m).then_inc(loaded, 16)
                    sp.dma_start(brow[:, i, :], b.rearrange("(a n) -> a n", a=1)).then_inc(loaded, 16)

            @block.gpsimd
            def _(pool):
                nc.gpsimd.memset(avg[:], 1.0 / RUN).then_inc(made, 1)
                pool.wait_ge(made, 1)
                nc.gpsimd.affine_select(out=avg[:], in_=avg[:], compare_op=ALU.is_ge, fill=0.0, base=RUN * WIN,
                                        pattern=[[-RUN, WIN + LM]], channel_multiplier=1).then_inc(made, 1)
                pool.wait_ge(made, 2)
                nc.gpsimd.affine_select(out=avg[:], in_=avg[:], compare_op=ALU.is_ge, fill=0.0, base=RUN - 1 - RUN * WIN,
                                        pattern=[[RUN, WIN + LM]], channel_multiplier=-1).then_inc(made, 1)

            @block.scalar
            def _(act):
                norm.act_std(act)
                def copy_xt(b, h):
                    act.wait_ge(turned, b * 2 + h + 1)
                    nc.scalar.activation(xt[:, h, :], ps_t[:].rearrange("p a b -> p (a b)"), ACT.Copy).then_inc(copied, 1)

                def sequence(b, last):
                    for t in range(TB + 2):
                        n = b * TB + t
                        if t < TB:
                            act.wait_ge(mx_ready, n + 1)
                            act.wait_ge(k3_ready, n + 1)
                            act.wait_ge(acc_done, n + 1)
                            nc.scalar.activation(ek[:, t % 4, :], ps_qkv[:, t % 4, P:2 * P], ACT.Exp, bias=nmx[:, t, 1:2], accum_out=sums[:, t, 1:2])
                            nc.scalar.activation(eq[:, t % 4, :], ps_qkv[:, t % 4, 0:P], ACT.Exp, bias=nmx[:, t, 0:1], accum_out=sums[:, t, 0:1]).then_inc(exp_ready, 1)
                        if t in (5, 9):
                            act.wait_ge(acc_done, n + 3)
                            nc.scalar.activation(eqt[:, t - 5:t - 1, :], ps_t[:], ACT.Copy).then_inc(copied, 1)
                    if not last:
                        copy_xt(b + 1, 0)
                        copy_xt(b + 1, 1)
                copy_xt(0, 0)
                copy_xt(0, 1)
                with act.Fori(0, BATCH - 1) as b:
                    sequence(b, False)
                sequence(BATCH - 1, True)

            @block.tensor
            def _(pe):
                pe.wait_ge(loaded, 16 * 6)
                pe.wait_ge(made, 3)
                pe.sem_inc(acc_done, 4)
                nc.tensor.matmul(ps_lm[:, 0:3 * P], g.ones[0:1, :], brow[:].rearrange("p a b -> p (a b)"), start=True, stop=True).then_inc(spread, 1)
                pe.wait_ge(spread, 2)
                def turn(b, h):
                    pe.wait_ge(xn_ready, b * 2 + h + 1)
                    pe.wait_ge(copied, b * 4 + h + 1)
                    for k in range(CT):
                        t = nc.tensor.transpose(ps_t[:, k, :], norm.xn[:, k, :], g.ident[:])
                    t.then_inc(turned, 1)

                def sequence(b, last):
                    for t in range(TB + 2):
                        n = b * TB + t
                        if t < TB:
                            if t % CT == 0:
                                pe.wait_ge(copied, b * 4 + 2 + t // CT)
                            pe.wait_ge(k3_ready, n + 1)
                            if t >= 4:
                                pe.wait_ge(exp_ready, n - 3)
                            out = ps_qkv[:, t % 4, 0:3 * P]
                            nc.tensor.matmul(out, xt[:, t // CT, t % CT * P:t % CT * P + P], w[:].rearrange("p a b -> p (a b)"),
                                             start=True, stop=True).then_inc(qkv_ready, 1)
                        if t >= 2:
                            r = t - 2
                            pe.wait_ge(k3_ready, n + 3)
                            nc.tensor.matmul(ps_m[:, 0:P], kk[:, r % 4, :], k3[:, r % 4, :], start=(r == 0), stop=(r == TB - 1))
                            nc.tensor.matmul(ps_lm[0:LM, 0:P], avg[:, WIN - PER * r:WIN - PER * r + LM], kk[:, r % 4, :],
                                             start=(r == 0), stop=(r == TB - 1))
                            pe.wait_ge(exp_ready, n - 1)
                            if r % 4 == 0:
                                pe.wait_ge(copied, b * 4 + 3 + r // 4)
                            nc.tensor.transpose(ps_t[:, r % 4, :], eq[:, r % 4, :], g.ident[:]).then_inc(acc_done, 1)
                    pe.wait_ge(mm_ready, b + 1)
                    nc.tensor.matmul(ps_o[:, 0, :], lm[:], lm[:], start=True, stop=True).then_inc(a_done, 1)
                    if not last:
                        turn(b + 1, 0)
                    pe.wait_ge(a_ready, b + 1)
                    nc.tensor.matmul(ps_o[:, 1, :], aa[:], mm[:], start=True, stop=True).then_inc(n_done, 1)
                    pe.wait_ge(n_ready, b + 1)
                    pe.wait_ge(copied, b * 4 + 5)
                    for h in range(2):
                        for k in range(CT):
                            o = nc.tensor.matmul(out_bank(h, k), eqt[:, h * CT + k, :], nn[:], start=True, stop=True)
                        o.then_inc(o_ready, 1)
                    if not last:
                        turn(b + 1, 1)
                turn(0, 0)
                turn(0, 1)
                with pe.Fori(0, BATCH - 1) as b:
                    sequence(b, False)
                sequence(BATCH - 1, True)

            @block.vector
            def _(dve):
                norm.dve_rstd(dve)
                dve.sem_inc(k3_ready, 4)
                dve.sem_inc(copied, 1)
                dve.wait_ge(spread, 1)
                nc.vector.tensor_copy(bias[:], ps_lm[:, 0:3 * P]).then_inc(spread, 1)
                def normalise(b, h):
                    if h:
                        dve.wait_ge(turned, b * 2 + 1)
                    norm.dve_rows(b * 2 + h).then_inc(xn_ready, 1)

                def sequence(b, last):
                    ch = Chain(dve, chain, b * STEPS)
                    for t in range(TB + 1):
                        n = b * TB + t
                        if t < TB:
                            dve.wait_ge(qkv_ready, n + 1)
                            out = ps_qkv[:, t % 4, 0:3 * P]
                            ch.link(nc.vector.tensor_tensor(out, out, bias[:], ALU.add))
                            nc.vector.tensor_reduce(nmx[:, t, :], ps_qkv[:, t % 4, 0:2 * P].rearrange("p (a b) -> p a b", a=2),
                                                    AX_X, ALU.max, negate=True).then_inc(mx_ready, 1)
                        if t >= 1:
                            r = t - 1
                            dve.wait_ge(exp_ready, n)
                            ch.link(nc.vector.reciprocal(rs[:, r, :], sums[:, r, :]))
                            dve.wait_ge(acc_done, n)
                            nc.vector.tensor_scalar(kk[:, r % 4, :], ek[:, r % 4, :], rs[:, r, 1:2], None, ALU.mult)
                            nc.vector.scalar_tensor_tensor(k3[:, r % 4, :], ek[:, r % 4, :], rs[:, r, 1:2], ps_qkv[:, r % 4, 2 * P:3 * P],
                                                           ALU.mult, ALU.mult).then_inc(k3_ready, 1)
                    dve.wait_ge(acc_done, b * TB + TB + 4)
                    nc.vector.tensor_copy(lm[:], ps_lm[0:LM, 0:P])
                    nc.vector.tensor_copy(mm[:], ps_m[:, 0:P]).then_inc(mm_ready, 1)
                    if not last:
                        normalise(b + 1, 0)
                    dve.wait_ge(a_done, b + 1)
                    nc.vector.tensor_copy(aa[:], ps_o[:, 0, :]).then_inc(a_ready, 1)
                    dve.wait_ge(n_done, b + 1)
                    nc.vector.tensor_copy(nn[:], ps_o[:, 1, :]).then_inc(n_ready, 1)
                    for h in range(2):
                        c = b * 2 + h
                        dve.wait_ge(o_ready, c + 1)
                        for k in range(CT):
                            t = h * CT + k
                            xk = tile_of(g.X, b * TB + t)
                            add = nc.vector.scalar_tensor_tensor(xk, out_bank(h, k), rs[:, t, 0:1], xk, ALU.mult, ALU.add)
                        add.then_inc(x_added, 1)
                    if not last:
                        normalise(b + 1, 1)
                    hold(dve, x_added, b * 2 + 2)
                    for h in range(2):
                        ch.link(dve_new_stats(nc, dve, g, raw, b * 2 + h, ch))
                    assert ch.n == STEPS, ch.n
                normalise(0, 0)
                normalise(0, 1)
                with dve.Fori(0, BATCH - 1) as b:
                    sequence(b, False)
                sequence(BATCH - 1, True)
        s.clear()


def causal_layer(nc, g, wq, bq, wk, bk, wv, bv, wp, bp, table, wq_sw, bq_sw, wk_sw, bk_sw, rope, onehot):
    H, D = 16, 8
    TB = SEQ // P
    NP = 3
    KD = NP * NP * D
    KM = KD + NP
    G4 = 4
    NG = H // G4
    SCALE = 1.0 / D ** 0.5
    NEG = -1.0e30
    W2 = 2 * P
    blocks = [(q4, kt) for q4 in range(2) for kt in range(4 * q4 + 4)]
    NS = NG * len(blocks) * G4
    BF = mybir.dt.bfloat16

    def span(q4, kt):
        lo, hi = max(kt * P, q4 * CHUNK), q4 * CHUNK + CHUNK
        return lo, min(max(kt * P + W2, lo), hi), hi

    near_of, last_of = {}, []
    i = 0
    for _ in range(NG):
        for q4, kt in blocks:
            for _ in range(G4):
                if span(q4, kt)[0] < span(q4, kt)[1]:
                    near_of[i] = len(near_of)
                i += 1
            if kt == 4 * q4 + 3:
                last_of.append(i - 1)
    NN = len(near_of)
    STEPS = 3 + 2 * NG + 2 * 4

    with ExitStack() as ctx:
        s = Scope(nc, ctx, "ca")
        norm = Norm(nc, g, s)
        w = s.sb("w", [P, 6, P])
        bcol = s.sb("bcol", [P, 4])
        brow = s.sb("brow", [1, 2, CT, P])
        cs = s.sb("cs", [P, 2, SEQ])
        bias_q = s.sb("bias_q", [P, H, W2])
        bias_k = s.sb("bias_k", [P, H, W2])
        xt = s.sb("xt", [P, 2, CHUNK])
        full = s.sb("full", [P, 2, SEQ])
        piece = s.sb("piece", [P, 2, NP, SEQ], BF)
        qst, kst = s.sb("qst", [KM, H, SEQ], BF), s.sb("kst", [KM, H, SEQ], BF)
        vp = s.sb("vp", [P, TB, H, D + 1])
        m_near, m_far, m_all = s.sb("m_near", [P, H * TB]), s.sb("m_far", [P, H * TB]), s.sb("m_all", [P, H * TB])
        m_rest, m_piece = s.sb("m_rest", [P, P]), s.sb("m_piece", [P, NP, P], BF)
        pt = s.sb("pt", [P, 8, CHUNK])
        t1, t2 = pt[:, 0:2, :], pt[:, 2:4, :]
        near = pt[:, 4:6, :].rearrange("p a (b n) -> p (a b) n", b=2)
        ysb, yrs = norm.xn[:].rearrange("p a b -> p (a b)"), s.sb("yrs", [P, CT, G4])
        yy = s.sb("yy", [P, TB, P])
        zero_row = xt[0:1, 0, :]
        raw = s.sb("raw", [P, CT, 6])
        ps = s.ps("ps", [P, 8, 512])
        dram_bias = nc.dram_tensor("scratch_bias", (2, H, 384), F32).ap()
        dram_toeplitz = nc.dram_tensor("scratch_toeplitz", (2, H, P, W2), F32).ap()
        dram_piece = nc.dram_tensor("scratch_piece", (2, NP, P, SEQ), BF).ap()
        dram_max = nc.dram_tensor("scratch_max", (NP, H * TB, P), BF).ap()

        loaded, bias_made, bias_stored, bias_loaded = (s.sem(n) for n in ("loaded", "bias_made", "bias_stored", "bias_loaded"))
        filled, buckets_ready, bias_ready = s.sem("filled"), s.sem("buckets_ready"), s.sem("bias_ready")
        chain = s.sem("chain")
        xn_ready, turned, xt_ready = s.sem("xn_ready"), s.sem("turned"), s.sem("xt_ready")
        proj_ready, proj_used, v_ready, v_used = (s.sem(n) for n in ("proj_ready", "proj_used", "v_ready", "v_used"))
        full_ready, piece1, rest1, piece2, piece3 = (s.sem(n) for n in ("full_ready", "piece1", "rest1", "piece2", "piece3"))
        pieces_stored, stacks_loaded = s.sem("pieces_stored"), s.sem("stacks_loaded")
        sq_ready, sq_used = s.sem("sq_ready"), s.sem("sq_used")
        m_ready, mt_ready, mp_ready, mp_stored, mp_loaded = (s.sem(n) for n in ("m_ready", "mt_ready", "mp_ready", "mp_stored", "mp_loaded"))
        st_ready, near_ready, p_ready, pv_done = (s.sem(n) for n in ("st_ready", "near_ready", "p_ready", "pv_done"))
        y_copied, yt_ready, yy_ready = (s.sem(n) for n in ("y_copied", "yt_ready", "yy_ready"))
        t_ready, t_copied, o_ready = (s.sem(n) for n in ("t_ready", "t_copied", "o_ready"))
        YB = NG * 2

        with nc.Block() as block:
            @block.sync
            def _(sp):
                for i, m in enumerate((wq, wq_sw, wk, wk_sw, wv, wp)):
                    sp.dma_start(w[:, i, :], m).then_inc(loaded, 16)
                for i, m in enumerate((bq, bq_sw, bk, bk_sw)):
                    sp.dma_start(bcol[:, i:i + 1], m.rearrange("(p a) -> p a", a=1)).then_inc(loaded, 16)
                for i, m in enumerate((bv, bp)):
                    for k in range(CT):
                        sp.dma_start(brow[:, i, k, :], m.rearrange("(a n) -> a n", a=1)).then_inc(loaded, 16)
                sp.dma_start(cs[:], rope).then_inc(loaded, 16)
                sp.dma_start(m_near[0:32, 0:H], table).then_inc(loaded, 16)
                sp.dma_start(near[0:33, 0:3, :].rearrange("p a b -> p (a b)"), onehot).then_inc(loaded, 16)
                sp.wait_ge(bias_made, 2)
                sp.dma_start(dram_bias.rearrange("a h n -> h a n"), full[0:H, :, 0:384]).then_inc(bias_stored, 16)
                sp.wait_ge(bias_stored, 16)
                for side, offset in ((1, P - 1), (0, P)):
                    sp.dma_start(dram_toeplitz[side], bass.AP(dram_bias.tensor, side * H * 384 + offset, [[384, H], [-1, P], [1, W2]])).then_inc(bias_stored, 16)
                sp.wait_ge(bias_stored, 48)
                for bias, side in ((bias_q, 1), (bias_k, 0)):
                    sp.dma_start(bias[:], dram_toeplitz[side].rearrange("h p w -> p h w")).then_inc(bias_loaded, 16)

                def store_pieces(b):
                    for side in range(2):
                        hold(sp, piece3, b * 2 + side + 1)
                        sp.dma_start(dram_piece[side].rearrange("n p t -> p n t"), piece[:, side]).then_inc(pieces_stored, 16)

                def stacks(b, more=True):
                    hold(sp, pieces_stored, b * 32 + 32)
                    if some(b):
                        hold(sp, st_ready, b * NS)
                    for side in range(2):
                        for a in range(NP):
                            for c in range(NP):
                                r = (a * NP + c) * D
                                dst = (qst, kst)[side]
                                src = dram_piece[side, (a, c)[side]].rearrange("(h d) t -> d h t", d=D)
                                sp.dma_start(dst[r:r + D], src).then_inc(stacks_loaded, 16)
                    hold(sp, stacks_loaded, b * 288 + 288)
                    hold(sp, mp_ready, b + 1)
                    sp.dma_start(dram_max.rearrange("n p t -> p n t"), m_piece[:]).then_inc(mp_stored, 16)
                    hold(sp, mp_stored, b * 16 + 16)
                    sp.dma_start(qst[KD:KM].rearrange("p h t -> p (h t)"), dram_max.rearrange("n p t -> n (p t)")).then_inc(mp_loaded, 16)
                    hold(sp, mp_loaded, b * 16 + 16)
                    if more:
                        store_pieces(b + 1)

                store_pieces(0)
                with sp.Fori(0, BATCH - 1) as b:
                    stacks(b)
                stacks(BATCH - 1, more=False)

            @block.gpsimd
            def _(pool):
                nc.gpsimd.memset(vp[:, :, :, D:D + 1], 1.0).then_inc(filled, 1)
                pool.wait_ge(filled, 1)
                nc.gpsimd.memset(zero_row, 0.0).then_inc(filled, 1)
                pool.wait_ge(filled, 2)
                nc.gpsimd.memset(m_near[32:33, 0:H], 1.0).then_inc(filled, 1)
                pool.wait_ge(filled, 3)
                nc.gpsimd.memset(m_far[:], NEG).then_inc(filled, 1)
                pool.wait_ge(filled, 4)
                nc.gpsimd.memset(kst[64:KM], 1.0).then_inc(filled, 1)

            @block.scalar
            def _(act):
                norm.act_std(act)
                act.sem_inc(p_ready, 4)
                act.wait_ge(bias_ready, 1)

                def prepare(b):
                    for h in range(2):
                        act.wait_ge(turned, b * 2 + h + 1)
                        nc.scalar.activation(xt[:, h, :], ps[:, 4, :], ACT.Copy).then_inc(xt_ready, 1)
                    act.wait_ge(full_ready, b * 2 + 2)
                    if some(b):
                        act.wait_ge(pieces_stored, b * 32)
                    for side in range(2):
                        nc.scalar.activation(piece[:, side, 0, :], full[:, side], ACT.Copy).then_inc(piece1, 1)
                    for side in range(2):
                        act.wait_ge(rest1, b * 2 + side + 1)
                        nc.scalar.activation(piece[:, side, 1, :], full[:, side], ACT.Copy).then_inc(piece2, 1)

                def sequence(b, more=True):
                    if more:
                        prepare(b + 1)

                    def copy_y(n):
                        act.wait_ge(pv_done, b * NS + last_of[n] + 9)
                        nc.scalar.activation(ysb, ps[:, 6, :], ACT.Copy).then_inc(y_copied, 1)

                    i = 0
                    for gr in range(NG):
                        for q4, kt in blocks:
                            lo, mid, hi = span(q4, kt)
                            c0 = q4 * CHUNK
                            for j in range(G4):
                                act.wait_ge(st_ready, b * NS + i + 1)
                                act.wait_ge(pv_done, b * NS + i + 1)
                                out, src = pt[:, i % 8, :], ps[:, i % 6, :]
                                if lo < mid:
                                    act.wait_ge(near_ready, b * NN + near_of[i] + 1)
                                nc.scalar.activation(out[:, lo - c0:hi - c0], src[:, lo - c0:hi - c0], ACT.Exp, scale=SCALE).then_inc(p_ready, 1)
                                i += 1
                            if kt == 0 and (gr, q4) != (0, 0):
                                copy_y(gr * 2 + q4 - 1)
                    copy_y(YB - 1)
                    for h in range(2):
                        act.wait_ge(t_ready, b * 2 + h + 1)
                        nc.scalar.activation(pt[:, h, :], ps[:, h, :], ACT.Copy).then_inc(t_copied, 1)

                prepare(0)
                with act.Fori(0, BATCH - 1) as b:
                    sequence(b)
                sequence(BATCH - 1, more=False)

            @block.tensor
            def _(pe):
                pe.wait_ge(loaded, 16 * 21)
                pe.wait_ge(filled, 5)
                for a in range(2):
                    nc.tensor.matmul(ps[0:H, a, 0:384], m_near[0:33, 0:H],
                                     near[0:33, 0:3, :].rearrange("p a b -> p (a b)")[:, a * 384:a * 384 + 384],
                                     start=True, stop=True).then_inc(buckets_ready, 1)
                nc.tensor.matmul(ps[:, 6, :], g.ones[0:1, :], zero_row, start=True, stop=True)
                pe.sem_inc(pv_done, 8)
                pe.wait_ge(bias_ready, 1)

                def prepare(b):
                    for h in range(2):
                        pe.wait_ge(xn_ready, b * 2 + h + 1)
                        if h:
                            pe.wait_ge(xt_ready, b * 2 + 1)
                        for k in range(CT):
                            last = nc.tensor.transpose(ps[:, 4, k * P:k * P + P], norm.xn[:, k, :], g.ident[:])
                        last.then_inc(turned, 1)
                    for h in range(2):
                        n = b * 2 + h
                        pe.wait_ge(xt_ready, n + 1)
                        pe.wait_ge(proj_used, n + 1)
                        for i in range(4):
                            last = nc.tensor.matmul(ps[:, i, :], w[:, i, :], xt[:, h, :], start=True, stop=True)
                        last.then_inc(proj_ready, 1)
                    pe.wait_ge(proj_used, b * 2 + 3)

                def sequence(b, more=True):
                    for h in range(2):
                        pe.wait_ge(v_used, b * 2 + h + 1)
                        nc.tensor.matmul(ps[:, 5, :], g.ones[0:1, :], brow[:, 0].rearrange("p a b -> p (a b)"), start=True, stop=False, skip_group_check=True)
                        for k in range(CT):
                            last = nc.tensor.matmul(ps[:, 5, k * P:k * P + P], xt[:, h, k * P:k * P + P], w[:, 4, :], start=False, stop=True, skip_group_check=True)
                        last.then_inc(v_ready, 1)

                    pe.wait_ge(v_used, b * 2 + 3)
                    pe.wait_ge(stacks_loaded, b * 288 + 288)
                    for h in range(H):
                        for qt in range(TB):
                            i = h * TB + qt
                            pe.wait_ge(sq_used, b * H * TB + i + 1)
                            r = 2 * (i % 3)
                            end = (qt + 1) * P
                            for c in range(0, end, 512):
                                e = min(c + 512, end)
                                last = nc.tensor.matmul(ps[:, r + c // 512, 0:e - c], qst[0:KD, h, qt * P:qt * P + P], kst[0:KD, h, c:e], start=True, stop=True)
                            last.then_inc(sq_ready, 1)
                    pe.wait_ge(m_ready, b + 1)
                    nc.tensor.transpose(ps[:, 7, 0:P], m_all[:], g.ident[:]).then_inc(mt_ready, 1)
                    if more:
                        prepare(b + 1)
                    pe.wait_ge(mp_loaded, b * 16 + 16)

                    def products(gr, q4, kt, i):
                        lo, _, hi = span(q4, kt)
                        c0 = q4 * CHUNK
                        if kt == 0:
                            pe.wait_ge(y_copied, b * YB + gr * 2 + q4 + 1)
                        for j in range(G4):
                            pe.wait_ge(p_ready, b * NS + i + j + 5)
                            nc.tensor.matmul(ps[32 * j:32 * j + D + 1, 6, lo - c0:hi - c0], vp[:, kt, gr * G4 + j, :], pt[:, (i + j) % 8, lo - c0:hi - c0],
                                             start=(kt == 0), stop=(kt == 4 * q4 + 3), skip_group_check=True).then_inc(pv_done, 1)

                    def turn_y(n):
                        pe.wait_ge(y_copied, b * YB + n + 2)
                        pe.wait_ge(yy_ready, b * YB + n + 1)
                        for k in range(CT):
                            last = nc.tensor.transpose(ps[:, 7, k * P:k * P + P], ysb[:, k * P:k * P + P], g.ident[:])
                        last.then_inc(yt_ready, 1)

                    i = 0
                    before = None
                    for gr in range(NG):
                        for q4, kt in blocks:
                            lo, _, hi = span(q4, kt)
                            c0 = q4 * CHUNK
                            for j in range(G4):
                                if i + j >= 6:
                                    pe.wait_ge(p_ready, b * NS + i + j - 1)
                                nc.tensor.matmul(ps[:, (i + j) % 6, lo - c0:hi - c0], kst[:, gr * G4 + j, kt * P:kt * P + P], qst[:, gr * G4 + j, lo:hi],
                                                 start=True, stop=True).then_inc(st_ready, 1)
                            if before:
                                products(*before)
                            if kt == 3 and (gr, q4) != (0, 0):
                                turn_y(gr * 2 + q4 - 1)
                            before = (gr, q4, kt, i)
                            i += G4
                    products(*before)
                    turn_y(YB - 1)
                    for h in range(2):
                        pe.wait_ge(yy_ready, b * YB + YB + 1)
                        pe.wait_ge(p_ready, b * NS + NS + 4)
                        for k in range(CT):
                            last = nc.tensor.transpose(ps[:, h, k * P:k * P + P], yy[:, h * CT + k, :], g.ident[:])
                        last.then_inc(t_ready, 1)
                    for h in range(2):
                        pe.wait_ge(t_copied, b * 2 + h + 1)
                        nc.tensor.matmul(ps[:, 2 + h, :], g.ones[0:1, :], brow[:, 1].rearrange("p a b -> p (a b)"), start=True, stop=False, skip_group_check=True)
                        for k in range(CT):
                            last = nc.tensor.matmul(ps[:, 2 + h, k * P:k * P + P], pt[:, h, k * P:k * P + P], w[:, 5, :], start=False, stop=True, skip_group_check=True)
                        last.then_inc(o_ready, 1)

                prepare(0)
                with pe.Fori(0, BATCH - 1) as b:
                    sequence(b)
                sequence(BATCH - 1, more=False)

            @block.vector
            def _(dve):
                norm.dve_rstd(dve)
                dve.wait_ge(buckets_ready, 2)
                dve.wait_ge(filled, 4)
                nc.vector.tensor_copy(full[0:H, 0, 0:384], ps[0:H, 0, 0:384]).then_inc(bias_made, 1)
                nc.vector.tensor_copy(full[0:H, 1, 0:384], ps[0:H, 1, 0:384]).then_inc(bias_made, 1)
                dve.sem_inc(proj_used, 1)
                dve.sem_inc(v_used, 1)
                dve.sem_inc(sq_used, 3)
                dve.sem_inc(y_copied, 1)
                dve.sem_inc(yy_ready, 1)
                dve.wait_ge(bias_loaded, 32)
                dve.sem_inc(bias_ready, 2)

                def prepare(b):
                    for h in range(2):
                        if h:
                            dve.wait_ge(turned, b * 2 + 1)
                        norm.dve_rows(b * 2 + h).then_inc(xn_ready, 1)
                    for h in range(2):
                        n = b * 2 + h
                        tt = slice(h * CHUNK, h * CHUNK + CHUNK)
                        dve.wait_ge(proj_ready, n + 1)
                        for side in range(2):
                            i = 2 * side
                            nc.vector.scalar_tensor_tensor(t1[:, side], ps[:, i, :], bcol[:, i:i + 1], cs[:, 0, tt], ALU.add, ALU.mult)
                            last = nc.vector.scalar_tensor_tensor(t2[:, side], ps[:, i + 1, :], bcol[:, i + 1:i + 2], cs[:, 1, tt], ALU.add, ALU.mult)
                        last.then_inc(proj_used, 1)
                        dve.wait_ge(proj_used, n + 2)
                        nc.vector.tensor_tensor(full[:, :, tt], t1, t2, ALU.add).then_inc(full_ready, 1)
                        dve.wait_ge(full_ready, n + 1)
                    for side in range(2):
                        dve.wait_ge(piece1, b * 2 + side + 1)
                        nc.vector.tensor_tensor(full[:, side], full[:, side], piece[:, side, 0, :], ALU.subtract).then_inc(rest1, 1)
                    for side in range(2):
                        dve.wait_ge(piece2, b * 2 + side + 1)
                        nc.vector.tensor_tensor(piece[:, side, 2, :], full[:, side], piece[:, side, 1, :], ALU.subtract).then_inc(piece3, 1)

                def sequence(b, more=True):
                    ch = Chain(dve, chain, b * STEPS)
                    for h in range(2):
                        dve.wait_ge(v_ready, b * 2 + h + 1)
                        nc.vector.tensor_copy(vp[:, h * CT:h * CT + CT, :, 0:D], ps[:, 5, :].rearrange("p (t h d) -> p t h d", t=CT, d=D)).then_inc(v_used, 1)

                    for h in range(H):
                        for qt in range(TB):
                            i = h * TB + qt
                            hold(dve, sq_ready, b * H * TB + i + 1)
                            r = 2 * (i % 3)
                            rows = ps[:, r:r + 2, :].rearrange("p a b -> p (a b)")
                            lo = max(qt - 1, 0) * P
                            hi = qt * P + P
                            if lo:
                                nc.vector.tensor_reduce(m_far[:, i:i + 1], rows[:, 0:lo], AX_X, ALU.max)
                            nc.vector.tensor_tensor_reduce(near[:, i % 4, 0:hi - lo], rows[:, lo:hi], bias_q[:, h, W2 - (hi - lo):W2], 1.0, NEG,
                                                           ALU.add, ALU.max, m_near[:, i:i + 1]).then_inc(sq_used, 1)
                    dve.wait_ge(sq_used, b * H * TB + H * TB + 3)
                    nc.vector.tensor_tensor(m_all[:], m_near[:], m_far[:], ALU.max).then_inc(m_ready, 1)
                    dve.wait_ge(mt_ready, b + 1)
                    ch.link(nc.vector.tensor_scalar(m_piece[:, 0, :], ps[:, 7, 0:P], -1.0, None, ALU.mult))
                    ch.link(nc.vector.scalar_tensor_tensor(m_rest[:], ps[:, 7, 0:P], -1.0, m_piece[:, 0, :], ALU.mult, ALU.subtract))
                    ch.link(nc.vector.tensor_copy(m_piece[:, 1, :], m_rest[:]))
                    nc.vector.tensor_tensor(m_piece[:, 2, :], m_rest[:], m_piece[:, 1, :], ALU.subtract).then_inc(mp_ready, 1)
                    if more:
                        prepare(b + 1)

                    def norm_y(n):
                        gr, q4 = n // 2, n % 2
                        dve.wait_ge(yt_ready, b * YB + n + 1)
                        turned_y = ps[:, 7, :].rearrange("p (t j d) -> p t j d", t=CT, j=G4)
                        ch.link(nc.vector.reciprocal(yrs[:], turned_y[:, :, :, D]))
                        nc.vector.tensor_tensor(yy[:, q4 * CT:q4 * CT + CT, gr * G4 * D:gr * G4 * D + G4 * D].rearrange("p t (j d) -> p t j d", d=D),
                                                turned_y[:, :, :, 0:D], yrs[:].unsqueeze(3).to_broadcast([P, CT, G4, D]), ALU.mult).then_inc(yy_ready, 1)

                    i = 0
                    for gr in range(NG):
                        for q4, kt in blocks:
                            lo, mid, hi = span(q4, kt)
                            c0 = q4 * CHUNK
                            for j in range(G4):
                                if lo < mid:
                                    dve.wait_ge(st_ready, b * NS + i + 1)
                                    nc.vector.tensor_tensor(ps[:, i % 6, lo - c0:mid - c0], ps[:, i % 6, lo - c0:mid - c0],
                                                            bias_k[:, gr * G4 + j, lo - kt * P:mid - kt * P], ALU.add).then_inc(near_ready, 1)
                                i += 1
                            if kt == 3 and (gr, q4) != (0, 0):
                                norm_y(gr * 2 + q4 - 1)
                    norm_y(YB - 1)
                    for h in range(2):
                        c = b * 2 + h
                        dve.wait_ge(o_ready, c + 1)
                        xc = g.X[:, bass.ds(c * CT, CT), :]
                        ch.link(nc.vector.tensor_tensor(xc, ps[:, 2 + h, :].rearrange("p (t d) -> p t d", t=CT), xc, ALU.add))
                        ch.link(dve_new_stats(nc, dve, g, raw, c, ch))
                    assert ch.n == STEPS, ch.n

                prepare(0)
                with dve.Fori(0, BATCH - 1) as b:
                    sequence(b)
                sequence(BATCH - 1, more=False)
        s.clear()


def memory_layer(nc, g, wq, wq_sw, wk, wk_sw, wv, w_out, ln_g, ln_b, mem_beta, rope):
    H, D, SEG = 16, 64, 32
    W = SEQ // SEG
    QH = 4
    NQ = H // QH
    PB = QH // 2
    SCALE = D ** -0.5
    E1 = D + 1
    STEPS = NQ * 8
    with ExitStack() as ctx:
        s = Scope(nc, ctx, "im")
        norm = Norm(nc, g, s)
        w4 = s.sb("w4", [P, 4, H // 2, P])
        wv_s = s.sb("wv", [P, H * D])
        wo = s.sb("wo", [P, H // 2, P])
        lncol = s.sb("lncol", [P, 2])
        cs = s.sb("cs", [P, 2, SEG])
        mask = s.sb("mask", [P, SEG])
        gate = s.sb("gate", [P, 3, H])
        XT = s.sb("xt_all", [P, W, BATCH * SEG])
        xw = s.sb("xw", [P, P])
        ee, rr = s.sb("ee", [P, 4 * P]), s.sb("rr", [P, 4 * P])
        t1, t2 = s.sb("t1", [P, 4 * P]), s.sb("t2", [P, 4 * P])
        rope_qk = s.sb("rope_qk", [P, 2, 2 * PB, P])
        el = s.sb("el", [P, 2, 2 * PB, P])
        mem = s.sb("mem", [P, NQ, PB, BATCH, E1])
        zinc = s.sb("zinc", [P, NQ, PB, BATCH])
        vt = s.sb("vt", [P, NQ, QH, D])
        skt = s.sb("skt", [P, NQ, PB, P])
        u1, uu = s.sb("u1", [P, QH, D]), s.sb("uu", [P, 2, QH, D])
        rd = s.sb("rd", [P, QH])
        s1, s2 = s.sb("s1", [P, QH, SEG]), s.sb("s2", [P, QH, SEG])
        pe_, pt = s.sb("pe_", [P, QH, SEG]), s.sb("pt", [P, 2, QH, SEG])
        uu_e, pt_e = s.sb("uu_e", [P, 2, QH, BATCH, D]), s.sb("pt_e", [P, 2, QH, BATCH, SEG])
        own = s.sb("own", [P, BATCH, SEG])
        mx, sm, rs = s.sb("mx", [P, QH]), s.sb("sm", [P, 2, QH]), s.sb("rs", [P, QH])
        dn = s.sb("dn", [P, QH])
        m1, m2 = s.sb("m1", [P, 2, QH, D]), s.sb("m2", [P, QH, D])
        oo = s.sb("oo", [P, H * D])
        ot = s.sb("ot", [P, H // 2, P])
        raw = s.sb("raw", [P, CT, 6])
        b_a, b_s, b_v, b_sc, b_pv, b_pr, b_nu, b_up = (s.ps(n, [P, 512]) for n in ("b_a", "b_s", "b_v", "b_sc", "b_pv", "b_pr", "b_nu", "b_up"))

        names = ("loaded", "made", "g_ready", "setup", "chain", "xn_ready", "turned", "xt_ready", "xw_ready", "proj_ready", "v_ready",
                 "er_ready", "v_copied", "ab_used", "el_ready", "rope_ready", "sk_turned", "sk_copied", "prev_ready", "num_ready", "s_ready",
                 "s1_ready", "s2_ready", "p_ready", "pt_ready", "u_ready", "m1_ready", "pv_ready", "upd_ready", "m2_ready",
                 "mem_ready", "prev_even", "s_even", "num_even", "ue_ready", "pte_ready", "o_ready", "ot_ready", "ot_copied", "out_ready", "x_ready", "stats")
        S = {n: s.sem(n) for n in names}

        def score_view(ap):
            return ap[:, 0:QH * SEG].rearrange("p (h k) -> p h k", h=QH)

        def head_view(ap, width):
            return ap[:, 0:QH * width].rearrange("p (h d) -> p h d", h=QH)

        def segment(w, project, recall, update, turn, add, first=False, last=False):
            for slot in range(NQ):
                k = w * NQ + slot
                if slot != 2 and not last:
                    project(w, slot, k)
                if not (first and slot < 1 or last and slot > 0):
                    recall(w, (slot - 1) % NQ, k - 1)
                if slot == 2 and not first:
                    turn(w)
                if not (first and slot < 2 or last and slot > 1):
                    update(w, (slot - 2) % NQ, k - 2)
                if slot == 2 and not last:
                    project(w, slot, k)
                if slot == 2 and not first:
                    add(w)

        def idle(*_):
            pass

        with nc.Block() as block:
            @block.sync
            def _(sp):
                for i, m in enumerate((wq, wq_sw, wk, wk_sw)):
                    sp.dma_start(w4[:, i], m.rearrange("d (n f) -> d n f", f=P)).then_inc(S["loaded"], 16)
                sp.dma_start(wv_s[:], wv).then_inc(S["loaded"], 16)
                sp.dma_start(wo[:], w_out.rearrange("(n f) d -> f n d", f=P)).then_inc(S["loaded"], 16)
                sp.dma_start(lncol[:, 0:1], ln_g.rearrange("(p a) -> p a", a=1)).then_inc(S["loaded"], 16)
                sp.dma_start(lncol[:, 1:2], ln_b.rearrange("(p a) -> p a", a=1)).then_inc(S["loaded"], 16)
                sp.dma_start(cs[:], rope).then_inc(S["loaded"], 16)
                sp.dma_start(gate[:, 0, :], mem_beta.rearrange("a h b c -> (a h b c)").partition_broadcast(P)).then_inc(S["loaded"], 16)

            @block.gpsimd
            def _(pool):
                nc.gpsimd.memset(mask[:], 0.0).then_inc(S["made"], 1)
                for b in range(BATCH):
                    pool.wait_ge(S["made"], b + 1)
                    nc.gpsimd.affine_select(out=mask[32 * b:32 * b + 32, :], in_=mask[32 * b:32 * b + 32, :], compare_op=ALU.is_ge, fill=-1.0e30,
                                            base=0, pattern=[[-1, SEG]], channel_multiplier=1).then_inc(S["made"], 1)
                pool.wait_ge(S["made"], 5)
                nc.gpsimd.memset(mem[:], 0.0).then_inc(S["made"], 1)
                pool.wait_ge(S["made"], 6)
                nc.gpsimd.memset(mem[:, :, :, :, D], 1.0e-6).then_inc(S["made"], 1)
                nc.gpsimd.memset(uu_e[:], 0.0).then_inc(S["made"], 1)
                nc.gpsimd.memset(own[:], 0.0).then_inc(S["made"], 1)
                for b in range(BATCH):
                    pool.wait_ge(S["made"], 9 + b)
                    nc.gpsimd.memset(own[SEG * b:SEG * b + SEG, b, :], 1.0).then_inc(S["made"], 1)
                pool.wait_ge(S["made"], 13)

                def project(w, q, k):
                    if some(k - 1):
                        pool.wait_ge(S["s_ready"], k - 1)
                    pool.wait_ge(S["ab_used"], k + 2)
                    nc.gpsimd.tensor_tensor(rope_qk[:, q % 2].rearrange("p a b -> p (a b)"), t1[:], t2[:], ALU.add).then_inc(S["rope_ready"], 1)

                def recall(w, q, k):
                    r = q % 2
                    pool.wait_ge(S["pt_ready"], k + 1)
                    if some(k - 1):
                        pool.wait_ge(S["pv_ready"], k - 1)
                    shape = [P, QH, BATCH, SEG]
                    nc.gpsimd.tensor_tensor(pt_e[:, r], pt[:, r].unsqueeze(2).to_broadcast(shape), own[:].unsqueeze(1).to_broadcast(shape), ALU.mult).then_inc(S["pte_ready"], 1)

                def update(w, q, k):
                    if q == 0 and some(w):
                        pool.wait_ge(S["ot_ready"], w)
                    pool.wait_ge(S["m2_ready"], k + 1)
                    nc.gpsimd.tensor_tensor(oo[:, q * QH * D:(q + 1) * QH * D].rearrange("p (h d) -> p h d", h=QH), m1[:, q % 2], m2[:], ALU.add).then_inc(S["o_ready"], 1)

                stages = (project, recall, update, idle, idle)
                segment(0, *stages, first=True)
                with pool.Fori(1, W) as w:
                    segment(w, *stages)
                segment(W, *stages, last=True)

            @block.scalar
            def _(act):
                norm.act_std(act)
                act.wait_ge(S["loaded"], 160)
                nc.scalar.activation(gate[:, 1, :], gate[:, 0, :], ACT.Exp, scale=-1.0)
                nc.scalar.activation(gate[:, 2, :], gate[:, 0, :], ACT.Exp).then_inc(S["g_ready"], 1)
                with act.Fori(0, BATCH) as b:
                    for h in range(2):
                        act.wait_ge(S["turned"], b * 2 + h + 1)
                        out = XT[:, h * 16:h * 16 + 16, bass.ds(b * SEG, SEG)]
                        nc.scalar.activation(out, b_a[:].rearrange("p (w t) -> p w t", t=SEG), ACT.Identity, scale=lncol[:, 0:1], bias=lncol[:, 1:2]).then_inc(S["xt_ready"], 1)
                act.wait_ge(S["xt_ready"], 8)

                def project(w, q, k):
                    if q == 0:
                        if some(k):
                            act.wait_ge(S["v_ready"], k)
                        nc.scalar.activation(xw[:], XT[:, bass.ds(w, 1), :].rearrange("p a b -> p (a b)"), ACT.Copy).then_inc(S["xw_ready"], 1)
                    act.wait_ge(S["proj_ready"], k + 1)
                    act.wait_ge(S["el_ready"], k + 1)
                    nc.scalar.activation(ee[:], b_a[:], ACT.Exp)
                    nc.scalar.activation(rr[:], b_a[:], ACT.Relu).then_inc(S["er_ready"], 1)
                    act.wait_ge(S["v_ready"], k + 1)
                    nc.scalar.activation(vt[:, q].rearrange("p a b -> p (a b)"), b_v[:, 0:QH * D], ACT.Copy).then_inc(S["v_copied"], 1)

                def recall(w, q, k):
                    act.wait_ge(S["sk_turned"], k + 1)
                    nc.scalar.activation(skt[:, q].rearrange("p a b -> p (a b)"), b_up[:, 0:PB * P], ACT.Copy).then_inc(S["sk_copied"], 1)
                    act.wait_ge(S["u_ready"], k + 2)
                    for b in range(BATCH):
                        tok = slice(SEG * b, SEG * b + SEG)
                        last = nc.scalar.activation(uu_e[tok, q % 2, :, b, :], uu[tok, q % 2], ACT.Copy)
                    last.then_inc(S["ue_ready"], 1)
                    act.wait_ge(S["s2_ready"], k + 1)
                    nc.scalar.activation(pe_[:], s2[:], ACT.Exp, scale=SCALE).then_inc(S["p_ready"], 1)

                def turn(w):
                    act.wait_ge(S["ot_ready"], w)
                    nc.scalar.activation(ot[:, 0:4].rearrange("p a b -> p (a b)"), b_a[:], ACT.Copy)
                    nc.scalar.activation(ot[:, 4:8].rearrange("p a b -> p (a b)"), b_s[:], ACT.Copy).then_inc(S["ot_copied"], 1)

                stages = (project, recall, idle, turn, idle)
                segment(0, *stages, first=True)
                with act.Fori(1, W) as w:
                    segment(w, *stages)
                segment(W, *stages, last=True)

            @block.tensor
            def _(pe):
                def project(w, q, k):
                    pe.wait_ge(S["ab_used"], k + 1)
                    if q == 2 and some(w):
                        pe.wait_ge(S["ot_copied"], w)
                    x = XT[:, bass.ds(w, 1), :].rearrange("p a b -> p (a b)")
                    for i in range(2):
                        for n in range(PB):
                            c = (i * PB + n) * P
                            nc.tensor.matmul(b_a[:, c:c + P], w4[:, 2 * i, q * PB + n, :], x, start=True, stop=True)
                            last = nc.tensor.matmul(b_s[:, c:c + P], w4[:, 2 * i + 1, q * PB + n, :], x, start=True, stop=True)
                    last.then_inc(S["proj_ready"], 1)
                    pe.wait_ge(S["v_copied"], k + 1)
                    if q == 0:
                        pe.wait_ge(S["xw_ready"], w + 1)
                    if q == NQ - 1 and some(w):
                        pe.wait_ge(S["x_ready"], w)
                    nc.tensor.matmul(b_v[:, 0:QH * D], xw[:], wv_s[:, q * QH * D:(q + 1) * QH * D], start=True, stop=True).then_inc(S["v_ready"], 1)

                def for_heads(parity, fn):
                    half = slice(D * parity, D * parity + D)
                    for blk in range(PB):
                        for b in range(BATCH):
                            last = fn(2 * blk + parity, half, blk, b, slice(SEG * b, SEG * b + SEG))
                    return last

                def recall(w, q, k):
                    r = q % 2
                    pe.wait_ge(S["el_ready"], k + 2)
                    if some(k - 1):
                        pe.wait_ge(S["mem_ready"], k - 1)
                    elif k == 1:
                        pe.wait_ge(S["sk_copied"], k)
                    for n in range(PB):
                        last = nc.tensor.transpose(b_up[:, n * P:n * P + P], el[:, r, PB + n, :], g.ident[:])
                    last.then_inc(S["sk_turned"], 1)
                    prev = lambda h, half, blk, b, tok: nc.tensor.matmul(b_pr[tok, h * E1:h * E1 + E1], el[half, r, PB + blk, tok], mem[half, q, blk, b, :], start=True, stop=True, skip_group_check=True)
                    score = lambda h, half, blk, b, tok: nc.tensor.matmul(b_sc[tok, h * SEG:h * SEG + SEG], rope_qk[half, r, blk, tok], rope_qk[half, r, PB + blk, tok], start=True, stop=True, skip_group_check=True)
                    num = lambda h, half, blk, b, tok: nc.tensor.matmul(b_nu[tok, h * E1:h * E1 + E1], el[half, r, blk, tok], mem[half, q, blk, b, :], start=True, stop=True, skip_group_check=True)
                    hold(pe, S["u_ready"], k + 1)
                    for_heads(0, prev).then_inc(S["prev_even"], 1)
                    hold(pe, S["rope_ready"], k + 1)
                    hold(pe, S["s1_ready"], k + 1)
                    for_heads(0, score).then_inc(S["s_even"], 1)
                    hold(pe, S["prev_even"], k + 1)
                    for_heads(1, prev).then_inc(S["prev_ready"], 1)
                    hold(pe, S["m1_ready"], k + 1)
                    for_heads(0, num).then_inc(S["num_even"], 1)
                    hold(pe, S["s_even"], k + 1)
                    for_heads(1, score).then_inc(S["s_ready"], 1)
                    hold(pe, S["num_even"], k + 1)
                    for_heads(1, num).then_inc(S["num_ready"], 1)

                def update(w, q, k):
                    r = q % 2
                    if isinstance(k, int) and k == W * NQ - 1:
                        pe.wait_ge(S["mem_ready"], k)
                    else:
                        pe.wait_ge(S["sk_copied"], k + 2)
                    pe.wait_ge(S["ue_ready"], k + 1)
                    for h in range(QH):
                        half, c = slice(D * (h % 2), D * (h % 2) + D), h // 2 * BATCH * D
                        last = nc.tensor.matmul(b_up[half, c:c + BATCH * D], skt[:, q, h // 2, half], uu_e[:, r, h].rearrange("p b d -> p (b d)"), start=True, stop=True, skip_group_check=True)
                    last.then_inc(S["upd_ready"], 1)
                    pe.wait_ge(S["pte_ready"], k + 1)
                    if some(k):
                        pe.wait_ge(S["m2_ready"], k)
                    for h in range(QH):
                        last = nc.tensor.matmul(b_pv[:, h * D:h * D + D], pt_e[:, r, h].rearrange("p b t -> p (b t)"), vt[:, q, h, :], start=True, stop=True)
                    last.then_inc(S["pv_ready"], 1)

                def turn(w):
                    pe.wait_ge(S["o_ready"], w * NQ)
                    pe.wait_ge(S["ab_used"], w * NQ + 1 if isinstance(w, int) and w == W else w * NQ + 3)
                    for n in range(H // 2):
                        last = nc.tensor.transpose((b_a, b_s)[n // 4][:, n % 4 * P:n % 4 * P + P], oo[:, n * P:n * P + P], g.ident[:])
                    last.then_inc(S["ot_ready"], 1)

                def add(w):
                    pe.wait_ge(S["ot_copied"], w)
                    pe.wait_ge(S["v_copied"], w * NQ + 1 if isinstance(w, int) and w == W else w * NQ + 4)
                    for n in range(H // 2):
                        last = nc.tensor.matmul(b_v[:, 0:P], ot[:, n, :], wo[:, n, :], start=(n == 0), stop=(n == H // 2 - 1))
                    last.then_inc(S["out_ready"], 1)

                pe.wait_ge(S["loaded"], 160)
                pe.wait_ge(S["made"], 13)
                with pe.Fori(0, 2 * BATCH) as c:
                    pe.wait_ge(S["xn_ready"], c + 1)
                    for n in range(CT):
                        last = nc.tensor.transpose(b_a[:, n * P:n * P + P], norm.xn[:, n, :], g.ident[:])
                    last.then_inc(S["turned"], 1)
                pe.wait_ge(S["xt_ready"], 2 * BATCH)
                stages = (project, recall, update, turn, add)
                segment(0, *stages, first=True)
                with pe.Fori(1, W) as w:
                    segment(w, *stages)
                segment(W, *stages, last=True)

            @block.vector
            def _(dve):
                norm.dve_rstd(dve)
                st = Chain(dve, S["setup"])
                dve.wait_ge(S["g_ready"], 1)
                dve.wait_ge(S["made"], 13)
                st.link(nc.vector.tensor_scalar_add(gate[:, 1:3, :], gate[:, 1:3, :], 1.0))
                for n, credit in (("ab_used", 1), ("v_copied", 1), ("el_ready", 1), ("u_ready", 1), ("s1_ready", 1), ("m1_ready", 1)):
                    dve.sem_inc(S[n], credit)
                with dve.Fori(0, 2 * BATCH) as c:
                    norm.dve_rows(c).then_inc(S["xn_ready"], 1)
                    dve.wait_ge(S["xt_ready"], c + 1)

                def project(w, q, k, ch):
                    dve.wait_ge(S["proj_ready"], k + 1)
                    if some(k):
                        dve.wait_ge(S["rope_ready"], k)
                    seg = lambda ap: ap.rearrange("p (n t) -> p n t", t=SEG)
                    tab = lambda i: bc(cs[:, i, :], 4 * P // SEG)
                    nc.vector.tensor_tensor(seg(t2[:]), seg(b_s[:]), tab(1), ALU.mult)
                    dve.wait_ge(S["er_ready"], k + 1)
                    nc.vector.tensor_tensor(seg(t1[:]), seg(b_a[:]), tab(0), ALU.mult).then_inc(S["ab_used"], 1)
                    e2 = el[:, q % 2].rearrange("p a b -> p (a b)")
                    nc.vector.scalar_tensor_tensor(e2, ee[:], 1.0, rr[:], ALU.min, ALU.add).then_inc(S["el_ready"], 1)
                    dve.wait_ge(S["el_ready"], k + 2)
                    nc.vector.tensor_reduce(zinc[:, q].rearrange("p a b -> p (a b)"), el[:, q % 2, PB:2 * PB].rearrange("p a (b t) -> p (a b) t", t=SEG), AX_X, ALU.add)

                def recall_and_update(w, q, k, ch, recalls=True, updates=True):
                    r, kw, qw = q % 2, k - 1, (q - 1) % NQ
                    rw = qw % 2
                    pr, nu = head_view(b_pr, E1), head_view(b_nu, E1)
                    m = mem[:, qw].rearrange("p a b e -> p (a b) e")
                    done = {}

                    def mark(name, ins):
                        ch.mark(ins)
                        done[name] = ch.n

                    def after(name):
                        dve.wait_ge(S["chain"], ch.base + done[name])

                    if recalls:
                        dve.wait_ge(S["prev_ready"], k + 1)
                        mark("rd", nc.vector.reciprocal(rd[:], pr[:, :, D]))
                    if updates:
                        dve.wait_ge(S["pt_ready"], kw + 1)
                        if some(kw):
                            dve.wait_ge(S["m2_ready"], kw)
                        mark("rsum", nc.vector.tensor_tensor(rs[:], sm[:, rw], gate[:, 2, qw * QH:qw * QH + QH], ALU.mult))
                    if recalls:
                        after("rd")
                        mark("u1", nc.vector.tensor_tensor(u1[:], pr[:, :, 0:D], bl(rd[:], D), ALU.mult))
                    if updates:
                        after("rsum")
                        mark("rs", nc.vector.reciprocal(rs[:], rs[:]))
                    if recalls:
                        dve.wait_ge(S["s_ready"], k + 1)
                        nc.vector.tensor_tensor(s1[:], score_view(b_sc), bc(mask[:], QH), ALU.add).then_inc(S["s1_ready"], 1)
                        dve.wait_ge(S["v_copied"], k + 2)
                        after("u1")
                        nc.vector.tensor_tensor(uu[:, r], vt[:, q], u1[:], ALU.subtract).then_inc(S["u_ready"], 1)
                        dve.wait_ge(S["s1_ready"], k + 2)
                        mark("mx", nc.vector.tensor_reduce(mx[:], s1[:], AX_X, ALU.max))
                        dve.wait_ge(S["num_ready"], k + 1)
                        mark("den", nc.vector.scalar_tensor_tensor(dn[:], nu[:, :, D], 1.0e-6, gate[:, 1, q * QH:q * QH + QH], ALU.add, ALU.mult))
                        after("mx")
                        nc.vector.tensor_tensor(s2[:], s1[:], bl(mx[:], SEG), ALU.subtract).then_inc(S["s2_ready"], 1)
                        after("den")
                        mark("dn", nc.vector.reciprocal(dn[:], dn[:]))
                    if updates:
                        dve.wait_ge(S["upd_ready"], kw + 1)
                        mark("mem", nc.vector.tensor_tensor(m[:, :, 0:D], m[:, :, 0:D], b_up[:].rearrange("p (n d) -> p n d", d=D), ALU.add))
                    if recalls:
                        after("dn")
                        if some(k - 1):
                            dve.wait_ge(S["o_ready"], k - 1)
                        nc.vector.tensor_tensor(m1[:, r], nu[:, :, 0:D], bl(dn[:], D), ALU.mult).then_inc(S["m1_ready"], 1)
                    if updates:
                        after("mem")
                        nc.vector.tensor_tensor(m[:, :, D], m[:, :, D], zinc[:, qw].rearrange("p a b -> p (a b)"), ALU.add).then_inc(S["mem_ready"], 1)
                    if recalls:
                        dve.wait_ge(S["p_ready"], k + 1)
                        nc.vector.tensor_reduce(sm[:, r], pe_[:], AX_X, ALU.add)
                        nc.vector.transpose(pt[:, r].rearrange("p a b -> p (a b)"), pe_[:].rearrange("p a b -> p (a b)")).then_inc(S["pt_ready"], 1)
                    if updates:
                        after("rs")
                        if some(kw):
                            dve.wait_ge(S["o_ready"], kw)
                        dve.wait_ge(S["pv_ready"], kw + 1)
                        nc.vector.tensor_tensor(m2[:], head_view(b_pv, D), bl(rs[:], D), ALU.mult).then_inc(S["m2_ready"], 1)

                first_links = []

                def step(w, n, j, tile):
                    ch = Chain(dve, S["chain"], first_links[0] + (w - 1) * STEPS if first_links else 0)

                    def add(w):
                        dve.wait_ge(S["out_ready"], w)
                        for b in range(BATCH):
                            rows = g.X[SEG * j:SEG * j + SEG, bass.ds(tile + b * (SEQ // P), 1), :].rearrange("p a d -> p (a d)")
                            last = nc.vector.tensor_tensor(rows, b_v[SEG * b:SEG * b + SEG, 0:P], rows, ALU.add)
                        last.then_inc(S["x_ready"], 1)

                    first, last = n == "first", n == "last"
                    for slot in range(NQ):
                        k = w * NQ + slot
                        if slot != 2 and not last:
                            project(w, slot, k, ch)
                        recalls, updates = not (first and slot < 1 or last and slot > 0), not (first and slot < 2 or last and slot > 1)
                        if recalls or updates:
                            recall_and_update(w, (slot - 1) % NQ, k - 1, ch, recalls, updates)
                        if slot == 2 and not last:
                            project(w, slot, k, ch)
                        if slot == 2 and not first:
                            add(w)
                    assert n != "inner" or ch.n == STEPS, ch.n
                    first_links.append(ch.n)

                step(0, "first", None, None)
                with dve.Fori(0, W // 4 - 1) as i:
                    for j in range(4):
                        step(i * 4 + (j + 1), "inner", j, i)
                for j in range(4):
                    w = W - 3 + j
                    step(w, "last" if w == W else "inner", j, W // 4 - 1)
                dve.wait_ge(S["x_ready"], W)
                with dve.Fori(0, NC_) as c:
                    ch = Chain(dve, S["stats"], c * 3)
                    ch.link(dve_new_stats(nc, dve, g, raw, c, ch))
        s.clear()


class Globals:
    pass




def build(nc, a, out):
    with ExitStack() as ctx:
        s = Scope(nc, ctx, "g")
        g = Globals()
        g.X = s.sb("x", [P, NT, P])
        g.MV, g.mv4 = s.sb("mv", [P, NT, 2]), s.sb("mv4", [P, CT, 2])
        g.ident, g.ones = s.sb("ident", [P, P]), s.sb("ones", [P, P])
        g.eps, g.iota8 = s.sb("eps", [P, 1]), s.sb("iota8", [P, 8])
        g.stored = s.sem("stored")
        E0, E1 = a["L0_ffn_gate"].shape[1], a["L1_ffn_w_router"].shape[1]
        first_weights, later_weights = ctx.enter_context(ExitStack()), ctx.enter_context(ExitStack())
        s0 = Scope(nc, first_weights, "w0")
        w1, w3, w2 = (s0.sb(n, sh) for n, sh in (("w1", [P, E0, 512]), ("w3", [P, E0, 512]), ("w2", [P, E0, 4, P])))
        gate = s0.sb("gate", [P, E0])
        g.weights_loaded = s.sem("weights_loaded")

        def load_weights(sp):
            for dst, src in ((gate[:], a["L0_ffn_gate"]), (w1[:], a["L0_ffn_experts_w1"].rearrange("e h i -> h e i")),
                             (w3[:], a["L0_ffn_experts_w3"].rearrange("e h i -> h e i")),
                             (w2[:], a["L0_ffn_experts_w2"].rearrange("e (b i) h -> i e b h", i=P))):
                sp.dma_start(dst, src).then_inc(g.weights_loaded, 16)
        g.load_weights = load_weights
        later = {}

        def load_later_weights():
            s1 = Scope(nc, later_weights, "w1")
            wv, wp, router = (s1.sb(n, sh) for n, sh in (("wv", [P, E1, 1024]), ("wproj", [P, E1, 4, P]), ("router", [P, E1])))
            later.update(wv=wv, wp=wp, router=router)
            with nc.Block() as block:
                @block.sync
                def _(sp):
                    for dst, src in ((router[:], a["L1_ffn_w_router"]), (wv[:], a["L1_ffn_w_v"].rearrange("e d h -> d e h")),
                                     (wp[:], a["L1_ffn_w_proj"].rearrange("e (b i) d -> i e b d", i=P))):
                        sp.dma_start(dst, src).then_inc(g.weights_loaded, 16)

        load_and_constants(nc, g, a["L0_attn_a_x"])

        def l0_experts(name):
            expert_layer(nc, g, name, E0, 2, 16 * 4, gate, lambda e: tile_of(w1, e), lambda e: tile_of(w3, e), lambda e, j: tile_of(w2[:, :, j, :], e))

        def l1_experts(name):
            wv, wp, router = later["wv"], later["wp"], later["router"]
            expert_layer(nc, g, name, E1, 1, 16 * 7, router, lambda e: tile_of(wv[:, :, 0:512], e), lambda e: tile_of(wv[:, :, 512:1024], e), lambda e, j: tile_of(wp[:, :, j, :], e))

        layers = [
            lambda: ssm_layer(nc, g, *(a["L0_attn_a_" + n] for n in ("W_in", "b_in", "log_A", "B_p", "C_p", "W_out", "b_out", "gamma", "beta"))),
            lambda: l0_experts("ffn0"),
            lambda: landmark_layer(nc, g, *(a["L0_attn_b_" + n] for n in ("Wq", "bq", "Wk", "bk", "Wv", "bv"))),
            lambda: l0_experts("ffn1"),
            lambda: causal_layer(nc, g, *(a["L1_attn_a_" + n] for n in ("Wq", "bq", "Wk", "bk", "Wv", "bv", "Wp", "bp", "rel_bias_table", "Wq_swapped", "bq_swapped", "Wk_swapped", "bk_swapped")), a["rope_a"], a["buckets"]),
            lambda: l1_experts("ffn2"),
            lambda: memory_layer(nc, g, a["wq_halves"], a["wq_swapped"], a["wk_halves"], a["wk_swapped"], a["wv"], *(a["L1_attn_b_" + n] for n in ("w_out", "ln_g", "ln_b", "mem_beta")), a["rope_b"]),
            lambda: l1_experts("ffn3"),
        ]
        for n in range(len(layers)):
            if n == 4:
                first_weights.close()
                load_later_weights()
            layers[n]()
        later_weights.close()
        with nc.Block() as block:
            @block.sync
            def _(sp):
                sp.dma_start(out.rearrange("b (n p) d -> p (b n) d", p=P), g.X[:]).then_inc(g.stored, 16)
                sp.wait_ge(g.stored, 16)


def shape_constants():
    import math

    import numpy as np

    T, D = 1024, 8
    inv = (1.0 / 10000.0 ** (np.arange(0, D, 2, dtype=np.float32) / D)).astype(np.float32)
    ang = (np.arange(T, dtype=np.float32)[None, :] * inv[:, None]).astype(np.float32)
    cos, sin = np.cos(ang), np.sin(ang)
    rope = np.stack([np.tile(np.concatenate([cos, cos]), (16, 1)), np.tile(np.concatenate([-sin, sin]), (16, 1))], 1)

    def bucket(n):
        if n < 16:
            return n
        big = np.log(np.float32(n) / np.float32(16)) / np.float32(math.log(8.0)) * np.float32(16)
        return min(16 + int(big), 31)

    pick = np.zeros((33, 2, 384), np.float32)
    for u in range(384):
        for side, n in ((0, u - 128), (1, 255 - u)):
            if n < 0:
                pick[32, side, u] = -1.0e30
            else:
                pick[bucket(n), side, u] += 1.0
                pick[31, side, u] -= 1.0
    freq = 10000.0 ** (-np.arange(0, 64, 2, dtype=np.float64) / 64)
    ang = freq[:, None] * np.arange(32)[None, :]
    cos, sin = np.cos(ang), np.sin(ang)
    rope_b = np.stack([np.tile(np.concatenate([cos, cos]), (2, 1)), np.tile(np.concatenate([-sin, sin]), (2, 1))], 1)
    return rope.astype(np.float32), pick.reshape(33, 768), rope_b.astype(np.float32)


_INS = ['L0_attn_a_x', 'L0_attn_a_W_in', 'L0_attn_a_b_in', 'L0_attn_a_log_A', 'L0_attn_a_B_p', 'L0_attn_a_C_p', 'L0_attn_a_W_out', 'L0_attn_a_b_out', 'L0_attn_a_gamma', 'L0_attn_a_beta', 'L0_attn_b_Wq', 'L0_attn_b_bq', 'L0_attn_b_Wk', 'L0_attn_b_bk', 'L0_attn_b_Wv', 'L0_attn_b_bv', 'L0_ffn_gate', 'L0_ffn_experts_w1', 'L0_ffn_experts_w2', 'L0_ffn_experts_w3', 'L1_attn_a_Wq', 'L1_attn_a_bq', 'L1_attn_a_Wk', 'L1_attn_a_bk', 'L1_attn_a_Wv', 'L1_attn_a_bv', 'L1_attn_a_Wp', 'L1_attn_a_bp', 'L1_attn_a_rel_bias_table', 'L1_attn_b_w_qkv', 'L1_attn_b_w_out', 'L1_attn_b_ln_g', 'L1_attn_b_ln_b', 'L1_attn_b_mem_beta', 'L1_ffn_w_router', 'L1_ffn_w_v', 'L1_ffn_w_proj']


def kernel(**inputs):
    import numpy as _np
    import concourse.bacc as _bacc
    from concourse import mybir as _mybir
    from concourse.bass_utils import run_bass_kernel_spmd as _run

    laid = dict(inputs)
    for name in ("L0_attn_a_W_in", "L0_attn_a_W_out"):
        laid[name] = _np.asarray(inputs[name]).T
    for name in ("Wq", "bq", "Wk", "bk"):
        m = _np.asarray(inputs["L1_attn_a_" + name])
        laid["L1_attn_a_" + name + "_swapped"] = m.reshape(m.shape[:-1] + (16, 2, 4))[..., ::-1, :].reshape(m.shape)
    qkv = _np.asarray(inputs["L1_attn_b_w_qkv"])
    for i, side in enumerate("qk"):
        m = qkv[:, i * 1024:i * 1024 + 1024].reshape(128, 16, 32, 2)
        laid["w" + side + "_halves"] = m.transpose(0, 1, 3, 2).reshape(128, 1024)
        laid["w" + side + "_swapped"] = m[..., ::-1].transpose(0, 1, 3, 2).reshape(128, 1024)
    laid["wv"] = qkv[:, 2048:]
    del laid["L1_attn_b_w_qkv"]
    laid["rope_a"], laid["buckets"], laid["rope_b"] = shape_constants()
    nc = _bacc.Bacc("TRN2", target_bir_lowering=False, num_devices=1)
    arrays, aps = {}, {}
    for name in laid:
        arr = _np.ascontiguousarray(laid[name])
        arrays[f"in_{name}_dram"] = arr
        aps[name] = nc.dram_tensor(f"in_{name}_dram", arr.shape, _mybir.dt.from_np(arr.dtype), kind="ExternalInput").ap()
    out = nc.dram_tensor("out_0_dram", (4, 1024, 128), _mybir.dt.float32, kind="ExternalOutput").ap()
    build(nc, aps, out)
    r = _run(nc, [arrays], core_ids=[0])
    return r.results[0]["out_0_dram"]
```
